# Optimizing a Trainium2 kernel written in Bass

```python
import numpy as np
import jax
import jax.numpy as jnp

def _softmax(x, axis=-1):
    return jax.nn.softmax(x, axis=axis)

def _gelu(x):
    return jax.nn.gelu(x, approximate=True)

def _silu(x):
    return jax.nn.silu(x)

def _sigmoid(x):
    return jax.nn.sigmoid(x)

def _layernorm(x, axis=-1, eps=1e-05):
    m = jnp.mean(x, axis=axis, keepdims=True)
    v = jnp.var(x, axis=axis, keepdims=True)
    return (x - m) / jnp.sqrt(v + eps)

def _scatter_add(tgt, idx, src, axis=0):
    return tgt.at[idx].add(src)

def _segment_sum(src, seg, n):
    return jax.ops.segment_sum(src, seg, n)
kernel_name = 'mk_sandwich_d1_jaxref_r8_afd374'

def setup_inputs(seed: int=0):
    np.random.seed(seed)
    _w = jnp.asarray

    def _L0_attn_setup():
        import jax, jax.numpy as jnp
        import numpy as np
        D_MODEL = 128
        D_INNER = 256
        N_HEADS = 8
        HEAD_DIM = D_INNER // N_HEADS
        D_STATE = 64
        CHUNK = 64
        D_CONV = 4
        EPS = float(np.finfo(np.float32).eps)
        PROJ_OUT = 2 * D_INNER + 2 * N_HEADS * D_STATE + N_HEADS

        def rmsnorm(x, w):
            return x * jax.lax.rsqrt(jnp.mean(x * x, axis=-1, keepdims=True) + EPS) * w

        def ssd_scan(x, dt, B_in, C_in, A_log):
            Bz, S, H, P = x.shape
            N = B_in.shape[-1]
            nc = S // CHUNK
            A = -jnp.exp(A_log)
            resh = lambda t: jnp.moveaxis(t.reshape((Bz, nc, CHUNK) + t.shape[2:]), 1, 0)
            xs = (resh(x), resh(dt), resh(B_in), resh(C_in))
            mask = jnp.tril(jnp.ones((CHUNK, CHUNK), bool))
            h0 = jnp.zeros((Bz, H, P, N), jnp.float32)

            def step(h, inp):
                x_c, dt_c, B_c, C_c = inp
                lcs = jnp.cumsum(dt_c * A, axis=1)
                lcsT = jnp.transpose(lcs, (0, 2, 1))
                diff = lcsT[:, :, :, None] - lcsT[:, :, None, :]
                M = jnp.exp(jnp.where(mask, diff, -jnp.inf))
                G = jnp.einsum('blhn,bihn->bhli', C_c, B_c)
                intra = jnp.einsum('bhli,bihp->blhp', M * G, x_c)
                inter = jnp.einsum('blh,blhn,bhpn->blhp', jnp.exp(lcs), C_c, h)
                total_decay = jnp.exp(lcsT[:, :, -1])
                h_new = total_decay[:, :, None, None] * h + jnp.einsum('bhl,blhp,blhn->bhpn', M[:, :, -1, :], x_c, B_c)
                return (h_new, intra + inter)
            _, ys = jax.lax.scan(step, h0, xs)
            return jnp.moveaxis(ys, 0, 1).reshape(Bz, S, H, P)
        key = jax.random.key(seed)
        ks = jax.random.split(key, 8)
        hidden = jax.random.normal(ks[0], (2, 512, D_MODEL), jnp.float32)
        w_in_proj = 0.02 * jax.random.normal(ks[1], (D_MODEL, PROJ_OUT), jnp.float32)
        conv_w = 0.2 * jax.random.normal(ks[2], (D_INNER, 1, D_CONV), jnp.float32)
        conv_b = jnp.zeros((D_INNER,), jnp.float32)
        w_dt = 0.02 * jax.random.normal(ks[3], (N_HEADS, D_INNER), jnp.float32)
        b_dt = 0.02 * jax.random.normal(ks[4], (D_INNER,), jnp.float32)
        A_log = jax.random.uniform(ks[5], (N_HEADS,), jnp.float32, np.log(0.001), np.log(0.1))
        D = jnp.ones((N_HEADS,), jnp.float32)
        w_out_proj = 0.02 * jax.random.normal(ks[6], (D_INNER, D_MODEL), jnp.float32)
        return {'hidden': hidden, 'w_norm_in': jnp.ones((D_MODEL,), jnp.float32), 'w_in_proj': w_in_proj, 'conv_w': conv_w, 'conv_b': conv_b, 'w_dt': w_dt, 'b_dt': b_dt, 'A_log': A_log, 'D': D, 'w_norm_out': jnp.ones((D_INNER,), jnp.float32), 'w_out_proj': w_out_proj}
    _L0_attn_in = _L0_attn_setup()

    def _L0_ffn_setup():
        import jax, jax.numpy as jnp
        import numpy as np
        E = 8
        D = 128
        H = 256
        TOP_K = 2
        key = jax.random.key(seed)
        k_x, k_g, k_w1, k_w2 = jax.random.split(key, 4)
        B, S = (4, 256)
        inp = {'input': jax.random.normal(k_x, (B, S, D), dtype=jnp.float32), 'Wg': jax.random.normal(k_g, (D, E), dtype=jnp.float32) * 0.02, 'W1': jax.random.normal(k_w1, (E, D, H), dtype=jnp.float32) * 0.02, 'b1': jnp.zeros((E, H), dtype=jnp.float32), 'W2': jax.random.normal(k_w2, (E, H, D), dtype=jnp.float32) * 0.02, 'b2': jnp.zeros((E, D), dtype=jnp.float32)}
        return inp
    _L0_ffn_in = _L0_ffn_setup()
    _d = {'L0_attn_hidden': _L0_attn_in['hidden'], 'L0_attn_w_norm_in': _L0_attn_in['w_norm_in'], 'L0_attn_w_in_proj': _L0_attn_in['w_in_proj'], 'L0_attn_conv_w': _L0_attn_in['conv_w'], 'L0_attn_conv_b': _L0_attn_in['conv_b'], 'L0_attn_w_dt': _L0_attn_in['w_dt'], 'L0_attn_b_dt': _L0_attn_in['b_dt'], 'L0_attn_A_log': _L0_attn_in['A_log'], 'L0_attn_D': _L0_attn_in['D'], 'L0_attn_w_norm_out': _L0_attn_in['w_norm_out'], 'L0_attn_w_out_proj': _L0_attn_in['w_out_proj'], 'L0_ffn_Wg': _L0_ffn_in['Wg'], 'L0_ffn_W1': _L0_ffn_in['W1'], 'L0_ffn_b1': _L0_ffn_in['b1'], 'L0_ffn_W2': _L0_ffn_in['W2'], 'L0_ffn_b2': _L0_ffn_in['b2']}
    _x0 = _d['L0_attn_hidden']
    _d['L0_attn_hidden'] = jax.random.normal(jax.random.fold_in(jax.random.key(seed), 1), (8, 1024, 128), dtype=_x0.dtype)
    del _x0
    return _d

def reference(L0_attn_hidden, L0_attn_w_norm_in, L0_attn_w_in_proj, L0_attn_conv_w, L0_attn_conv_b, L0_attn_w_dt, L0_attn_b_dt, L0_attn_A_log, L0_attn_D, L0_attn_w_norm_out, L0_attn_w_out_proj, L0_ffn_Wg, L0_ffn_W1, L0_ffn_b1, L0_ffn_W2, L0_ffn_b2):

    def _L0_attn_ref(hidden, w_norm_in, w_in_proj, conv_w, conv_b, w_dt, b_dt, A_log, D, w_norm_out, w_out_proj):
        import jax, jax.numpy as jnp
        import numpy as np
        D_MODEL = 128
        D_INNER = 256
        N_HEADS = 8
        HEAD_DIM = D_INNER // N_HEADS
        D_STATE = 64
        CHUNK = 64
        D_CONV = 4
        EPS = float(np.finfo(np.float32).eps)
        PROJ_OUT = 2 * D_INNER + 2 * N_HEADS * D_STATE + N_HEADS

        def rmsnorm(x, w):
            return x * jax.lax.rsqrt(jnp.mean(x * x, axis=-1, keepdims=True) + EPS) * w

        def ssd_scan(x, dt, B_in, C_in, A_log):
            Bz, S, H, P = x.shape
            N = B_in.shape[-1]
            nc = S // CHUNK
            A = -jnp.exp(A_log)
            resh = lambda t: jnp.moveaxis(t.reshape((Bz, nc, CHUNK) + t.shape[2:]), 1, 0)
            xs = (resh(x), resh(dt), resh(B_in), resh(C_in))
            mask = jnp.tril(jnp.ones((CHUNK, CHUNK), bool))
            h0 = jnp.zeros((Bz, H, P, N), jnp.float32)

            def step(h, inp):
                x_c, dt_c, B_c, C_c = inp
                lcs = jnp.cumsum(dt_c * A, axis=1)
                lcsT = jnp.transpose(lcs, (0, 2, 1))
                diff = lcsT[:, :, :, None] - lcsT[:, :, None, :]
                M = jnp.exp(jnp.where(mask, diff, -jnp.inf))
                G = jnp.einsum('blhn,bihn->bhli', C_c, B_c)
                intra = jnp.einsum('bhli,bihp->blhp', M * G, x_c)
                inter = jnp.einsum('blh,blhn,bhpn->blhp', jnp.exp(lcs), C_c, h)
                total_decay = jnp.exp(lcsT[:, :, -1])
                h_new = total_decay[:, :, None, None] * h + jnp.einsum('bhl,blhp,blhn->bhpn', M[:, :, -1, :], x_c, B_c)
                return (h_new, intra + inter)
            _, ys = jax.lax.scan(step, h0, xs)
            return jnp.moveaxis(ys, 0, 1).reshape(Bz, S, H, P)
        Bz, S, _ = hidden.shape
        residual = hidden
        h = rmsnorm(hidden, w_norm_in)
        proj = h @ w_in_proj
        o1, o2 = (D_INNER, 2 * D_INNER)
        o3 = o2 + N_HEADS * D_STATE
        o4 = o3 + N_HEADS * D_STATE
        z = proj[..., :o1]
        x = proj[..., o1:o2]
        B_flat = proj[..., o2:o3]
        C_flat = proj[..., o3:o4]
        dt_raw = proj[..., o4:]
        xt = jnp.transpose(x, (0, 2, 1))
        xc = jax.lax.conv_general_dilated(xt, conv_w, (1,), [(D_CONV - 1, 0)], dimension_numbers=('NCH', 'OIH', 'NCH'), feature_group_count=D_INNER) + conv_b[None, :, None]
        x = jax.nn.silu(jnp.transpose(xc, (0, 2, 1)))
        dt = jax.nn.softplus(dt_raw @ w_dt + b_dt)
        dt_h = dt.reshape(Bz, S, N_HEADS, HEAD_DIM).mean(-1)
        B_ssm = B_flat.reshape(Bz, S, N_HEADS, D_STATE)
        C_ssm = C_flat.reshape(Bz, S, N_HEADS, D_STATE)
        x_h = x.reshape(Bz, S, N_HEADS, HEAD_DIM)
        y = ssd_scan(x_h, dt_h, B_ssm, C_ssm, A_log)
        y = y + x_h * D[None, None, :, None]
        y = y.reshape(Bz, S, D_INNER)
        y = y * jax.nn.silu(z)
        y = rmsnorm(y, w_norm_out)
        return residual + y @ w_out_proj

    def _L0_ffn_ref(input, Wg, W1, b1, W2, b2):
        import jax, jax.numpy as jnp
        import numpy as np
        E = 8
        D = 128
        H = 256
        TOP_K = 2
        logits = jnp.einsum('bsd,de->bse', input, Wg)
        probs = jax.nn.softmax(logits, axis=-1)
        top_vals, top_idx = jax.lax.top_k(probs, TOP_K)
        top_vals = top_vals / jnp.sum(top_vals, axis=-1, keepdims=True)
        onehot = jax.nn.one_hot(top_idx, E, dtype=input.dtype)
        mask = jnp.sum(onehot, axis=2)
        scores = jnp.sum(onehot * top_vals[..., None], axis=2)
        xm = input[None] * jnp.moveaxis(mask, -1, 0)[..., None]
        h = jnp.einsum('ebsd,edh->ebsh', xm, W1) + b1[:, None, None, :]
        h = jax.nn.relu(h)
        y = jnp.einsum('ebsh,ehd->ebsd', h, W2) + b2[:, None, None, :]
        out = jnp.sum(y * jnp.moveaxis(scores, -1, 0)[..., None], axis=0)
        return out
    x = L0_attn_hidden
    x = x + _layernorm(_L0_attn_ref(_layernorm(x, axis=-1), L0_attn_w_norm_in, L0_attn_w_in_proj, L0_attn_conv_w, L0_attn_conv_b, L0_attn_w_dt, L0_attn_b_dt, L0_attn_A_log, L0_attn_D, L0_attn_w_norm_out, L0_attn_w_out_proj), axis=-1)
    x = x + _layernorm(_L0_ffn_ref(_layernorm(x, axis=-1), L0_ffn_Wg, L0_ffn_W1, L0_ffn_b1, L0_ffn_W2, L0_ffn_b2), axis=-1)
    return x

_drawn_inputs = setup_inputs


def setup_inputs(seed=0):
    import zlib

    import numpy as np

    out = dict(_drawn_inputs(seed))
    spreads = {'L0_attn_w_norm_in': (1.0, 0.2),
     'L0_attn_conv_b': (0.0, 0.1),
     'L0_attn_D': (1.0, 0.2),
     'L0_attn_w_norm_out': (1.0, 0.2),
     'L0_ffn_b1': (0.0, 0.1),
     'L0_ffn_b2': (0.0, 0.1)}
    factors = {'L0_attn_w_dt': 64.0, 'L0_attn_b_dt': 41.261}
    for name, (base, spread) in spreads.items():
        noise = np.random.default_rng([zlib.crc32(name.encode()), seed]).standard_normal(out[name].shape)
        drawn = base * np.exp(spread * noise) if base else spread * noise
        out[name] = jnp.asarray(drawn.astype(out[name].dtype))
    for name, factor in factors.items():
        out[name] = (out[name] * factor).astype(out[name].dtype)
    return out
```

```python
from contextlib import ExitStack

import numpy as np
import concourse.bass as bass
from concourse import mybir

ALU = mybir.AluOpType
ACT = mybir.ActivationFunctionType
F32 = mybir.dt.float32
F32R = mybir.dt.float32r
BF16 = mybir.dt.bfloat16
AX = mybir.AxisListType.X

P = 128
BATCH, SEQ, D = 8, 1024, 128
TOK = BATCH * SEQ
TILES = TOK // P
TG = 4
GT = TG * P
GROUPS = TOK // GT
GB = SEQ // GT
DI, NH, HD, NS, KC = 256, 8, 32, 64, 4
NP = NH // 2
HH = NH // 2
NB = DI // P
O_X, O_B, O_C, O_DT = DI, 2 * DI, 2 * DI + NH * NS, 2 * DI + 2 * NH * NS
PROJ = O_DT + NH
WCOLS = O_DT + DI
LN_EPS = 1e-5
RMS_EPS = float(np.finfo(np.float32).eps)
NE, FH = 8, 256
FB = FH // P
PARTS = 3


class Signal:

    def __init__(self, nc, name, per):
        self.sem, self.per = nc.alloc_semaphore(name), per

    def of(self, idx, k=None):
        return idx * self.per + (self.per if k is None else k)


def due(idx):
    return not isinstance(idx, int) or idx >= 0


def apart(eng, idx):
    if not isinstance(idx, int):
        eng.nop(nofuse=True)


def build(nc, hidden, w_norm_in, w_in, conv_w, conv_b, w_dt, b_dt, a_log, d_skip, w_norm_out, w_out,
          wg, w1, b1, w2, b2, out):
    xall = nc.alloc_sbuf_tensor("xall", [P, TILES, D], F32)
    banks = [nc.alloc_psum_tensor(f"bank{i}", [P, 512], F32) for i in range(8)]
    with ExitStack() as attention_buffers:
        attention(nc, attention_buffers, xall, banks, hidden, w_norm_in, w_in, conv_w, conv_b, w_dt, b_dt, a_log,
                  d_skip, w_norm_out, w_out)
    with ExitStack() as expert_buffers:
        experts(nc, expert_buffers, xall, banks, wg, w1, b1, w2, b2, out)


def static(a, n):
    return slice(a, a + n)


def dynamic(a, n):
    return bass.ds(a, n)


def col(i, w=P):
    return slice(i * w, (i + 1) * w)


def attention(nc, buffers, xall, banks, hidden, w_norm_in, w_in, conv_w, conv_b, w_dt, b_dt, a_log,
              d_skip, w_norm_out, w_out):
    def sb(name, shape, dt=F32):
        return buffers.enter_context(nc.sbuf_tensor(name, shape, dt))

    def sig(name, per=1):
        return Signal(nc, name, per)

    PE, DVE, SE, PL = nc.tensor, nc.vector, nc.scalar, nc.gpsimd

    s1 = sb("ln1_scale", [P, TILES])
    nb1 = sb("ln1_shift", [P, TILES])

    ident = sb("ident", [P, P])
    ones = sb("ones", [P, P])
    zeros = sb("zeros", [P, 1])
    neghalf = sb("neghalf", [P, TG])
    sel_a = sb("sel_a", [P, NH, P], BF16)
    negsel = sb("negsel", [P, NH, P], BF16)
    sel_e = sb("sel_e", [P, NB, P], BF16)
    hsum = sb("hsum", [P, NB, NH])

    m_flat = sb("m", [P, 2 * NH * P])
    mg_flat = sb("mg", [P, 2 * NH * P])
    wraw, wf = m_flat[:, 0:PROJ], mg_flat[:, 0:WCOLS]
    whi = sb("whi", [P, WCOLS], F32R)
    wlo = sb("wlo", [P, WCOLS], F32R)
    wdt_rows = sb("wdt_rows", [NH, DI])
    wdt_in_t = sb("wdt_in_t", [NH, P])
    wn_in = sb("wn_in", [P, 1])
    cw = sb("cw", [P, NB, KC])
    cb = sb("cb", [P, NB])
    bdt = sb("bdt", [P, NB])
    alog = sb("alog", [NH, 1])
    ascale = sb("ascale", [NH, 1])
    dcol = sb("dcol", [P, NB])
    wn_out = sb("wn_out", [P, NB])
    wo_raw = sb("wo_raw", [P, NB, D])
    wo = sb("wo", [P, NB, D])

    h = sb("h", [P, 2, TG, D])
    st6 = sb("st6", [P, TG, 6])
    mv = sb("mv", [P, TG, 2])
    lnt = sb("lnt", [P, 6, TG])
    thi = sb("thi", [P, GT], F32R)
    tlo = sb("tlo", [P, GT], F32R)
    dtv = sb("dtv", [P, NB, GT])
    dta = sb("dta", [P, NB, GT])
    cs = sb("cs", [NH, GT])
    resid1 = sb("resid1", [NH, GT])
    mid = sb("mid", [NH, GT], BF16)
    parts = sb("parts", [P, 2, GT], BF16)
    xraw = sb("xraw", [P, 2, NB, KC - 1 + GT])
    xth = sb("xth", [P, NB, GT])
    xt = sb("xt", [P, 2, NB, GT])
    bt = sb("bt", [P, 2, NP, GT])
    ct = sb("ct", [P, 2, NP, TG, 2, P])
    zth = sb("zth", [P, GT])
    zt = sb("zt", [P, 2, NB, GT])

    edec = sb("edec", [P, 2, NB, P])
    tdec = sb("tdec", [P, 2, NP])
    m = m_flat[:].rearrange("p (b h l) -> p b h l", b=2, h=NH)
    mg = mg_flat[:].rearrange("p (b h l) -> p b h l", b=2, h=NH)
    btok = sb("btok", [P, 2, NP * P])
    xtok = sb("xtok", [P, 2, DI])
    xw = sb("xw", [P, 2, DI])
    state = sb("state", [P, 2, NP, HD])
    decayed = sb("decayed", [P, NP, HD])
    y1 = sb("y1", [P, NB, P])
    y2 = sb("y2", [P, NB, P])
    y3 = sb("y3", [P, NB, P])
    y4 = sb("y4", [P, 2, NB, P])
    ysq = sb("ysq", [P, 2, NB, P])
    og = sb("og", [P, 2, TG, D + 2])
    pt = sb("pt", [P, 6, TG])
    xn = sb("xn", [P, TG, D])
    ob = sb("ob", [P, TG, D])
    pst6 = sb("pst6", [P, TG, 6])
    pmv = sb("pmv", [P, TG, 2])
    xb = sb("xb", [P, TG, D])

    loaded0 = nc.alloc_semaphore("x_first_groups_loaded")
    loaded1 = nc.alloc_semaphore("x_other_groups_loaded")
    w_loaded = nc.alloc_semaphore("weights_loaded")
    const_step = sig("pool_constants_built", 1)
    prep = sig("dve_weights_prepared", 1)
    prep_pe = sig("pe_dt_weights_made", 1)
    prep_act = sig("act_decay_rates_made", 1)

    ln_stats = sig("ln_stats_ready", 2 * TG)
    coef_step = sig("ln1_coefficient_steps", 10)
    h_ready = sig("h_ready", TG)
    fr_done = sig("front_products_done", 16)
    thi_ready = sig("thi_ready")
    tlo_ready = sig("tlo_ready")
    dtv_ready = sig("dtv_ready", NB)
    dta_ready = sig("softplus_tail_ready", 3)
    dtr_ready = sig("softplus_ready", 2)
    scan_ready = sig("log_decay_scanned", TG)
    part_ready = sig("log_decay_parts_ready", 5)
    xraw_ready = sig("xraw_ready", NB)
    hist_ready = sig("conv_history_ready")
    conv_step = sig("conv_steps", NB * KC)
    xth_ready = sig("xth_ready", NB)
    xt_ready = sig("xt_ready", NB)
    bt_ready = sig("bt_ready", NP)
    cta_ready = sig("c_by_act_ready", 4)
    ctd_ready = sig("c_by_dve_ready", 4)
    zth_ready = sig("zth_ready", NB)
    zt_ready = sig("zt_ready", NB)

    btr_done = sig("b_turned")
    xtr_done = sig("x_turned")
    dd_done = sig("log_decays_done", 2)
    gg_done = sig("scores_done", 2)
    ee_done = sig("decay_rows_done")
    oo_done = sig("out_projected")
    yy_done = sig("y_products_done")
    ss_done = sig("state_products_done")
    e_ready = sig("decay_rows_ready", 3)
    m_ready = sig("decays_ready", 2)
    btok_ready = sig("btok_ready")
    xtok_ready = sig("xtok_ready")
    ysq_ready = sig("ysq_ready")
    og_ready = sig("og_ready")
    mm_ready = sig("decays_masked", 2)
    xw_ready = sig("xw_ready", 2)
    dec_ready = sig("state_decayed")
    y4_ready = sig("y_gated")
    mg_ready = sig("scores_decayed", 2)
    state_ready = sig("state_ready", 2)
    y_step = sig("y_steps", 4)
    post_pool1 = sig("post_rms", 2)
    xn_ready = sig("xn_ready", TG)
    post_dve1 = sig("post_stats", 3 * TG)
    post_pool2 = sig("post_ln2", 4)
    xb_ready = sig("xb_ready", TG)
    x2_ready = sig("x2_ready", TG)

    def fr_uses(f, g):
        pieces = [[("h", tlo_ready, f, 1), ("dt0", dta_ready, f, None), ("dt1", dta_ready, f, None),
                   ("x0", xraw_ready, f, 1)],
                  [("x1", xraw_ready, f, 2), ("b0", bt_ready, f, 1), ("b1", bt_ready, f, 2), ("b2", bt_ready, f, 3)],
                  [("b3", bt_ready, f, 4), ("c0", cta_ready, f, 2), ("c1", cta_ready, f, 4),
                   ("a", scan_ready, f, TG)],
                  [("c2", ctd_ready, f, 2), ("c3", ctd_ready, f, 4), ("z0", zt_ready, f, 1), ("z1", zt_ready, f, 2)]]
        pieces[0][1] = ("dt0", dtv_ready, f, 1)
        pieces[0][2] = ("dt1", dtv_ready, f, 2)
        seq = []
        for i in range(TG):
            if g is not None:
                seq.append((("xtr", i), xtok_ready, g * TG + i, 1))
            seq += [((key,), s, n, k) for key, s, n, k in pieces[i]] if f is not None else [None] * 4
        return seq

    BLOCK = {"dt0": O_DT, "dt1": O_DT + P, "x0": O_X, "x1": O_X + P, "z0": 0, "z1": P}
    BLOCK.update({f"b{j}": O_B + j * P for j in range(NP)})
    BLOCK.update({f"c{j}": O_C + j * P for j in range(NP)})
    FR_INDEX = {k: n for n, k in enumerate(
        ["h", "dt0", "dt1", "x0", "x1", "b0", "b1", "b2", "b3", "c0", "c1", "a", "c2", "c3", "z0", "z1"])}

    class Front:

        def __init__(self, g, f, before):
            self.seq, self.before = fr_uses(f, g), before
            self.at = {u[0]: n for n, u in enumerate(self.seq) if u}

        def bank(self, *key):
            return banks[self.at[key] % 2]

        def free(self, eng, *key):
            both = self.before + self.seq
            n = len(self.before) + self.at[key] - 2
            while n >= 0 and both[n] is None:
                n -= 2
            if n >= 0:
                _, s, idx, k = both[n]
                eng.wait_ge(s.sem, s.of(idx, k))

    def load_all(sp):
        small = dict(allow_slow_non_contiguous=True)
        v = hidden.rearrange("b (n p) d -> p (b n) d", p=P)
        first = 2 * TG
        sp.dma_start(xall[:, 0:TG, :], v[:, 0:TG, :]).then_inc(loaded0, 16)
        sp.dma_start(wraw, w_in).then_inc(w_loaded, 16)
        sp.dma_start(xall[:, TG:first, :], v[:, TG:first, :]).then_inc(loaded0, 16)
        cvec = lambda a: a.rearrange("(n p) -> p n", p=P)
        sp.dma_start(wn_in[:], cvec(w_norm_in), **small).then_inc(w_loaded, 16)
        sp.dma_start(cw[:], conv_w.rearrange("(n p) o k -> p n (o k)", p=P)).then_inc(w_loaded, 16)
        sp.dma_start(cb[:], cvec(conv_b), **small).then_inc(w_loaded, 16)
        sp.dma_start(bdt[:], cvec(b_dt), **small).then_inc(w_loaded, 16)
        sp.dma_start(wdt_rows[:], w_dt).then_inc(w_loaded, 16)
        sp.dma_start(alog[:], a_log.rearrange("(h o) -> h o", o=1), **small).then_inc(w_loaded, 16)
        for n in range(NB):
            for q in range(P // HD):
                hh = n * (P // HD) + q
                sp.dma_start(dcol[q * HD:(q + 1) * HD, n:n + 1],
                             d_skip[hh:hh + 1].rearrange("(h o) -> h o", o=1).to_broadcast([HD, 1]), **small
                             ).then_inc(w_loaded, 16)
        sp.dma_start(wn_out[:], cvec(w_norm_out), **small).then_inc(w_loaded, 16)
        sp.dma_start(wo_raw[:], w_out.rearrange("(n p) d -> p n d", p=P)).then_inc(w_loaded, 16)
        sp.dma_start(xall[:, first:TILES, :], v[:, first:TILES, :]).then_inc(loaded1, 16)

    W_LOADS = 17 * 16

    def pool_constants(pl):
        step = [0]

        def then(ins):
            ins.then_inc(const_step.sem, 1)
            step[0] += 1
            pl.wait_ge(const_step.sem, const_step.of(0, step[0]))

        for ap, v in ((ident[:], 0.0), (ones[:], 1.0), (neghalf[:], -0.5), (zeros[:], 0.0), (sel_a[:], 0.0),
                      (negsel[:], 0.0), (sel_e[:], 0.0), (hsum[:], 0.0), (parts[:], 0.0), (ct[:], 0.0),
                      (state[:], 0.0)):
            then(PL.memset(ap, v))
        then(PL.affine_select(out=ident[:], in_=ident[:], compare_op=ALU.not_equal, fill=1.0, base=0,
                              pattern=[[-1, P]], channel_multiplier=1))
        for k in range(PARTS):
            then(PL.affine_select(out=sel_a[:], in_=sel_a[:], compare_op=ALU.not_equal, fill=1.0, base=-32 * k,
                                  pattern=[[-1, NH], [0, P]], channel_multiplier=1))
            then(PL.affine_select(out=negsel[:], in_=negsel[:], compare_op=ALU.not_equal, fill=-1.0, base=-32 * k,
                                  pattern=[[-1, NH], [0, P]], channel_multiplier=1))
            for n in range(NB):
                v = sel_e[:, n, :].rearrange("p (q d) -> p q d", d=HD)
                then(PL.affine_select(out=v, in_=v, compare_op=ALU.not_equal, fill=1.0, base=-32 * k - 4 * n,
                                      pattern=[[-1, P // HD], [0, HD]], channel_multiplier=1))
        for n in range(NB):
            for q in range(P // HD):
                then(PL.memset(hsum[q * HD:(q + 1) * HD, n, n * 4 + q:n * 4 + q + 1], 1.0))
        return step[0]

    CONSTS = 11 + 1 + PARTS * (2 + NB) + NB * 4
    PREP = 14

    def dve_prepare(dve):
        step = [0]

        def then(ins):
            ins.then_inc(prep.sem, 1)
            step[0] += 1
            dve.wait_ge(prep.sem, prep.of(0, step[0]))

        dve.wait_ge(w_loaded, W_LOADS)
        then(DVE.tensor_scalar(wf[:, O_X:O_DT], wraw[:, O_X:O_DT], wn_in[:, 0:1], None, ALU.mult))
        then(DVE.tensor_scalar(wf[:, 0:O_X], wraw[:, 0:O_X], wn_in[:, 0:1], 0.5, ALU.mult, ALU.mult))
        then(DVE.tensor_scalar(cw[:], cw[:], 0.5, None, ALU.mult))
        then(DVE.tensor_scalar(cb[:], cb[:], 0.5, None, ALU.mult))
        for n in range(NB):
            then(DVE.tensor_scalar(wo[:, n, :], wo_raw[:, n, :], wn_out[:, n:n + 1], None, ALU.mult))
        then(DVE.tensor_copy(whi[:, 0:O_DT], wf[:, 0:O_DT]))
        then(DVE.tensor_tensor(wlo[:, 0:O_DT], wf[:, 0:O_DT], whi[:, 0:O_DT].bitcast(F32), ALU.subtract))
        dve.wait_ge(prep_pe.sem, prep_pe.of(0, 1))
        then(DVE.tensor_copy(wdt_in_t[:], banks[7][0:NH, 0:P]))
        dve.wait_ge(prep_pe.sem, prep_pe.of(0, 2))
        then(DVE.tensor_scalar(wf[:, O_DT:WCOLS], banks[6][:, 0:DI], wn_in[:, 0:1], None, ALU.mult))
        then(DVE.tensor_copy(whi[:, O_DT:WCOLS], wf[:, O_DT:WCOLS]))
        then(DVE.tensor_tensor(wlo[:, O_DT:WCOLS], wf[:, O_DT:WCOLS], whi[:, O_DT:WCOLS].bitcast(F32),
                               ALU.subtract))
        dve.wait_ge(prep_act.sem, prep_act.of(0, 1))
        then(DVE.tensor_scalar(ascale[:], alog[:], -1.0 / HD, None, ALU.mult))
        then(DVE.memset(og[:], 0.0))
        assert step[0] == PREP

    def pe_prepare(pe):
        pe.wait_ge(const_step.sem, const_step.of(0, CONSTS))
        pe.wait_ge(w_loaded, W_LOADS)
        PE.transpose(banks[7][0:NH, 0:P], wraw[:, O_DT:PROJ], ident[:]).then_inc(prep_pe.sem, 1)
        pe.wait_ge(prep.sem, prep.of(0, 9))
        PE.matmul(banks[6][:, 0:DI], wdt_in_t[:], wdt_rows[:], start=True, stop=True).then_inc(prep_pe.sem, 1)

    def act_prepare(act):
        act.wait_ge(w_loaded, W_LOADS)
        SE.activation(alog[:], alog[:], ACT.Exp).then_inc(prep_act.sem, 1)

    def dve_stats(dve, f, dyn):
        xg = lambda i: xall[:, dyn(f * TG + i, 1), :].rearrange("p o d -> p (o d)")
        if due(f - 1):
            dve.wait_ge(coef_step.sem, coef_step.of(f - 1))
        for i in range(TG):
            DVE.bn_stats(st6[:, i, :], xg(i)).then_inc(ln_stats.sem, 1)
        for i in range(TG):
            dve.wait_ge(ln_stats.sem, ln_stats.of(f, i + 1))
            apart(dve, f)
            DVE.bn_aggr(mv[:, i, :], st6[:, i, :]).then_inc(ln_stats.sem, 1)

    def pool_norm(pl, f, dyn):
        mean, var = mv[:, :, 0], mv[:, :, 1]
        rs, ns = s1[:, dyn(f * TG, TG)], nb1[:, dyn(f * TG, TG)]
        pl.wait_ge(ln_stats.sem, ln_stats.of(f))
        if due(f - 1):
            pl.wait_ge(h_ready.sem, h_ready.of(f - 1))
        apart(pl, f)
        PL.tensor_scalar(lnt[:, 0, :], var, LN_EPS, None, ALU.add).then_inc(coef_step.sem, 1)
        pl.wait_ge(coef_step.sem, coef_step.of(f, 1))
        apart(pl, f)
        PL.tensor_tensor(rs, lnt[:, 0, :], neghalf[:], ALU.pow).then_inc(coef_step.sem, 1)
        pl.wait_ge(coef_step.sem, coef_step.of(f, 2))
        apart(pl, f)
        PL.tensor_tensor(lnt[:, 1, :], rs, rs, ALU.mult).then_inc(coef_step.sem, 1)
        pl.wait_ge(coef_step.sem, coef_step.of(f, 3))
        apart(pl, f)
        PL.tensor_tensor(lnt[:, 2, :], lnt[:, 1, :], var, ALU.mult).then_inc(coef_step.sem, 1)
        pl.wait_ge(coef_step.sem, coef_step.of(f, 4))
        apart(pl, f)
        PL.tensor_scalar(lnt[:, 3, :], lnt[:, 2, :], RMS_EPS, None, ALU.add).then_inc(coef_step.sem, 1)
        pl.wait_ge(coef_step.sem, coef_step.of(f, 5))
        apart(pl, f)
        PL.tensor_tensor(lnt[:, 4, :], lnt[:, 3, :], neghalf[:], ALU.pow).then_inc(coef_step.sem, 1)
        pl.wait_ge(coef_step.sem, coef_step.of(f, 6))
        apart(pl, f)
        PL.tensor_tensor(lnt[:, 0, :], lnt[:, 4, :], rs, ALU.mult).then_inc(coef_step.sem, 1)
        pl.wait_ge(coef_step.sem, coef_step.of(f, 7))
        apart(pl, f)
        PL.tensor_scalar(lnt[:, 5, :], mean, -1.0, None, ALU.mult).then_inc(coef_step.sem, 1)
        pl.wait_ge(coef_step.sem, coef_step.of(f, 8))
        apart(pl, f)
        PL.tensor_tensor(ns, lnt[:, 5, :], rs, ALU.mult).then_inc(coef_step.sem, 1)
        pl.wait_ge(coef_step.sem, coef_step.of(f, 9))
        apart(pl, f)
        PL.tensor_tensor(lnt[:, 1, :], lnt[:, 5, :], lnt[:, 0, :], ALU.mult).then_inc(coef_step.sem, 1)

    def dve_h(dve, f, par, dyn):
        dve.wait_ge(coef_step.sem, coef_step.of(f))
        if due(f - 2):
            dve.wait_ge(fr_done.sem, fr_done.of(f - 2, 1))
        for i in range(TG):
            x = xall[:, dyn(f * TG + i, 1), :].rearrange("p o d -> p (o d)")
            DVE.tensor_scalar(h[:, par, i, :], x, lnt[:, 0, i:i + 1], lnt[:, 1, i:i + 1],
                              ALU.mult, ALU.add).then_inc(h_ready.sem, 1)

    def pe_front(pe, f, par, fr, piece):
        keys = [["h", "dt0", "dt1", "x0"], ["x1", "b0", "b1", "b2"], ["b3", "c0", "c1", "a"],
                ["c2", "c3", "z0", "z1"]][piece]
        for key in keys:
            bank = fr.bank(key)
            fr.free(pe, key)
            if key == "h":
                pe.wait_ge(h_ready.sem, h_ready.of(f))
                for i in range(TG):
                    mm = PE.transpose(bank[:, col(i)], h[:, par, i, :], ident[:])
            elif key == "a":
                pe.wait_ge(dtr_ready.sem, dtr_ready.of(f))
                for n in range(NB):
                    mm = PE.matmul(bank[0:NH, :], hsum[:, n, :], dtv[:, n, :], start=n == 0, stop=n == NB - 1)
            else:
                if key == "dt0":
                    pe.wait_ge(thi_ready.sem, thi_ready.of(f))
                    pe.wait_ge(tlo_ready.sem, tlo_ready.of(f))
                    pe.wait_ge(prep.sem, prep.of(0, PREP))
                w = slice(BLOCK[key], BLOCK[key] + P)
                PE.matmul(bank[:], whi[:, w], thi[:], start=True, stop=False)
                PE.matmul(bank[:], whi[:, w], tlo[:], start=False, stop=False)
                mm = PE.matmul(bank[:], wlo[:, w], thi[:], start=False, stop=True)
            mm.then_inc(fr_done.sem, 1)

    def fdone(eng, f, key):
        eng.wait_ge(fr_done.sem, fr_done.of(f, FR_INDEX[key] + 1))

    def act_front(act, f, par, fr, piece):
        if piece == 0:
            fdone(act, f, "h")
            if due(f - 1):
                act.wait_ge(fr_done.sem, fr_done.of(f - 1, 16))
            SE.activation(thi[:], fr.bank("h")[:], ACT.Copy).then_inc(thi_ready.sem, 1)
            fdone(act, f, "x0")
            if due(f - 1):
                act.wait_ge(hist_ready.sem, hist_ready.of(f - 1))
            if due(f - 2):
                act.wait_ge(conv_step.sem, conv_step.of(f - 2))
            SE.activation(xraw[:, par, 0, KC - 1:], fr.bank("x0")[:], ACT.Copy).then_inc(xraw_ready.sem, 1)
        if piece == 1:
            fdone(act, f, "x1")
            SE.activation(xraw[:, par, 1, KC - 1:], fr.bank("x1")[:], ACT.Copy).then_inc(xraw_ready.sem, 1)
            act.wait_ge(dtv_ready.sem, dtv_ready.of(f))
            if due(f - 1):
                act.wait_ge(dtr_ready.sem, dtr_ready.of(f - 1))
            SE.activation(dta[:], dtv[:], ACT.Abs).then_inc(dta_ready.sem, 1)
            act.wait_ge(dta_ready.sem, dta_ready.of(f, 1))
            SE.activation(dta[:], dta[:], ACT.Exp, scale=-1.0).then_inc(dta_ready.sem, 1)
            if due(f - 2):
                act.wait_ge(gg_done.sem, gg_done.of((f - 2) * TG + TG - 1))
            for j in range(3):
                fdone(act, f, f"b{j}")
                SE.activation(bt[:, par, j, :], fr.bank(f"b{j}")[:], ACT.Copy).then_inc(bt_ready.sem, 1)
            act.wait_ge(dta_ready.sem, dta_ready.of(f, 2))
            SE.activation(dta[:], dta[:], ACT.Ln, bias=1.0).then_inc(dta_ready.sem, 1)
        if piece == 2:
            fdone(act, f, "b3")
            SE.activation(bt[:, par, 3, :], fr.bank("b3")[:], ACT.Copy).then_inc(bt_ready.sem, 1)
            if due(f - 2):
                act.wait_ge(yy_done.sem, yy_done.of((f - 2) * TG + TG - 1))
            for j in range(2):
                fdone(act, f, f"c{j}")
                split_c(SE.copy, j, par, fr, cta_ready)
            for n in range(NB):
                act.wait_ge(conv_step.sem, conv_step.of(f, (KC - 1) * NB + n + 1))
                if due(f - 1):
                    act.wait_ge(xt_ready.sem, xt_ready.of(f - 1))
                SE.activation(xth[:, n, :], xt[:, par, n, :], ACT.Tanh).then_inc(xth_ready.sem, 1)
        if piece == 3:
            for n in range(NB):
                fdone(act, f, f"z{n}")
                if n:
                    act.wait_ge(zt_ready.sem, zt_ready.of(f, n))
                else:
                    if due(f - 1):
                        act.wait_ge(zt_ready.sem, zt_ready.of(f - 1))
                SE.activation(zth[:], fr.bank(f"z{n}")[:], ACT.Tanh).then_inc(zth_ready.sem, 1)

    def split_c(copy, j, par, fr, ready):
        for q in range(2):
            rows = slice(q * NS, (q + 1) * NS)
            copy(ct[rows, par, j, :, q, :], fr.bank(f"c{j}")[rows, :].rearrange("p (t l) -> p t l", l=P)
                 ).then_inc(ready.sem, 1)

    def dve_front(dve, f, par, fr, piece):
        if piece == 0:
            dve.wait_ge(thi_ready.sem, thi_ready.of(f))
            if due(f - 1):
                dve.wait_ge(fr_done.sem, fr_done.of(f - 1, 16))
            DVE.tensor_tensor(tlo[:], fr.bank("h")[:], thi[:].bitcast(F32), ALU.subtract).then_inc(tlo_ready.sem, 1)
            for n in range(NB):
                fdone(dve, f, f"dt{n}")
                if n == 0:
                    if due(f - 1):
                        dve.wait_ge(fr_done.sem, fr_done.of(f - 1, FR_INDEX["a"] + 1))
                DVE.tensor_scalar(dtv[:, n, :], fr.bank(f"dt{n}")[:], bdt[:, n:n + 1], None,
                                  ALU.add).then_inc(dtv_ready.sem, 1)
        if piece == 1:
            dve.wait_ge(hist_ready.sem, hist_ready.of(f))
            if due(f - 2):
                dve.wait_ge(y_step.sem, y_step.of((f - 2) * TG + TG - 1))
            for k in range(KC):
                for n in range(NB):
                    dve.wait_ge(xraw_ready.sem, xraw_ready.of(f, n + 1))
                    src = xraw[:, par, n, k:k + GT]
                    if k == 0:
                        ins = DVE.tensor_scalar(xt[:, par, n, :], src, cw[:, n, 0:1], cb[:, n:n + 1], ALU.mult, ALU.add)
                    else:
                        dve.wait_ge(conv_step.sem, conv_step.of(f, (k - 1) * NB + n + 1))
                        ins = DVE.scalar_tensor_tensor(out=xt[:, par, n, :], in0=src, scalar=cw[:, n, k:k + 1],
                                                       in1=xt[:, par, n, :], op0=ALU.mult, op1=ALU.add)
                    ins.then_inc(conv_step.sem, 1)
        if piece == 2:
            for n in range(NB):
                dve.wait_ge(xth_ready.sem, xth_ready.of(f, n + 1))
                DVE.scalar_tensor_tensor(out=xt[:, par, n, :], in0=xth[:, n, :], scalar=1.0, in1=xt[:, par, n, :],
                                         op0=ALU.add, op1=ALU.mult).then_inc(xt_ready.sem, 1)
            fdone(dve, f, "a")
            if due(f - 1):
                dve.wait_ge(part_ready.sem, part_ready.of(f - 1))
            for i in range(TG):
                DVE.tensor_tensor_scan(cs[:, col(i)], ones[0:NH, :], fr.bank("a")[0:NH, col(i)], 0.0,
                                       ALU.mult, ALU.add).then_inc(scan_ready.sem, 1)
        if piece == 3:
            for j in (2, 3):
                fdone(dve, f, f"c{j}")
                if j == 2:
                    if due(f - 2):
                        dve.wait_ge(yy_done.sem, yy_done.of((f - 2) * TG + TG - 1))
                split_c(DVE.tensor_copy, j, par, fr, ctd_ready)
            dve.wait_ge(scan_ready.sem, scan_ready.of(f))
            if due(f - 2):
                dve.wait_ge(ee_done.sem, ee_done.of((f - 2) * TG + TG - 1))
            pr = lambda k: parts[32 * k:32 * k + NH, par, :]
            DVE.tensor_scalar(pr(0), cs[:], ascale[:, 0:1], None, ALU.mult).then_inc(part_ready.sem, 1)
            dve.wait_ge(part_ready.sem, part_ready.of(f, 1))
            DVE.scalar_tensor_tensor(out=resid1[:], in0=cs[:], scalar=ascale[:, 0:1], in1=pr(0),
                                     op0=ALU.mult, op1=ALU.subtract).then_inc(part_ready.sem, 1)
            dve.wait_ge(part_ready.sem, part_ready.of(f, 2))
            DVE.tensor_copy(pr(1), resid1[:]).then_inc(part_ready.sem, 1)
            DVE.tensor_copy(mid[:], resid1[:]).then_inc(part_ready.sem, 1)
            for n in range(NB):
                dve.wait_ge(zth_ready.sem, zth_ready.of(f, n + 1))
                DVE.scalar_tensor_tensor(out=zt[:, par, n, :], in0=zth[:], scalar=1.0, in1=fr.bank(f"z{n}")[:],
                                         op0=ALU.add, op1=ALU.mult).then_inc(zt_ready.sem, 1)
                if n == 0:
                    dve.wait_ge(part_ready.sem, part_ready.of(f, 4))
                    DVE.tensor_tensor(pr(2), resid1[:], mid[:], ALU.subtract).then_inc(part_ready.sem, 1)

    def pool_front(pl, f, par, piece, first_of_batch):
        if piece == 0:
            if due(f - 2):
                pl.wait_ge(conv_step.sem, conv_step.of(f - 2))
            for_hist = xraw[:, par, :, 0:KC - 1]
            if first_of_batch:
                apart(pl, f)
                ins = PL.memset(for_hist, 0.0)
            else:
                if due(f - 1):
                    pl.wait_ge(xraw_ready.sem, xraw_ready.of(f - 1))
                apart(pl, f)
                ins = PL.tensor_copy(for_hist, xraw[:, 1 - par, :, GT:GT + KC - 1])
            ins.then_inc(hist_ready.sem, 1)
        if piece == 1:
            pl.wait_ge(dta_ready.sem, dta_ready.of(f, 1))
            apart(pl, f)
            PL.tensor_scalar(dtv[:], dtv[:], 0.0, None, ALU.max).then_inc(dtr_ready.sem, 1)
            pl.wait_ge(dtr_ready.sem, dtr_ready.of(f, 1))
            pl.wait_ge(dta_ready.sem, dta_ready.of(f))
            apart(pl, f)
            PL.tensor_tensor(dtv[:], dtv[:], dta[:], ALU.add).then_inc(dtr_ready.sem, 1)

    def pe_scores(pe, t, i, g, par, tp, fr):
        c = col(i)
        if i == 0:
            pe.wait_ge(bt_ready.sem, bt_ready.of(g))
            pe.wait_ge(cta_ready.sem, cta_ready.of(g))
            pe.wait_ge(ctd_ready.sem, ctd_ready.of(g))
            pe.wait_ge(part_ready.sem, part_ready.of(g))
            pe.wait_ge(xt_ready.sem, xt_ready.of(g))
        if due(t - 1):
            pe.wait_ge(state_ready.sem, state_ready.of(t - 1))
        for j in range(NP):
            mm = PE.transpose(banks[7][:, col(j)], bt[:, par, j, c], ident[:])
        mm.then_inc(btr_done.sem, 1)
        for hf in range(2):
            bank = banks[2 + hf]
            if due(t - 1):
                pe.wait_ge(m_ready.sem, m_ready.of(t - 1, hf + 1))
            PE.matmul(bank[:], parts[:, par, c], negsel[:, hf * HH:(hf + 1) * HH, :], start=True, stop=False,
                      skip_group_check=True)
            for q in range(HH):
                mm = PE.matmul(bank[:, col(q)], sel_a[:, hf * HH + q, :], parts[:, par, c], start=False,
                               stop=q == HH - 1, skip_group_check=True)
            mm.then_inc(dd_done.sem, 1)
        fr.free(pe, "xtr", i)
        for n in range(NB):
            mm = PE.transpose(fr.bank("xtr", i)[:, col(n)], xt[:, par, n, c], ident[:])
        mm.then_inc(xtr_done.sem, 1)
        for hf in range(2):
            bank = banks[4 + hf]
            if due(t - 1):
                pe.wait_ge(mg_ready.sem, mg_ready.of(t - 1, hf + 1))
            for j in range(2):
                mm = PE.matmul(bank[:, col(j, 2 * P)], bt[:, par, 2 * hf + j, c], ct[:, par, 2 * hf + j, i, :, :],
                               start=True, stop=True)
            mm.then_inc(gg_done.sem, 1)
        if due(t - 1):
            pe.wait_ge(y_step.sem, y_step.of(t - 1, 3))
        for n in range(NB):
            PE.matmul(banks[6][:, col(n)], sel_e[:, n, :], parts[:, par, c], start=True, stop=True,
                      skip_group_check=True)
        last = parts[:, par, i * P + P - 1:i * P + P]
        PE.matmul(banks[6][:, DI:DI + NH], last.to_broadcast([P, P]), sel_a[:, :, 0], start=True, stop=True,
                  skip_group_check=True).then_inc(ee_done.sem, 1)

    def pe_out_tile(pe, t, tp, last=False):
        pe.wait_ge(y4_ready.sem, y4_ready.of(t))
        pe.wait_ge(ysq_ready.sem, ysq_ready.of(t))
        if last:
            pe.wait_ge(state_ready.sem, state_ready.of(t))
        else:
            pe.wait_ge(btok_ready.sem, btok_ready.of(t + 1))
        bank = banks[7]
        for n in range(NB):
            PE.matmul(bank[:, 0:D], y4[:, tp, n, :], wo[:, n, :], start=n == 0, stop=n == NB - 1)
        for n in range(NB):
            mm = PE.matmul(bank[:, D:2 * D], ysq[:, tp, n, :], ones[:], start=n == 0, stop=n == NB - 1)
        mm.then_inc(oo_done.sem, 1)

    def pe_y(pe, t, i, g, par, tp, first_tile):
        pe.wait_ge(xtok_ready.sem, xtok_ready.of(t))
        pe.wait_ge(e_ready.sem, e_ready.of(t))
        pe.wait_ge(mg_ready.sem, mg_ready.of(t, 1))
        for hd in range(NH):
            if hd == HH:
                pe.wait_ge(mg_ready.sem, mg_ready.of(t, 2))
            q, n = hd % 4, hd // 4
            PE.matmul(banks[6][q * HD:(q + 1) * HD, col(n)], xtok[:, tp, hd * HD:(hd + 1) * HD], mg[:, tp, hd, :],
                      start=True, stop=True, skip_group_check=True)
        if due(t - 1):
            pe.wait_ge(state_ready.sem, state_ready.of(t - 1))
        for hd in range(NH):
            q, n = hd % 4, hd // 4
            mm = PE.matmul(banks[6][q * HD:(q + 1) * HD, DI + n * P:DI + (n + 1) * P],
                           state[:, 1 - tp, hd // 2, :], ct[:, par, hd // 2, i, hd % 2, :],
                           start=True, stop=True, skip_group_check=True)
        mm.then_inc(yy_done.sem, 1)
        pe.wait_ge(btok_ready.sem, btok_ready.of(t))
        pe.wait_ge(xw_ready.sem, xw_ready.of(t))
        if due(t - 1):
            pe.wait_ge(og_ready.sem, og_ready.of(t - 1))
        for j in range(NP):
            n = j // 2
            mm = PE.matmul(banks[7][:, col(j)], btok[:, tp, col(j)], xw[:, tp, col(n)], start=True, stop=True,
                           skip_group_check=True)
        mm.then_inc(ss_done.sem, 1)

    def act_tile(act, t, i, g, par, tp, fr):
        act.wait_ge(btr_done.sem, btr_done.of(t))
        if due(t - 2):
            act.wait_ge(ss_done.sem, ss_done.of(t - 2))
        SE.activation(btok[:, tp, :], banks[7][:], ACT.Copy).then_inc(btok_ready.sem, 1)
        for hf in range(2):
            act.wait_ge(dd_done.sem, dd_done.of(t, hf + 1))
            if hf == 0:
                if due(t - 2):
                    act.wait_ge(mg_ready.sem, mg_ready.of(t - 2))
                    act.wait_ge(xw_ready.sem, xw_ready.of(t - 2))
            SE.activation(m[:, tp, hf * HH:(hf + 1) * HH, :], banks[2 + hf][:].rearrange("p (h l) -> p h l", l=P),
                          ACT.Exp).then_inc(m_ready.sem, 1)
        act.wait_ge(xtr_done.sem, xtr_done.of(t))
        if due(t - 2):
            act.wait_ge(yy_done.sem, yy_done.of(t - 2))
            act.wait_ge(xw_ready.sem, xw_ready.of(t - 2))
        SE.activation(xtok[:, tp, :], fr.bank("xtr", i)[:, 0:DI], ACT.Copy).then_inc(xtok_ready.sem, 1)
        act.wait_ge(ee_done.sem, ee_done.of(t))
        if due(t - 2):
            act.wait_ge(y_step.sem, y_step.of(t - 2))
            act.wait_ge(dec_ready.sem, dec_ready.of(t - 2))
        SE.activation(edec[:, tp, :, :], banks[6][:, 0:DI].rearrange("p (n l) -> p n l", l=P),
                      ACT.Exp).then_inc(e_ready.sem, 1)
        for q in range(2):
            rows = slice(q * NS, (q + 1) * NS)
            SE.activation(tdec[rows, tp, :], banks[6][rows, DI + q:DI + NH:2], ACT.Exp).then_inc(e_ready.sem, 1)

    def act_square(act, t, tp):
        act.wait_ge(y4_ready.sem, y4_ready.of(t))
        if due(t - 2):
            act.wait_ge(oo_done.sem, oo_done.of(t - 2))
        SE.activation(ysq[:, tp, :, :], y4[:, tp, :, :], ACT.Square).then_inc(ysq_ready.sem, 1)

    def act_out(act, t, i, par, g):
        if i == 0:
            if due(g - 2):
                act.wait_ge(post_dve1.sem, post_dve1.of(g - 2))
        act.wait_ge(oo_done.sem, oo_done.of(t))
        SE.activation(og[:, par, i, 0:D + 1], banks[7][:, 0:D + 1], ACT.Copy).then_inc(og_ready.sem, 1)

    def pool_tile(pl, t, i, g, par, tp, first_tile):
        for hf in range(2):
            v = m[:, tp, hf * HH:(hf + 1) * HH, :]
            pl.wait_ge(m_ready.sem, m_ready.of(t, hf + 1))
            apart(pl, t)
            PL.affine_select(out=v, in_=v, compare_op=ALU.is_ge, fill=0.0, base=0, pattern=[[0, HH], [1, P]],
                             channel_multiplier=-1).then_inc(mm_ready.sem, 1)
        pl.wait_ge(xtok_ready.sem, xtok_ready.of(t))
        if due(t - 2):
            pl.wait_ge(ss_done.sem, ss_done.of(t - 2))
        for hf in range(2):
            pl.wait_ge(mm_ready.sem, mm_ready.of(t, hf + 1))
            apart(pl, t)
            PL.tensor_tensor(xw[:, tp, col(hf)].rearrange("p (h d) -> p h d", d=HD),
                             xtok[:, tp, col(hf)].rearrange("p (h d) -> p h d", d=HD),
                             m[:, tp, hf * HH:(hf + 1) * HH, P - 1:P].to_broadcast([P, HH, HD]),
                             ALU.mult).then_inc(xw_ready.sem, 1)
        pl.wait_ge(e_ready.sem, e_ready.of(t))
        if due(t - 1):
            pl.wait_ge(state_ready.sem, state_ready.of(t - 1))
        apart(pl, t)
        PL.tensor_tensor(decayed[:], state[:, 1 - tp, :, :],
                         tdec[:, tp, :].rearrange("p (j o) -> p j o", o=1).to_broadcast([P, NP, HD]),
                         ALU.mult).then_inc(dec_ready.sem, 1)

    def pool_gate(pl, t, i, par, tp):
        pl.wait_ge(y_step.sem, y_step.of(t))
        if due(t - 2):
            pl.wait_ge(oo_done.sem, oo_done.of(t - 2))
        apart(pl, t)
        PL.tensor_tensor(y4[:, tp, :, :], y3[:], zt[:, par, :, col(i)], ALU.mult).then_inc(y4_ready.sem, 1)

    def dve_scores(dve, t, tp):
        if due(t - 2):
            dve.wait_ge(yy_done.sem, yy_done.of(t - 2))
        for hf in range(2):
            heads = slice(hf * HH, (hf + 1) * HH)
            dve.wait_ge(gg_done.sem, gg_done.of(t, hf + 1))
            dve.wait_ge(mm_ready.sem, mm_ready.of(t, hf + 1))
            DVE.tensor_tensor(mg[:, tp, heads, :], banks[4 + hf][:].rearrange("p (h l) -> p h l", l=P),
                              m[:, tp, heads, :], ALU.mult).then_inc(mg_ready.sem, 1)

    def dve_y(dve, t, i, par, tp):
        dve.wait_ge(yy_done.sem, yy_done.of(t))
        dve.wait_ge(e_ready.sem, e_ready.of(t))
        DVE.tensor_tensor(y1[:], banks[6][:, DI:2 * DI].rearrange("p (n l) -> p n l", l=P), edec[:, tp, :, :],
                          ALU.mult).then_inc(y_step.sem, 1)
        for n in range(NB):
            DVE.scalar_tensor_tensor(out=y2[:, n, :], in0=xt[:, par, n, col(i)], scalar=dcol[:, n:n + 1],
                                     in1=banks[6][:, col(n)], op0=ALU.mult, op1=ALU.add).then_inc(y_step.sem, 1)
        dve.wait_ge(y_step.sem, y_step.of(t, 3))
        if due(t - 1):
            dve.wait_ge(y4_ready.sem, y4_ready.of(t - 1))
        DVE.tensor_tensor(y3[:], y1[:], y2[:], ALU.add).then_inc(y_step.sem, 1)

    def dve_state(dve, t, tp, last_of_batch):
        dve.wait_ge(ss_done.sem, ss_done.of(t))
        dve.wait_ge(dec_ready.sem, dec_ready.of(t))
        for q in range(2):
            rows = slice(q * NS, (q + 1) * NS)
            if last_of_batch:
                DVE.memset(state[rows, tp, :, :], 0.0).then_inc(state_ready.sem, 1)
                continue
            s = banks[7][rows, :].rearrange("p (n k d) -> p n k d", n=NB, d=HD)[:, :, q:q + 7:6, :]
            DVE.tensor_tensor(state[rows, tp, :, :].rearrange("p (n j) d -> p n j d", n=2), s,
                              decayed[rows, :, :].rearrange("p (n j) d -> p n j d", n=2),
                              ALU.add).then_inc(state_ready.sem, 1)

    def pool_post1(pl, g, par):
        pl.wait_ge(og_ready.sem, og_ready.of(g * TG + TG - 1))
        apart(pl, g)
        PL.tensor_scalar(pt[:, 0, :], og[:, par, :, D], 1.0 / DI, RMS_EPS, ALU.mult, ALU.add
                         ).then_inc(post_pool1.sem, 1)
        pl.wait_ge(post_pool1.sem, post_pool1.of(g, 1))
        apart(pl, g)
        PL.tensor_tensor(pt[:, 1, :], pt[:, 0, :], neghalf[:], ALU.pow).then_inc(post_pool1.sem, 1)

    def dve_xn(dve, g, dyn):
        for i in range(TG):
            t1 = dyn(g * TG + i, 1)
            DVE.tensor_scalar(xn[:, i, :], xall[:, t1, :].rearrange("p o d -> p (o d)"), s1[:, t1], nb1[:, t1],
                              ALU.mult, ALU.add).then_inc(xn_ready.sem, 1)

    def dve_post1(dve, g, par):
        dve.wait_ge(post_pool1.sem, post_pool1.of(g))
        for i in range(TG):
            dve.wait_ge(xn_ready.sem, xn_ready.of(g, i + 1))
            DVE.scalar_tensor_tensor(out=ob[:, i, :], in0=og[:, par, i, 0:D], scalar=pt[:, 1, i:i + 1],
                                     in1=xn[:, i, :], op0=ALU.mult, op1=ALU.add).then_inc(post_dve1.sem, 1)
        for i in range(TG):
            dve.wait_ge(post_dve1.sem, post_dve1.of(g, i + 1))
            DVE.bn_stats(pst6[:, i, :], ob[:, i, :]).then_inc(post_dve1.sem, 1)
        for i in range(TG):
            dve.wait_ge(post_dve1.sem, post_dve1.of(g, TG + i + 1))
            apart(dve, g)
            DVE.bn_aggr(pmv[:, i, :], pst6[:, i, :]).then_inc(post_dve1.sem, 1)

    def pool_post2(pl, g):
        pl.wait_ge(post_dve1.sem, post_dve1.of(g))
        apart(pl, g)
        PL.tensor_scalar(pt[:, 2, :], pmv[:, :, 1], LN_EPS, None, ALU.add).then_inc(post_pool2.sem, 1)
        pl.wait_ge(post_pool2.sem, post_pool2.of(g, 1))
        apart(pl, g)
        PL.tensor_tensor(pt[:, 3, :], pt[:, 2, :], neghalf[:], ALU.pow).then_inc(post_pool2.sem, 1)
        pl.wait_ge(post_pool2.sem, post_pool2.of(g, 2))
        apart(pl, g)
        PL.tensor_scalar(pt[:, 4, :], pmv[:, :, 0], -1.0, None, ALU.mult).then_inc(post_pool2.sem, 1)
        pl.wait_ge(post_pool2.sem, post_pool2.of(g, 3))
        apart(pl, g)
        PL.tensor_tensor(pt[:, 5, :], pt[:, 4, :], pt[:, 3, :], ALU.mult).then_inc(post_pool2.sem, 1)

    def dve_post2(dve, g, dyn):
        dve.wait_ge(post_pool2.sem, post_pool2.of(g))
        for i in range(TG):
            DVE.tensor_scalar(xb[:, i, :], xall[:, dyn(g * TG + i, 1), :].rearrange("p o d -> p (o d)"),
                              pt[:, 5, i:i + 1], None, ALU.add).then_inc(xb_ready.sem, 1)
        for i in range(TG):
            dve.wait_ge(xb_ready.sem, xb_ready.of(g, i + 1))
            DVE.scalar_tensor_tensor(out=xall[:, dyn(g * TG + i, 1), :].rearrange("p o d -> p (o d)"),
                                     in0=ob[:, i, :], scalar=pt[:, 3, i:i + 1],
                                     in1=xb[:, i, :], op0=ALU.mult, op1=ALU.add).then_inc(x2_ready.sem, 1)

    def run(eng, what, b, u, last):
        g = b * GB + u
        dyn = static if isinstance(b, int) else dynamic
        par = u
        ahead = not (last and u == GB - 1)
        f = g + 1 if ahead else None
        prior = fr_uses(g, g - 1 if not (isinstance(g, int) and g == 0) else None)
        if isinstance(g, int) and g == 0:
            prior = [x for x in prior if x]
        fr = Front(g, f, prior)
        norm = not (last)
        for i in range(TG):
            t, tp = g * TG + i, i % 2
            what(eng, t=t, i=i, g=g, f=f, par=par, tp=tp, fr=fr, dyn=dyn, norm=norm,
                 end_of_batch=u == GB - 1 and i == TG - 1, begin=isinstance(t, int) and t == 0, fu=(u + 1) % GB)

    def pe_body(pe, t, i, g, f, par, tp, fr, dyn, norm, end_of_batch, begin, fu):
        pe_scores(pe, t, i, g, par, tp, fr)
        if not begin:
            pe_out_tile(pe, t - 1, 1 - tp)
        if f is not None:
            pe_front(pe, f, fu, fr, i)
        pe_y(pe, t, i, g, par, tp, begin)

    def act_body(act, t, i, g, f, par, tp, fr, dyn, norm, end_of_batch, begin, fu):
        act_tile(act, t, i, g, par, tp, fr)
        if not begin:
            act_square(act, t - 1, 1 - tp)
            act_out(act, t - 1, (i - 1) % TG, par if i else 1 - par, g)
        if f is not None:
            act_front(act, f, fu, fr, i)

    def dve_body(dve, t, i, g, f, par, tp, fr, dyn, norm, end_of_batch, begin, fu):
        dve_scores(dve, t, tp)
        if f is not None:
            dve_front(dve, f, fu, fr, i)
        dve_y(dve, t, i, par, tp)
        dve_state(dve, t, tp, end_of_batch)
        has_post = not (isinstance(g, int) and g == 0)
        if i == 1 and has_post:
            dve_xn(dve, g - 1, dyn)
            dve_post1(dve, g - 1, 1 - par)
        if i == 2 and has_post:
            dve_post2(dve, g - 1, dyn)
        if i == 2 and norm:
            dve_stats(dve, g + 2, dyn)
        if i == 3 and norm:
            dve_h(dve, g + 2, par, dyn)

    def pool_body(pl, t, i, g, f, par, tp, fr, dyn, norm, end_of_batch, begin, fu):
        pool_tile(pl, t, i, g, par, tp, begin)
        if f is not None:
            pool_front(pl, f, fu, i, fu == 0)
        has_post = not (isinstance(g, int) and g == 0)
        if i == 1 and has_post:
            pool_post1(pl, g - 1, 1 - par)
        pool_gate(pl, t, i, par, tp)
        if i == 1 and has_post:
            pool_post2(pl, g - 1)
        if i == 2 and norm:
            if isinstance(g, int) and g == 0:
                pl.wait_ge(loaded1, 16)
            pool_norm(pl, g + 2, dyn)

    def over_sequences(eng, body):
        for u in range(GB):
            run(eng, body, 0, u, False)
        with eng.Fori(1, BATCH - 1) as b:
            for u in range(GB):
                run(eng, body, b, u, False)
        for u in range(GB):
            run(eng, body, BATCH - 1, u, True)

    G_LAST, T_LAST = GROUPS - 1, TILES - 1
    with nc.Block() as block:
        @block.sync
        def _(sp):
            load_all(sp)

        @block.tensor
        def _(pe):
            pe_prepare(pe)
            fr = Front(None, 0, [])
            for piece in range(4):
                pe_front(pe, 0, 0, fr, piece)
            over_sequences(pe, pe_body)
            pe_out_tile(pe, T_LAST, T_LAST % 2, last=True)

        @block.scalar
        def _(act):
            act_prepare(act)
            fr = Front(None, 0, [])
            for piece in range(4):
                act_front(act, 0, 0, fr, piece)
            over_sequences(act, act_body)
            act_square(act, T_LAST, T_LAST % 2)
            act_out(act, T_LAST, TG - 1, 1, G_LAST)

        @block.vector
        def _(dve):
            dve.wait_ge(loaded0, 32)
            dve_stats(dve, 0, static)
            dve_h(dve, 0, 0, static)
            dve_stats(dve, 1, static)
            dve_prepare(dve)
            dve_h(dve, 1, 1, static)
            dve.wait_ge(const_step.sem, const_step.of(0, CONSTS))
            fr = Front(None, 0, [])
            for piece in range(4):
                dve_front(dve, 0, 0, fr, piece)
            dve.wait_ge(loaded1, 16)
            over_sequences(dve, dve_body)
            dve_xn(dve, G_LAST, static)
            dve_post1(dve, G_LAST, 1)
            dve_post2(dve, G_LAST, static)

        @block.gpsimd
        def _(pl):
            assert pool_constants(pl) == CONSTS
            pl.wait_ge(loaded0, 32)
            pool_norm(pl, 0, static)
            pool_norm(pl, 1, static)
            for piece in range(4):
                pool_front(pl, 0, 0, piece, True)
            over_sequences(pl, pool_body)
            pool_post1(pl, G_LAST, 1)
            pool_post2(pl, G_LAST)


def experts(nc, buffers, xall, banks, wg_d, w1_d, b1_d, w2_d, b2_d, out):
    def sb(name, shape, dt=F32):
        return buffers.enter_context(nc.sbuf_tensor("moe_" + name, shape, dt))

    def sig(name, per=1):
        return Signal(nc, "moe_" + name, per)

    PE, DVE, SE, PL = nc.tensor, nc.vector, nc.scalar, nc.gpsimd

    ident = sb("ident", [P, P])
    neghalf = sb("neghalf", [P, TG])
    ones3 = sb("ones3", [P, P], BF16)
    b2p = sb("b2_parts", [P, NE * D], BF16)
    b2row = sb("b2_row", [1, NE * D])
    b2res = sb("b2_rest", [1, NE * D])
    b2mid = sb("b2_mid", [1, NE * D], BF16)
    w1f = sb("w1", [P, NE, FH])
    w1hi = sb("w1_hi", [P, NE, FH], F32R)
    w1lo = sb("w1_lo", [P, NE, FH], F32R)
    w2 = sb("w2", [P, NE, FB, D])
    wg = sb("wg", [P, NE])
    b1row = sb("b1_rows", [NE * FB, P])
    b1 = sb("b1", [P, NE * FB])
    rank = sb("rank", [P, TG, NE])
    iota = sb("iota", [P, TG, NE])

    st6 = sb("st6", [P, TG, 6])
    mv = sb("mv", [P, TG, 2])
    lnt = sb("lnt", [P, 4, TG])
    h = sb("h", [P, TG, D])
    thi = sb("t_hi", [P, 2, GT], F32R)
    tlo = sb("t_lo", [P, 2, GT], F32R)
    tf = sb("t", [P, GT])
    route = sb("route", [P, 10, TG, NE])
    rmax = sb("rmax", [P, 6, TG])
    scores = sb("scores", [P, 2, TG, NE])
    hid = sb("hid", [P, 2, FB, GT])
    acc = sb("acc", [P, 2, TG, D])
    post = sb("post", [P, 4, TG])
    pst6 = sb("pst6", [P, TG, 6])
    pmv = sb("pmv", [P, TG, 2])
    xb = sb("xb", [P, TG, D])
    outb = sb("outb", [P, 2, TG, D])

    loaded = nc.alloc_semaphore("moe_weights_loaded")
    LOADS = 5 * 16
    const_step = sig("constants", 1)
    prep = sig("weights_prepared", 1)
    prep_pe = sig("b1_turned", 1)
    ln_stats = sig("ln_stats_ready", 2 * TG)
    coef_step = sig("ln_coefficient_steps", 4)
    h_ready = sig("h_ready", TG)
    turned = sig("h_turned")
    thi_ready = sig("t_hi_ready")
    tf_ready = sig("t_ready")
    tlo_ready = sig("t_lo_ready")
    logits = sig("logits_done")
    route_a = sig("route_before_exp", 2)
    exp_ready = sig("exp_ready")
    ROUTE = 13
    route_b = sig("route_steps", ROUTE)
    up_done = sig("up_done", NE * FB)
    hid_ready = sig("hidden_ready", NE * FB)
    down_done = sig("down_done", NE)
    acc_step = sig("mix_steps", NE * TG)
    stats2 = sig("post_stats", 2 * TG)
    post_pool = sig("post_ln", 4)
    xb_ready = sig("xb_ready", TG)
    out_ready = sig("out_ready", TG)
    stored = [nc.alloc_semaphore(f"moe_stored{u}") for u in range(2)]

    def tile(g, i, dyn):
        return xall[:, dyn(g * TG + i, 1), :].rearrange("p o d -> p (o d)")

    def pool_constants(pl):
        n = [0]

        def then(ins):
            ins.then_inc(const_step.sem, 1)
            n[0] += 1
            pl.wait_ge(const_step.sem, const_step.of(0, n[0]))

        for ap, v in ((ident[:], 0.0), (neghalf[:], -0.5), (ones3[:], 0.0), (b2p[:], 0.0)):
            then(PL.memset(ap, v))
        then(PL.affine_select(out=ident[:], in_=ident[:], compare_op=ALU.not_equal, fill=1.0, base=0,
                              pattern=[[-1, P]], channel_multiplier=1))
        for k in range(PARTS):
            then(PL.memset(ones3[32 * k:32 * k + 1, :], 1.0))
        for e in range(NE):
            then(PL.memset(rank[:, :, e:e + 1], float(NE - e)))
        return n[0]

    CONSTS = 4 + 1 + PARTS + NE
    PREP = 9

    def dve_prepare(dve):
        n = [0]

        def then(ins):
            ins.then_inc(prep.sem, 1)
            n[0] += 1
            dve.wait_ge(prep.sem, prep.of(0, n[0]))

        dve.wait_ge(loaded, LOADS)
        dve.wait_ge(const_step.sem, const_step.of(0, CONSTS))
        then(DVE.tensor_copy(w1hi[:], w1f[:]))
        then(DVE.tensor_tensor(w1lo[:], w1f[:], w1hi[:].bitcast(F32), ALU.subtract))
        then(DVE.tensor_copy(b2p[0:1, :], b2row[:]))
        then(DVE.tensor_tensor(b2res[:], b2row[:], b2p[0:1, :], ALU.subtract))
        then(DVE.tensor_copy(b2p[32:33, :], b2res[:]))
        then(DVE.tensor_copy(b2mid[:], b2res[:]))
        then(DVE.tensor_tensor(b2p[64:65, :], b2res[:], b2mid[:], ALU.subtract))
        dve.wait_ge(prep_pe.sem, prep_pe.of(0, 1))
        then(DVE.tensor_copy(b1[:], banks[7][:, 0:NE * FB]))
        then(DVE.memset(acc[:], 0.0))
        assert n[0] == PREP

    def dve_stats(dve, f, dyn):
        if due(f - 1):
            dve.wait_ge(coef_step.sem, coef_step.of(f - 1))
        for i in range(TG):
            DVE.bn_stats(st6[:, i, :], tile(f, i, dyn)).then_inc(ln_stats.sem, 1)
        for i in range(TG):
            dve.wait_ge(ln_stats.sem, ln_stats.of(f, i + 1))
            apart(dve, f)
            DVE.bn_aggr(mv[:, i, :], st6[:, i, :]).then_inc(ln_stats.sem, 1)

    def pool_norm(pl, f):
        pl.wait_ge(ln_stats.sem, ln_stats.of(f))
        if due(f - 1):
            pl.wait_ge(h_ready.sem, h_ready.of(f - 1))
        apart(pl, f)
        PL.tensor_scalar(lnt[:, 0, :], mv[:, :, 1], LN_EPS, None, ALU.add).then_inc(coef_step.sem, 1)
        pl.wait_ge(coef_step.sem, coef_step.of(f, 1))
        apart(pl, f)
        PL.tensor_tensor(lnt[:, 1, :], lnt[:, 0, :], neghalf[:], ALU.pow).then_inc(coef_step.sem, 1)
        pl.wait_ge(coef_step.sem, coef_step.of(f, 2))
        apart(pl, f)
        PL.tensor_scalar(lnt[:, 2, :], mv[:, :, 0], -1.0, None, ALU.mult).then_inc(coef_step.sem, 1)
        pl.wait_ge(coef_step.sem, coef_step.of(f, 3))
        apart(pl, f)
        PL.tensor_tensor(lnt[:, 3, :], lnt[:, 2, :], lnt[:, 1, :], ALU.mult).then_inc(coef_step.sem, 1)

    def dve_h(dve, f, dyn):
        dve.wait_ge(coef_step.sem, coef_step.of(f))
        if due(f - 1):
            dve.wait_ge(turned.sem, turned.of(f - 1))
        for i in range(TG):
            DVE.tensor_scalar(h[:, i, :], tile(f, i, dyn), lnt[:, 1, i:i + 1], lnt[:, 3, i:i + 1],
                              ALU.mult, ALU.add).then_inc(h_ready.sem, 1)

    def pe_turn(pe, f):
        pe.wait_ge(h_ready.sem, h_ready.of(f))
        if due(f - 1):
            pe.wait_ge(tlo_ready.sem, tlo_ready.of(f - 1))
            pe.wait_ge(tf_ready.sem, tf_ready.of(f - 1))
        for i in range(TG):
            mm = PE.transpose(banks[6][:, col(i)], h[:, i, :], ident[:])
        mm.then_inc(turned.sem, 1)

    def act_turned(act, f, par):
        act.wait_ge(turned.sem, turned.of(f))
        if due(f - 2):
            act.wait_ge(up_done.sem, up_done.of(f - 2))
        SE.activation(thi[:, par, :], banks[6][:], ACT.Copy).then_inc(thi_ready.sem, 1)
        if due(f - 1):
            act.wait_ge(logits.sem, logits.of(f - 1))
        SE.activation(tf[:], banks[6][:], ACT.Copy).then_inc(tf_ready.sem, 1)

    def dve_turned(dve, f, par):
        dve.wait_ge(thi_ready.sem, thi_ready.of(f))
        dve.wait_ge(tf_ready.sem, tf_ready.of(f))
        if due(f - 2):
            dve.wait_ge(up_done.sem, up_done.of(f - 2))
        DVE.tensor_tensor(tlo[:, par, :], banks[6][:], thi[:, par, :].bitcast(F32),
                          ALU.subtract).then_inc(tlo_ready.sem, 1)

    def pe_logits(pe, f):
        pe.wait_ge(tf_ready.sem, tf_ready.of(f))
        if due(f - 1):
            pe.wait_ge(route_a.sem, route_a.of(f - 1))
        for i in range(TG):
            mm = PE.matmul(banks[7][:, i * NE:(i + 1) * NE], tf[:, col(i)], wg[:], start=True, stop=True,
                           skip_group_check=True)
        mm.then_inc(logits.sem, 1)

    def wide(v):
        return v.rearrange("p (t o) -> p t o", o=1).to_broadcast([P, TG, NE])

    def dve_route_a(dve, f):
        lg = banks[7][:, 0:TG * NE].rearrange("p (t e) -> p t e", e=NE)
        dve.wait_ge(logits.sem, logits.of(f))
        if due(f - 1):
            dve.wait_ge(route_b.sem, route_b.of(f - 1))
        DVE.tensor_reduce(rmax[:, 0, :], lg, AX, ALU.max).then_inc(route_a.sem, 1)
        dve.wait_ge(route_a.sem, route_a.of(f, 1))
        if due(f - 1):
            dve.wait_ge(exp_ready.sem, exp_ready.of(f - 1))
        DVE.tensor_tensor(route[:, 0], lg, wide(rmax[:, 0, :]), ALU.subtract).then_inc(route_a.sem, 1)

    def act_exp(act, f):
        act.wait_ge(route_a.sem, route_a.of(f))
        if due(f - 1):
            act.wait_ge(route_b.sem, route_b.of(f - 1))
        SE.activation(route[:, 1], route[:, 0], ACT.Exp).then_inc(exp_ready.sem, 1)

    def dve_route_b(dve, f, par):
        d, e, r = route[:, 0], route[:, 1], lambda k: route[:, 2 + k]
        dve.wait_ge(route_a.sem, route_a.of(f))
        DVE.scalar_tensor_tensor(out=r(0), in0=d, scalar=0.0, in1=rank[:], op0=ALU.is_equal,
                                 op1=ALU.mult).then_inc(route_b.sem, 1)
        dve.wait_ge(route_b.sem, route_b.of(f, 1))
        DVE.tensor_reduce(rmax[:, 1, :], r(0), AX, ALU.max).then_inc(route_b.sem, 1)
        dve.wait_ge(route_b.sem, route_b.of(f, 2))
        DVE.tensor_tensor(r(1), rank[:], wide(rmax[:, 1, :]), ALU.is_equal).then_inc(route_b.sem, 1)
        dve.wait_ge(route_b.sem, route_b.of(f, 3))
        DVE.scalar_tensor_tensor(out=r(2), in0=r(1), scalar=-1e30, in1=d, op0=ALU.mult,
                                 op1=ALU.add).then_inc(route_b.sem, 1)
        dve.wait_ge(route_b.sem, route_b.of(f, 4))
        DVE.tensor_reduce(rmax[:, 2, :], r(2), AX, ALU.max).then_inc(route_b.sem, 1)
        dve.wait_ge(route_b.sem, route_b.of(f, 5))
        DVE.tensor_tensor(r(3), r(2), wide(rmax[:, 2, :]), ALU.is_equal).then_inc(route_b.sem, 1)
        dve.wait_ge(route_b.sem, route_b.of(f, 6))
        DVE.tensor_tensor(r(4), r(3), rank[:], ALU.mult).then_inc(route_b.sem, 1)
        dve.wait_ge(route_b.sem, route_b.of(f, 7))
        DVE.tensor_reduce(rmax[:, 3, :], r(4), AX, ALU.max).then_inc(route_b.sem, 1)
        dve.wait_ge(route_b.sem, route_b.of(f, 8))
        DVE.tensor_tensor(r(5), rank[:], wide(rmax[:, 3, :]), ALU.is_equal).then_inc(route_b.sem, 1)
        dve.wait_ge(route_b.sem, route_b.of(f, 9))
        DVE.tensor_tensor(r(6), r(1), r(5), ALU.add).then_inc(route_b.sem, 1)
        dve.wait_ge(route_b.sem, route_b.of(f, 10))
        dve.wait_ge(exp_ready.sem, exp_ready.of(f))
        DVE.tensor_tensor(r(7), r(6), e, ALU.mult).then_inc(route_b.sem, 1)
        dve.wait_ge(route_b.sem, route_b.of(f, 11))
        DVE.tensor_reduce(rmax[:, 4, :], r(7), AX, ALU.add).then_inc(route_b.sem, 1)
        dve.wait_ge(route_b.sem, route_b.of(f, 12))
        DVE.reciprocal(rmax[:, 5, :], rmax[:, 4, :]).then_inc(route_b.sem, 1)
        dve.wait_ge(route_b.sem, route_b.of(f))
        if due(f - 2):
            dve.wait_ge(acc_step.sem, acc_step.of(f - 2))
        DVE.tensor_tensor(scores[:, par], r(7), wide(rmax[:, 5, :]), ALU.mult).then_inc(score_ready.sem, 1)

    score_ready = sig("scores_ready")

    def pe_up(pe, g, par, e):
        if e == 0:
            pe.wait_ge(thi_ready.sem, thi_ready.of(g))
            pe.wait_ge(tlo_ready.sem, tlo_ready.of(g))
        for n in range(FB):
            k = e * FB + n
            bank = banks[k % 4]
            if k >= 4:
                pe.wait_ge(hid_ready.sem, hid_ready.of(g, k - 3))
            else:
                if due(g - 1):
                    pe.wait_ge(hid_ready.sem, hid_ready.of(g - 1, NE * FB + k - 3))
            w = slice(n * P, (n + 1) * P)
            PE.matmul(bank[:], w1hi[:, e, w], thi[:, par, :], start=True, stop=False)
            PE.matmul(bank[:], w1hi[:, e, w], tlo[:, par, :], start=False, stop=False)
            PE.matmul(bank[:], w1lo[:, e, w], thi[:, par, :], start=False, stop=True).then_inc(up_done.sem, 1)

    def act_hidden(act, g, e):
        for n in range(FB):
            k = e * FB + n
            act.wait_ge(up_done.sem, up_done.of(g, k + 1))
            if e > 1 or due(g - 1):
                act.wait_ge(down_done.sem, down_done.of(g, e - 1))
            SE.activation(hid[:, e % 2, n, :], banks[k % 4][:], ACT.Relu, bias=b1[:, k:k + 1]
                          ).then_inc(hid_ready.sem, 1)

    def pe_down(pe, g, e):
        bank = banks[4 + e % 2]
        if e > 1 or due(g - 1):
            pe.wait_ge(acc_step.sem, acc_step.of(g, (e - 1) * TG))
        PE.matmul(bank[:], ones3[:], b2p[:, e * D:(e + 1) * D].rearrange("p (o d) -> p o d", o=1).to_broadcast([P, TG, D]),
                  start=True, stop=False, skip_group_check=True)
        pe.wait_ge(hid_ready.sem, hid_ready.of(g, (e + 1) * FB))
        for i in range(TG):
            for n in range(FB):
                mm = PE.matmul(bank[:, col(i)], hid[:, e % 2, n, col(i)], w2[:, e, n, :], start=False,
                               stop=i == TG - 1 and n == FB - 1, skip_group_check=True)
        mm.then_inc(down_done.sem, 1)

    def dve_mix(dve, g, par, e):
        dve.wait_ge(down_done.sem, down_done.of(g, e + 1))
        if e == 0:
            dve.wait_ge(score_ready.sem, score_ready.of(g))
            if due(g - 2):
                dve.wait_ge(stats2.sem, stats2.of(g - 2))
                dve.wait_ge(out_ready.sem, out_ready.of(g - 2))
        for i in range(TG):
            y, s = banks[4 + e % 2][:, col(i)], scores[:, par, i, e:e + 1]
            if e == 0:
                ins = DVE.tensor_scalar(acc[:, par, i, :], y, s, None, ALU.mult)
            else:
                dve.wait_ge(acc_step.sem, acc_step.of(g, (e - 1) * TG + i + 1))
                ins = DVE.scalar_tensor_tensor(out=acc[:, par, i, :], in0=y, scalar=s, in1=acc[:, par, i, :],
                                               op0=ALU.mult, op1=ALU.add)
            ins.then_inc(acc_step.sem, 1)

    def dve_post1(dve, g, par):
        if due(g - 1):
            dve.wait_ge(post_pool.sem, post_pool.of(g - 1))
        for i in range(TG):
            dve.wait_ge(acc_step.sem, acc_step.of(g, (NE - 1) * TG + i + 1))
            DVE.bn_stats(pst6[:, i, :], acc[:, par, i, :]).then_inc(stats2.sem, 1)
        for i in range(TG):
            dve.wait_ge(stats2.sem, stats2.of(g, i + 1))
            apart(dve, g)
            DVE.bn_aggr(pmv[:, i, :], pst6[:, i, :]).then_inc(stats2.sem, 1)

    def pool_post(pl, g):
        pl.wait_ge(stats2.sem, stats2.of(g))
        if due(g - 1):
            pl.wait_ge(out_ready.sem, out_ready.of(g - 1))
        apart(pl, g)
        PL.tensor_scalar(post[:, 0, :], pmv[:, :, 1], LN_EPS, None, ALU.add).then_inc(post_pool.sem, 1)
        pl.wait_ge(post_pool.sem, post_pool.of(g, 1))
        apart(pl, g)
        PL.tensor_tensor(post[:, 1, :], post[:, 0, :], neghalf[:], ALU.pow).then_inc(post_pool.sem, 1)
        pl.wait_ge(post_pool.sem, post_pool.of(g, 2))
        apart(pl, g)
        PL.tensor_scalar(post[:, 2, :], pmv[:, :, 0], -1.0, None, ALU.mult).then_inc(post_pool.sem, 1)
        pl.wait_ge(post_pool.sem, post_pool.of(g, 3))
        apart(pl, g)
        PL.tensor_tensor(post[:, 3, :], post[:, 2, :], post[:, 1, :], ALU.mult).then_inc(post_pool.sem, 1)

    def dve_post2(dve, g, par, b, dyn):
        dve.wait_ge(post_pool.sem, post_pool.of(g))
        for i in range(TG):
            DVE.tensor_scalar(xb[:, i, :], tile(g, i, dyn), post[:, 3, i:i + 1], None,
                              ALU.add).then_inc(xb_ready.sem, 1)
        if not (isinstance(b, int) and b == 0):
            dve.wait_ge(stored[par], 1 + b * 16)
        for i in range(TG):
            dve.wait_ge(xb_ready.sem, xb_ready.of(g, i + 1))
            DVE.scalar_tensor_tensor(out=outb[:, par, i, :], in0=acc[:, par, i, :], scalar=post[:, 1, i:i + 1],
                                     in1=xb[:, i, :], op0=ALU.mult, op1=ALU.add).then_inc(out_ready.sem, 1)

    ov = out.rearrange("b (n p) d -> p (b n) d", p=P)

    def pe_body(pe, b, u, dyn, first, last):
        g, par = 2 * b + u, u
        for e in range(NE):
            pe_up(pe, g, par, e)
            if e:
                pe_down(pe, g, e - 1)
            elif not first:
                pe_down(pe, g - 1, NE - 1)
            if e == 2 and not last:
                pe_turn(pe, g + 1)
            if e == 4 and not last:
                pe_logits(pe, g + 1)

    def act_body(act, b, u, dyn, first, last):
        g, par = 2 * b + u, u
        for e in range(NE):
            act_hidden(act, g, e)
            if e == 2 and not last:
                act_turned(act, g + 1, 1 - par)
            if e == 5 and not last:
                act_exp(act, g + 1)

    def dve_body(dve, b, u, dyn, first, last):
        g, par = 2 * b + u, u
        if not last:
            dve_stats(dve, g + 1, dyn)
        for e in range(NE):
            if e:
                dve_mix(dve, g, par, e - 1)
            elif not first:
                dve_mix(dve, g - 1, 1 - par, NE - 1)
                dve_post1(dve, g - 1, 1 - par)
            if e == 1 and not last:
                dve_h(dve, g + 1, dyn)
            if e == 2 and not first:
                dve_post2(dve, g - 1, 1 - par, b if u else b - 1, dyn)
            if e == 3 and not last:
                dve_turned(dve, g + 1, 1 - par)
            if e == 5 and not last:
                dve_route_a(dve, g + 1)
            if e == 6 and not last:
                dve_route_b(dve, g + 1, 1 - par)

    def pool_body(pl, b, u, dyn, first, last):
        g = 2 * b + u
        if not last:
            pool_norm(pl, g + 1)
        if not first:
            pool_post(pl, g - 1)

    def over_groups(eng, body):
        for u in range(2):
            body(eng, 0, u, static, u == 0, False)
        with eng.Fori(1, GROUPS // 2 - 1) as b:
            for u in range(2):
                body(eng, b, u, dynamic, False, False)
        for u in range(2):
            body(eng, GROUPS // 2 - 1, u, static, False, u == 1)

    LAST = GROUPS - 1
    with nc.Block() as block:
        @block.sync
        def _(sp):
            sp.dma_start(w1f[:], w1_d.rearrange("e d h -> d e h")).then_inc(loaded, 16)
            sp.dma_start(wg[:], wg_d).then_inc(loaded, 16)
            sp.dma_start(b1row[:], b1_d.rearrange("e (n p) -> (e n) p", p=P)).then_inc(loaded, 16)
            sp.dma_start(b2row[:], b2_d.rearrange("(o e) d -> o (e d)", o=1)).then_inc(loaded, 16)
            sp.dma_start(w2[:], w2_d.rearrange("e (n p) d -> p e n d", p=P)).then_inc(loaded, 16)
            for u in range(2):
                sp.nop(nofuse=True).then_inc(stored[u], 1)
            with sp.Fori(0, GROUPS // 2) as b:
                for u in range(2):
                    g = 2 * b + u
                    sp.wait_ge(out_ready.sem, out_ready.of(g))
                    sp.dma_start(ov[:, bass.ds(g * TG, TG), :], outb[:, u, :, :]).then_inc(stored[u], 16)
            for u in range(2):
                sp.wait_ge(stored[u], 1 + 16 * GROUPS // 2)

        @block.tensor
        def _(pe):
            pe.wait_ge(loaded, LOADS)
            pe.wait_ge(const_step.sem, const_step.of(0, CONSTS))
            PE.transpose(banks[7][:, 0:NE * FB], b1row[:], ident[0:NE * FB, 0:NE * FB]).then_inc(prep_pe.sem, 1)
            pe.wait_ge(prep.sem, prep.of(0, PREP))
            pe_turn(pe, 0)
            pe_logits(pe, 0)
            over_groups(pe, pe_body)
            pe_down(pe, LAST, NE - 1)

        @block.scalar
        def _(act):
            act.wait_ge(prep.sem, prep.of(0, PREP))
            act_turned(act, 0, 0)
            act_exp(act, 0)
            over_groups(act, act_body)

        @block.vector
        def _(dve):
            dve_prepare(dve)
            dve_stats(dve, 0, static)
            dve_h(dve, 0, static)
            dve_turned(dve, 0, 0)
            dve_route_a(dve, 0)
            dve_route_b(dve, 0, 0)
            over_groups(dve, dve_body)
            dve_mix(dve, LAST, 1, NE - 1)
            dve_post1(dve, LAST, 1)
            dve_post2(dve, LAST, 1, GROUPS // 2 - 1, static)

        @block.gpsimd
        def _(pl):
            assert pool_constants(pl) == CONSTS
            pool_norm(pl, 0)
            over_groups(pl, pool_body)
            pool_post(pl, LAST)


_INS = ["L0_attn_hidden", "L0_attn_w_norm_in", "L0_attn_w_in_proj", "L0_attn_conv_w", "L0_attn_conv_b",
        "L0_attn_w_dt", "L0_attn_b_dt", "L0_attn_A_log", "L0_attn_D", "L0_attn_w_norm_out", "L0_attn_w_out_proj",
        "L0_ffn_Wg", "L0_ffn_W1", "L0_ffn_b1", "L0_ffn_W2", "L0_ffn_b2"]
_OUTS = [((BATCH, SEQ, D), "float32")]


def kernel(**inputs):
    import numpy as _np
    import concourse.bacc as _bacc
    from concourse import mybir as _mybir
    from concourse.bass_utils import run_bass_kernel_spmd as _run

    nc = _bacc.Bacc("TRN2", target_bir_lowering=False, num_devices=1)
    arrays, args = {}, []
    for name in _INS:
        a = _np.ascontiguousarray(inputs[name])
        arrays[f"in_{name}_dram"] = a
        args.append(nc.dram_tensor(f"in_{name}_dram", a.shape, _mybir.dt.from_np(a.dtype), kind="ExternalInput").ap())
    for i, (shape, dtype) in enumerate(_OUTS):
        dt = _mybir.dt.from_np(_np.dtype(dtype))
        args.append(nc.dram_tensor(f"out_{i}_dram", shape, dt, kind="ExternalOutput").ap())
    build(nc, *args)
    r = _run(nc, [arrays], core_ids=[0])
    return r.results[0]["out_0_dram"]
```

```python
from contextlib import ExitStack

import numpy as np
import concourse.bass as bass
from concourse import mybir

ALU = mybir.AluOpType
ACT = mybir.ActivationFunctionType
F32 = mybir.dt.float32
F32R = mybir.dt.float32r
BF16 = mybir.dt.bfloat16
AX = mybir.AxisListType.X

P = 128
BATCH, SEQ, D = 8, 1024, 128
TOK = BATCH * SEQ
TILES = TOK // P
TG = 4
GT = TG * P
GROUPS = TOK // GT
GB = SEQ // GT
DI, NH, HD, NS, KC = 256, 8, 32, 64, 4
NP = NH // 2
HH = NH // 2
SLOTS = 4
NB = DI // P
O_X, O_B, O_C, O_DT = DI, 2 * DI, 2 * DI + NH * NS, 2 * DI + 2 * NH * NS
PROJ = O_DT + NH
WCOLS = O_DT + DI
LN_EPS = 1e-5
RMS_EPS = float(np.finfo(np.float32).eps)
NE, FH = 8, 256
FB = FH // P
PARTS = 3


class Signal:

    def __init__(self, nc, name, per):
        self.sem, self.per = nc.alloc_semaphore(name), per

    def of(self, idx, k=None):
        return idx * self.per + (self.per if k is None else k)


def due(idx):
    return not isinstance(idx, int) or idx >= 0


def apart(eng, idx):
    if not isinstance(idx, int):
        eng.nop(nofuse=True)


def build(nc, hidden, w_norm_in, w_in, conv_w, conv_b, w_dt, b_dt, a_log, d_skip, w_norm_out, w_out,
          wg, w1, b1, w2, b2, out):
    xall = nc.alloc_sbuf_tensor("xall", [P, TILES, D], F32)
    banks = [nc.alloc_psum_tensor(f"bank{i}", [P, 512], F32) for i in range(8)]
    with ExitStack() as attention_buffers:
        attention(nc, attention_buffers, xall, banks, hidden, w_norm_in, w_in, conv_w, conv_b, w_dt, b_dt, a_log,
                  d_skip, w_norm_out, w_out)
    with ExitStack() as expert_buffers:
        experts(nc, expert_buffers, xall, banks, wg, w1, b1, w2, b2, out)


def static(a, n):
    return slice(a, a + n)


def dynamic(a, n):
    return bass.ds(a, n)


def col(i, w=P):
    return slice(i * w, (i + 1) * w)


def attention(nc, buffers, xall, banks, hidden, w_norm_in, w_in, conv_w, conv_b, w_dt, b_dt, a_log,
              d_skip, w_norm_out, w_out):
    def sb(name, shape, dt=F32):
        return buffers.enter_context(nc.sbuf_tensor(name, shape, dt))

    def sig(name, per=1):
        return Signal(nc, name, per)

    PE, DVE, SE, PL = nc.tensor, nc.vector, nc.scalar, nc.gpsimd

    s1 = sb("ln1_scale", [P, TILES])
    nb1 = sb("ln1_shift", [P, TILES])

    ident = sb("ident", [P, P])
    ones = sb("ones", [P, P])
    zeros = sb("zeros", [P, 1])
    neghalf = sb("neghalf", [P, TG])
    sel_a = sb("sel_a", [P, NH, P], BF16)
    negsel = sb("negsel", [P, NH, P], BF16)
    sel_e = sb("sel_e", [P, NB, P], BF16)
    hsum = sb("hsum", [P, NB, NH])

    m_flat = sb("m", [P, 2 * NH * P])
    mg_flat = sb("mg", [P, 2 * NH * P])
    wraw, wf = m_flat[:, 0:PROJ], mg_flat[:, 0:WCOLS]
    whi = sb("whi", [P, WCOLS], F32R)
    wlo = sb("wlo", [P, WCOLS], F32R)
    wdt_rows = sb("wdt_rows", [NH, DI])
    wdt_in_t = sb("wdt_in_t", [NH, P])
    wn_in = sb("wn_in", [P, 1])
    cw = sb("cw", [P, NB, KC])
    cb = sb("cb", [P, NB])
    bdt = sb("bdt", [P, NB])
    alog = sb("alog", [NH, 1])
    ascale = sb("ascale", [NH, 1])
    dcol = sb("dcol", [P, NB])
    wn_out = sb("wn_out", [P, NB])
    wo_raw = sb("wo_raw", [P, NB, D])
    wo = sb("wo", [P, NB, D])

    h = sb("h", [P, 2, TG, D])
    st6 = sb("st6", [P, TG, 6])
    mv = sb("mv", [P, TG, 2])
    lnt = sb("lnt", [P, 6, TG])
    thi = sb("thi", [P, GT], F32R)
    tlo = sb("tlo", [P, GT], F32R)
    dtv = sb("dtv", [P, NB, GT])
    dta = sb("dta", [P, NB, GT])
    cs = sb("cs", [NH, GT])
    resid1 = sb("resid1", [NH, GT])
    mid = sb("mid", [NH, GT], BF16)
    parts = sb("parts", [P, 2, GT], BF16)
    xraw = sb("xraw", [P, 2, NB, KC - 1 + GT])
    xth = sb("xth", [P, NB, GT])
    xt = sb("xt", [P, 2, NB, GT])
    bt = sb("bt", [P, 2, NP, GT])
    ct = sb("ct", [P, 2, NP, TG, 2, P])
    zth = sb("zth", [P, GT])
    zt = sb("zt", [P, 2, NB, GT])

    edec = sb("edec", [P, 2, NB, P])
    tdec = sb("tdec", [P, 2, NP])
    m = m_flat[:].rearrange("p (b h l) -> p b h l", b=2, h=NH)
    mg = mg_flat[:].rearrange("p (b h l) -> p b h l", b=2, h=NH)
    btok = sb("btok", [P, 2, NP * P])
    xtok = sb("xtok", [P, 2, DI])
    xw = sb("xw", [P, 2, DI])
    state = sb("state", [P, 2, NP, HD])
    decayed = sb("decayed", [P, NP, HD])
    y1 = sb("y1", [P, NB, P])
    y2 = sb("y2", [P, NB, P])
    y3 = sb("y3", [P, NB, P])
    y4 = sb("y4", [P, 2, NB, P])
    ysq = sb("ysq", [P, 2, NB, P])
    og = sb("og", [P, 2, TG, D + 2])
    pt = sb("pt", [P, 6, TG])
    xn = sb("xn", [P, TG, D])
    ob = sb("ob", [P, TG, D])
    pst6 = sb("pst6", [P, TG, 6])
    pmv = sb("pmv", [P, TG, 2])
    xb = sb("xb", [P, TG, D])

    loaded0 = nc.alloc_semaphore("x_first_groups_loaded")
    loaded1 = nc.alloc_semaphore("x_other_groups_loaded")
    w_loaded = nc.alloc_semaphore("weights_loaded")
    const_step = sig("pool_constants_built", 1)
    prep = sig("dve_weights_prepared", 1)
    prep_pe = sig("pe_dt_weights_made", 1)
    prep_act = sig("act_decay_rates_made", 1)

    ln_stats = sig("ln_stats_ready", 2 * TG)
    coef_step = sig("ln1_coefficient_steps", 10)
    h_ready = sig("h_ready", TG)
    fr_done = sig("front_products_done", 16)
    thi_ready = sig("thi_ready")
    tlo_ready = sig("tlo_ready")
    dtv_ready = sig("dtv_ready", NB)
    dta_ready = sig("softplus_tail_ready", 4)
    dtr_ready = sig("softplus_ready")
    scan_ready = sig("log_decay_scanned", TG)
    part_ready = sig("log_decay_parts_ready", 5)
    xraw_ready = sig("xraw_ready", NB)
    hist_ready = sig("conv_history_ready")
    conv_step = sig("conv_steps", NB * KC)
    xth_ready = sig("xth_ready", NB)
    xt_ready = sig("xt_ready", NB)
    bt_ready = sig("bt_ready", NP)
    cta_ready = sig("c_by_act_ready", 6)
    ctd_ready = sig("c_by_dve_ready", 2)
    zth_ready = sig("zth_ready", NB)
    zt_ready = sig("zt_ready", NB)

    btr_done = sig("b_turned")
    xtr_done = sig("x_turned")
    dd_done = sig("log_decays_done", 2)
    gg_done = sig("scores_done", 2)
    ee_done = sig("decay_rows_done")
    oo_done = sig("out_projected")
    yy_done = sig("y_products_done")
    ss_done = sig("state_products_done")
    e_ready = sig("decay_rows_ready", 3)
    m_ready = sig("decays_ready", 2)
    btok_ready = sig("btok_ready")
    xtok_ready = sig("xtok_ready")
    ysq_ready = sig("ysq_ready")
    og_ready = sig("og_ready")
    mm_ready = sig("decays_masked", 2)
    xw_ready = sig("xw_ready", 2)
    dec_ready = sig("state_decayed")
    y4_ready = sig("y_gated")
    mg_ready = sig("scores_decayed", 2)
    state_ready = sig("state_ready", 2)
    y_step = sig("y_steps", 4)
    post_pool1 = sig("post_rms", 2)
    xn_ready = sig("xn_ready", TG)
    post_dve1 = sig("post_stats", 3 * TG)
    post_pool2 = sig("post_ln2", 4)
    xb_ready = sig("xb_ready", TG)
    x2_ready = sig("x2_ready", TG)

    def fr_uses(f, g):
        products = [("h", tlo_ready, 1), ("dt0", dtv_ready, 1), ("dt1", dtv_ready, 2), ("x0", xraw_ready, 1),
                    ("x1", xraw_ready, 2), ("b0", bt_ready, 1), ("b1", bt_ready, 2), ("b2", bt_ready, 3),
                    ("b3", bt_ready, 4), ("c0", cta_ready, 2), ("c1", cta_ready, 4), ("a", scan_ready, TG),
                    ("c2", cta_ready, 6), ("c3", ctd_ready, 2), ("z0", zt_ready, 1), ("z1", zt_ready, 2)]
        seq = []
        for n, (key, s, k) in enumerate(products):
            if g is not None and n % SLOTS == SLOTS // 2:
                seq.append((("xtr", n // SLOTS), xtok_ready, g * TG + n // SLOTS, 1))
            seq.append(((key,), s, f, k) if f is not None else None)
        return seq

    FRONT = [["h", "dt0", "dt1", "x0"], ["x1", "b0", "b1", "b2"], ["b3", "c0", "c1", "a"], ["c2", "c3", "z0", "z1"]]
    BLOCK = {"dt0": O_DT, "dt1": O_DT + P, "x0": O_X, "x1": O_X + P, "z0": 0, "z1": P}
    BLOCK.update({f"b{j}": O_B + j * P for j in range(NP)})
    BLOCK.update({f"c{j}": O_C + j * P for j in range(NP)})
    FR_INDEX = {k: n for n, k in enumerate(sum(FRONT, []))}

    class Front:

        def __init__(self, g, f, before):
            self.seq, self.before = fr_uses(f, g), before
            self.at = {u[0]: n for n, u in enumerate(self.seq) if u}

        def bank(self, *key):
            return banks[self.at[key] % 2]

        def free(self, eng, *key):
            both = self.before + self.seq
            n = len(self.before) + self.at[key] - 2
            while n >= 0 and both[n] is None:
                n -= 2
            if n >= 0:
                _, s, idx, k = both[n]
                eng.wait_ge(s.sem, s.of(idx, k))

    def load_all(sp):
        small = dict(allow_slow_non_contiguous=True)
        v = hidden.rearrange("b (n p) d -> p (b n) d", p=P)
        first = 2 * TG
        sp.dma_start(xall[:, 0:TG, :], v[:, 0:TG, :]).then_inc(loaded0, 16)
        sp.dma_start(wraw, w_in).then_inc(w_loaded, 16)
        sp.dma_start(xall[:, TG:first, :], v[:, TG:first, :]).then_inc(loaded0, 16)
        cvec = lambda a: a.rearrange("(n p) -> p n", p=P)
        sp.dma_start(wn_in[:], cvec(w_norm_in), **small).then_inc(w_loaded, 16)
        sp.dma_start(cw[:], conv_w.rearrange("(n p) o k -> p n (o k)", p=P)).then_inc(w_loaded, 16)
        sp.dma_start(cb[:], cvec(conv_b), **small).then_inc(w_loaded, 16)
        sp.dma_start(bdt[:], cvec(b_dt), **small).then_inc(w_loaded, 16)
        sp.dma_start(wdt_rows[:], w_dt).then_inc(w_loaded, 16)
        sp.dma_start(alog[:], a_log.rearrange("(h o) -> h o", o=1), **small).then_inc(w_loaded, 16)
        for n in range(NB):
            for q in range(P // HD):
                hh = n * (P // HD) + q
                sp.dma_start(dcol[q * HD:(q + 1) * HD, n:n + 1],
                             d_skip[hh:hh + 1].rearrange("(h o) -> h o", o=1).to_broadcast([HD, 1]), **small
                             ).then_inc(w_loaded, 16)
        sp.dma_start(wn_out[:], cvec(w_norm_out), **small).then_inc(w_loaded, 16)
        sp.dma_start(wo_raw[:], w_out.rearrange("(n p) d -> p n d", p=P)).then_inc(w_loaded, 16)
        sp.dma_start(xall[:, first:TILES, :], v[:, first:TILES, :]).then_inc(loaded1, 16)

    W_LOADS = 17 * 16

    def pool_constants(pl):
        step = [0]

        def then(ins):
            ins.then_inc(const_step.sem, 1)
            step[0] += 1
            pl.wait_ge(const_step.sem, const_step.of(0, step[0]))

        for ap, v in ((ident[:], 0.0), (ones[:], 1.0), (neghalf[:], -0.5), (zeros[:], 0.0), (sel_a[:], 0.0),
                      (negsel[:], 0.0), (sel_e[:], 0.0), (hsum[:], 0.0), (parts[:], 0.0), (ct[:], 0.0),
                      (state[:], 0.0)):
            then(PL.memset(ap, v))
        then(PL.affine_select(out=ident[:], in_=ident[:], compare_op=ALU.not_equal, fill=1.0, base=0,
                              pattern=[[-1, P]], channel_multiplier=1))
        for k in range(PARTS):
            then(PL.affine_select(out=sel_a[:], in_=sel_a[:], compare_op=ALU.not_equal, fill=1.0, base=-32 * k,
                                  pattern=[[-1, NH], [0, P]], channel_multiplier=1))
            then(PL.affine_select(out=negsel[:], in_=negsel[:], compare_op=ALU.not_equal, fill=-1.0, base=-32 * k,
                                  pattern=[[-1, NH], [0, P]], channel_multiplier=1))
            for n in range(NB):
                v = sel_e[:, n, :].rearrange("p (q d) -> p q d", d=HD)
                then(PL.affine_select(out=v, in_=v, compare_op=ALU.not_equal, fill=1.0, base=-32 * k - 4 * n,
                                      pattern=[[-1, P // HD], [0, HD]], channel_multiplier=1))
        for n in range(NB):
            for q in range(P // HD):
                then(PL.memset(hsum[q * HD:(q + 1) * HD, n, n * 4 + q:n * 4 + q + 1], 1.0))
        return step[0]

    CONSTS = 11 + 1 + PARTS * (2 + NB) + NB * 4
    PREP = 14

    def dve_prepare(dve):
        step = [0]

        def then(ins):
            ins.then_inc(prep.sem, 1)
            step[0] += 1
            dve.wait_ge(prep.sem, prep.of(0, step[0]))

        dve.wait_ge(w_loaded, W_LOADS)
        then(DVE.tensor_scalar(wf[:, O_X:O_DT], wraw[:, O_X:O_DT], wn_in[:, 0:1], None, ALU.mult))
        then(DVE.tensor_scalar(wf[:, 0:O_X], wraw[:, 0:O_X], wn_in[:, 0:1], 0.5, ALU.mult, ALU.mult))
        then(DVE.tensor_scalar(cw[:], cw[:], 0.5, None, ALU.mult))
        then(DVE.tensor_scalar(cb[:], cb[:], 0.5, None, ALU.mult))
        for n in range(NB):
            then(DVE.tensor_scalar(wo[:, n, :], wo_raw[:, n, :], wn_out[:, n:n + 1], None, ALU.mult))
        then(DVE.tensor_copy(whi[:, 0:O_DT], wf[:, 0:O_DT]))
        then(DVE.tensor_tensor(wlo[:, 0:O_DT], wf[:, 0:O_DT], whi[:, 0:O_DT].bitcast(F32), ALU.subtract))
        dve.wait_ge(prep_pe.sem, prep_pe.of(0, 1))
        then(DVE.tensor_copy(wdt_in_t[:], banks[7][0:NH, 0:P]))
        dve.wait_ge(prep_pe.sem, prep_pe.of(0, 2))
        then(DVE.tensor_scalar(wf[:, O_DT:WCOLS], banks[6][:, 0:DI], wn_in[:, 0:1], None, ALU.mult))
        then(DVE.tensor_copy(whi[:, O_DT:WCOLS], wf[:, O_DT:WCOLS]))
        then(DVE.tensor_tensor(wlo[:, O_DT:WCOLS], wf[:, O_DT:WCOLS], whi[:, O_DT:WCOLS].bitcast(F32),
                               ALU.subtract))
        dve.wait_ge(prep_act.sem, prep_act.of(0, 1))
        then(DVE.tensor_scalar(ascale[:], alog[:], -1.0 / HD, None, ALU.mult))
        then(DVE.memset(og[:], 0.0))
        assert step[0] == PREP

    def pe_prepare(pe):
        pe.wait_ge(const_step.sem, const_step.of(0, CONSTS))
        pe.wait_ge(w_loaded, W_LOADS)
        PE.transpose(banks[7][0:NH, 0:P], wraw[:, O_DT:PROJ], ident[:]).then_inc(prep_pe.sem, 1)
        pe.wait_ge(prep.sem, prep.of(0, 9))
        PE.matmul(banks[6][:, 0:DI], wdt_in_t[:], wdt_rows[:], start=True, stop=True).then_inc(prep_pe.sem, 1)

    def act_prepare(act):
        act.wait_ge(w_loaded, W_LOADS)
        SE.activation(alog[:], alog[:], ACT.Exp).then_inc(prep_act.sem, 1)

    def dve_stats(dve, f, dyn):
        xg = lambda i: xall[:, dyn(f * TG + i, 1), :].rearrange("p o d -> p (o d)")
        if due(f - 1):
            dve.wait_ge(coef_step.sem, coef_step.of(f - 1))
        for i in range(TG):
            DVE.bn_stats(st6[:, i, :], xg(i)).then_inc(ln_stats.sem, 1)
        for i in range(TG):
            dve.wait_ge(ln_stats.sem, ln_stats.of(f, i + 1))
            apart(dve, f)
            DVE.bn_aggr(mv[:, i, :], st6[:, i, :]).then_inc(ln_stats.sem, 1)

    def pool_norm(pl, f, dyn):
        mean, var = mv[:, :, 0], mv[:, :, 1]
        rs, ns = s1[:, dyn(f * TG, TG)], nb1[:, dyn(f * TG, TG)]
        pl.wait_ge(ln_stats.sem, ln_stats.of(f))
        if due(f - 1):
            pl.wait_ge(h_ready.sem, h_ready.of(f - 1))
        apart(pl, f)
        PL.tensor_scalar(lnt[:, 0, :], var, LN_EPS, None, ALU.add).then_inc(coef_step.sem, 1)
        pl.wait_ge(coef_step.sem, coef_step.of(f, 1))
        apart(pl, f)
        PL.tensor_tensor(rs, lnt[:, 0, :], neghalf[:], ALU.pow).then_inc(coef_step.sem, 1)
        pl.wait_ge(coef_step.sem, coef_step.of(f, 2))
        apart(pl, f)
        PL.tensor_tensor(lnt[:, 1, :], rs, rs, ALU.mult).then_inc(coef_step.sem, 1)
        pl.wait_ge(coef_step.sem, coef_step.of(f, 3))
        apart(pl, f)
        PL.tensor_tensor(lnt[:, 2, :], lnt[:, 1, :], var, ALU.mult).then_inc(coef_step.sem, 1)
        pl.wait_ge(coef_step.sem, coef_step.of(f, 4))
        apart(pl, f)
        PL.tensor_scalar(lnt[:, 3, :], lnt[:, 2, :], RMS_EPS, None, ALU.add).then_inc(coef_step.sem, 1)
        pl.wait_ge(coef_step.sem, coef_step.of(f, 5))
        apart(pl, f)
        PL.tensor_tensor(lnt[:, 4, :], lnt[:, 3, :], neghalf[:], ALU.pow).then_inc(coef_step.sem, 1)
        pl.wait_ge(coef_step.sem, coef_step.of(f, 6))
        apart(pl, f)
        PL.tensor_tensor(lnt[:, 0, :], lnt[:, 4, :], rs, ALU.mult).then_inc(coef_step.sem, 1)
        pl.wait_ge(coef_step.sem, coef_step.of(f, 7))
        apart(pl, f)
        PL.tensor_scalar(lnt[:, 5, :], mean, -1.0, None, ALU.mult).then_inc(coef_step.sem, 1)
        pl.wait_ge(coef_step.sem, coef_step.of(f, 8))
        apart(pl, f)
        PL.tensor_tensor(ns, lnt[:, 5, :], rs, ALU.mult).then_inc(coef_step.sem, 1)
        pl.wait_ge(coef_step.sem, coef_step.of(f, 9))
        apart(pl, f)
        PL.tensor_tensor(lnt[:, 1, :], lnt[:, 5, :], lnt[:, 0, :], ALU.mult).then_inc(coef_step.sem, 1)

    def act_h(act, f, par, dyn):
        act.wait_ge(coef_step.sem, coef_step.of(f))
        if due(f - 2):
            act.wait_ge(fr_done.sem, fr_done.of(f - 2, 1))
        for i in range(TG):
            x = xall[:, dyn(f * TG + i, 1), :].rearrange("p o d -> p (o d)")
            SE.activation(h[:, par, i, :], x, ACT.Identity, scale=lnt[:, 0, i:i + 1], bias=lnt[:, 1, i:i + 1]
                          ).then_inc(h_ready.sem, 1)

    def pe_front(pe, f, par, fr, i, slot):
        key = FRONT[i][slot]
        bank = fr.bank(key)
        fr.free(pe, key)
        if key == "h":
            pe.wait_ge(h_ready.sem, h_ready.of(f))
            for i in range(TG):
                mm = PE.transpose(bank[:, col(i)], h[:, par, i, :], ident[:])
        elif key == "a":
            pe.wait_ge(dtr_ready.sem, dtr_ready.of(f))
            for n in range(NB):
                mm = PE.matmul(bank[0:NH, :], hsum[:, n, :], dtv[:, n, :], start=n == 0, stop=n == NB - 1)
        else:
            if key == "dt0":
                pe.wait_ge(thi_ready.sem, thi_ready.of(f))
                pe.wait_ge(tlo_ready.sem, tlo_ready.of(f))
                if isinstance(f, int) and f == 0:
                    pe.wait_ge(prep.sem, prep.of(0, PREP))
            w = slice(BLOCK[key], BLOCK[key] + P)
            PE.matmul(bank[:], whi[:, w], thi[:], start=True, stop=False)
            PE.matmul(bank[:], whi[:, w], tlo[:], start=False, stop=False)
            mm = PE.matmul(bank[:], wlo[:, w], thi[:], start=False, stop=True)
        mm.then_inc(fr_done.sem, 1)

    def fdone(f, key):
        return fr_done.of(f, FR_INDEX[key] + 1)

    def act_front(act, f, par, fr, i, slot):
        key = FRONT[i][slot]
        if key == "h":
            act.wait_ge(fr_done.sem, fdone(f, "h"))
            if due(f - 1):
                act.wait_ge(fr_done.sem, fr_done.of(f - 1, 16))
            SE.activation(thi[:], fr.bank("h")[:], ACT.Copy).then_inc(thi_ready.sem, 1)
        if key in ("dt0", "dt1"):
            n = int(key[2])
            act.wait_ge(fr_done.sem, fdone(f, key))
            if n == 0 and due(f - 1):
                act.wait_ge(dtr_ready.sem, dtr_ready.of(f - 1))
            SE.activation(dta[:, n, :], fr.bank(key)[:], ACT.Abs, bias=bdt[:, n:n + 1]).then_inc(dta_ready.sem, 1)
        if key in ("x0", "x1"):
            n = int(key[1])
            act.wait_ge(fr_done.sem, fdone(f, key))
            if n == 0:
                if due(f - 1):
                    act.wait_ge(hist_ready.sem, hist_ready.of(f - 1))
                if due(f - 2):
                    act.wait_ge(conv_step.sem, conv_step.of(f - 2))
            SE.activation(xraw[:, par, n, KC - 1:], fr.bank(key)[:], ACT.Copy).then_inc(xraw_ready.sem, 1)
            act.wait_ge(dta_ready.sem, dta_ready.of(f, 2 + n))
            if n == 0:
                SE.activation(dta[:], dta[:], ACT.Exp, scale=-1.0).then_inc(dta_ready.sem, 1)
            else:
                SE.activation(dta[:], dta[:], ACT.Ln, bias=1.0).then_inc(dta_ready.sem, 1)
        if key == "b3":
            for n in range(NB):
                act.wait_ge(conv_step.sem, conv_step.of(f, (KC - 1) * NB + n + 1))
                if due(f - 1):
                    act.wait_ge(xt_ready.sem, xt_ready.of(f - 1))
                SE.activation(xth[:, n, :], xt[:, par, n, :], ACT.Tanh).then_inc(xth_ready.sem, 1)
        if key in ("b0", "b1", "b2", "b3"):
            j = int(key[1])
            act.wait_ge(fr_done.sem, fdone(f, key))
            if j == 0 and due(f - 2):
                act.wait_ge(btr_done.sem, btr_done.of((f - 2) * TG + TG - 1))
                act.wait_ge(gg_done.sem, gg_done.of((f - 2) * TG + TG - 1))
            SE.activation(bt[:, par, j, :], fr.bank(key)[:], ACT.Copy).then_inc(bt_ready.sem, 1)
        if key in ("c0", "c1", "c2"):
            j = int(key[1])
            act.wait_ge(fr_done.sem, fdone(f, key))
            if j == 0 and due(f - 2):
                act.wait_ge(yy_done.sem, yy_done.of((f - 2) * TG + TG - 1))
            split_c(SE.copy, j, par, fr, cta_ready)
        if key in ("z0", "z1"):
            n = int(key[1])
            act.wait_ge(fr_done.sem, fdone(f, key))
            if n:
                act.wait_ge(zt_ready.sem, zt_ready.of(f, n))
            elif due(f - 1):
                act.wait_ge(zt_ready.sem, zt_ready.of(f - 1))
            SE.activation(zth[:], fr.bank(key)[:], ACT.Tanh).then_inc(zth_ready.sem, 1)

    def split_c(copy, j, par, fr, ready):
        for q in range(2):
            rows = slice(q * NS, (q + 1) * NS)
            copy(ct[rows, par, j, :, q, :], fr.bank(f"c{j}")[rows, :].rearrange("p (t l) -> p t l", l=P)
                 ).then_inc(ready.sem, 1)

    def dve_conv(dve, f, par, taps):
        for k in taps:
            for n in range(NB):
                dve.wait_ge(xraw_ready.sem, xraw_ready.of(f, n + 1))
                src = xraw[:, par, n, k:k + GT]
                if k == 0:
                    DVE.tensor_scalar(xt[:, par, n, :], src, cw[:, n, 0:1], cb[:, n:n + 1], ALU.mult, ALU.add
                                      ).then_inc(conv_step.sem, 1)
                else:
                    dve.wait_ge(conv_step.sem, conv_step.of(f, (k - 1) * NB + n + 1))
                    DVE.scalar_tensor_tensor(out=xt[:, par, n, :], in0=src, scalar=cw[:, n, k:k + 1],
                                             in1=xt[:, par, n, :], op0=ALU.mult, op1=ALU.add
                                             ).then_inc(conv_step.sem, 1)

    def dve_front(dve, f, par, fr, i, slot):
        key = FRONT[i][slot]
        if key == "h":
            dve.wait_ge(thi_ready.sem, thi_ready.of(f))
            if due(f - 1):
                dve.wait_ge(fr_done.sem, fr_done.of(f - 1, 16))
            DVE.tensor_tensor(tlo[:], fr.bank("h")[:], thi[:].bitcast(F32), ALU.subtract).then_inc(tlo_ready.sem, 1)
        if key in ("dt0", "dt1"):
            n = int(key[2])
            dve.wait_ge(dta_ready.sem, dta_ready.of(f, n + 1))
            if n == 0 and due(f - 1):
                dve.wait_ge(fr_done.sem, fdone(f - 1, "a"))
            DVE.tensor_scalar(dtv[:, n, :], fr.bank(key)[:], bdt[:, n:n + 1], 0.0, ALU.add, ALU.max
                              ).then_inc(dtv_ready.sem, 1)
        if key == "x1":
            dve.wait_ge(hist_ready.sem, hist_ready.of(f))
            if due(f - 2):
                dve.wait_ge(y_step.sem, y_step.of((f - 2) * TG + TG - 1))
            dve_conv(dve, f, par, range(0, KC // 2))
        if key == "b1":
            dve_conv(dve, f, par, range(KC // 2, KC))
        if key == "c1":
            for n in range(NB):
                dve.wait_ge(xth_ready.sem, xth_ready.of(f, n + 1))
                DVE.scalar_tensor_tensor(out=xt[:, par, n, :], in0=xth[:, n, :], scalar=1.0, in1=xt[:, par, n, :],
                                         op0=ALU.add, op1=ALU.mult).then_inc(xt_ready.sem, 1)
        if key == "a":
            dve.wait_ge(fr_done.sem, fdone(f, "a"))
            if due(f - 1):
                dve.wait_ge(part_ready.sem, part_ready.of(f - 1))
            for i in range(TG):
                DVE.tensor_tensor_scan(cs[:, col(i)], ones[0:NH, :], fr.bank("a")[0:NH, col(i)], 0.0,
                                       ALU.mult, ALU.add).then_inc(scan_ready.sem, 1)
        if key == "c2":
            dve.wait_ge(scan_ready.sem, scan_ready.of(f))
            if due(f - 2):
                dve.wait_ge(ee_done.sem, ee_done.of((f - 2) * TG + TG - 1))
            pr = lambda k: parts[32 * k:32 * k + NH, par, :]
            DVE.tensor_scalar(pr(0), cs[:], ascale[:, 0:1], None, ALU.mult).then_inc(part_ready.sem, 1)
            dve.wait_ge(part_ready.sem, part_ready.of(f, 1))
            DVE.scalar_tensor_tensor(out=resid1[:], in0=cs[:], scalar=ascale[:, 0:1], in1=pr(0),
                                     op0=ALU.mult, op1=ALU.subtract).then_inc(part_ready.sem, 1)
            dve.wait_ge(part_ready.sem, part_ready.of(f, 2))
            DVE.tensor_copy(mid[:], resid1[:]).then_inc(part_ready.sem, 1)
            DVE.tensor_copy(pr(1), resid1[:]).then_inc(part_ready.sem, 1)
            dve.wait_ge(part_ready.sem, part_ready.of(f, 3))
            DVE.tensor_tensor(pr(2), resid1[:], mid[:], ALU.subtract).then_inc(part_ready.sem, 1)
        if key == "c3":
            dve.wait_ge(fr_done.sem, fdone(f, "c3"))
            if due(f - 2):
                dve.wait_ge(yy_done.sem, yy_done.of((f - 2) * TG + TG - 1))
            split_c(DVE.tensor_copy, 3, par, fr, ctd_ready)
        if key in ("z0", "z1"):
            n = int(key[1])
            dve.wait_ge(zth_ready.sem, zth_ready.of(f, n + 1))
            DVE.scalar_tensor_tensor(out=zt[:, par, n, :], in0=zth[:], scalar=1.0, in1=fr.bank(key)[:],
                                     op0=ALU.add, op1=ALU.mult).then_inc(zt_ready.sem, 1)

    def pool_history(pl, f, par, first_of_batch):
        if due(f - 2):
            pl.wait_ge(conv_step.sem, conv_step.of(f - 2))
        if first_of_batch:
            apart(pl, f)
            PL.memset(xraw[:, par, :, 0:KC - 1], 0.0).then_inc(hist_ready.sem, 1)
        else:
            if due(f - 1):
                pl.wait_ge(xraw_ready.sem, xraw_ready.of(f - 1))
            apart(pl, f)
            PL.tensor_copy(xraw[:, par, :, 0:KC - 1], xraw[:, 1 - par, :, GT:GT + KC - 1]
                           ).then_inc(hist_ready.sem, 1)

    def pool_softplus(pl, f):
        pl.wait_ge(dta_ready.sem, dta_ready.of(f))
        pl.wait_ge(dtv_ready.sem, dtv_ready.of(f))
        apart(pl, f)
        PL.tensor_tensor(dtv[:], dtv[:], dta[:], ALU.add).then_inc(dtr_ready.sem, 1)

    def pe_decays(pe, t, i, g, par):
        c = col(i)
        if i == 0:
            pe.wait_ge(part_ready.sem, part_ready.of(g))
        for hf in range(2):
            bank = banks[2 + hf]
            if due(t - 1):
                pe.wait_ge(m_ready.sem, m_ready.of(t - 1, hf + 1))
            PE.matmul(bank[:], parts[:, par, c], negsel[:, hf * HH:(hf + 1) * HH, :], start=True, stop=False,
                      skip_group_check=True)
            for q in range(HH):
                mm = PE.matmul(bank[:, col(q)], sel_a[:, hf * HH + q, :], parts[:, par, c], start=False,
                               stop=q == HH - 1, skip_group_check=True)
            mm.then_inc(dd_done.sem, 1)

    def pe_scores(pe, t, i, g, par):
        if i == 0:
            pe.wait_ge(bt_ready.sem, bt_ready.of(g))
            pe.wait_ge(cta_ready.sem, cta_ready.of(g))
            pe.wait_ge(ctd_ready.sem, ctd_ready.of(g))
        for hf in range(2):
            bank = banks[4 + hf]
            if due(t - 1):
                pe.wait_ge(mg_ready.sem, mg_ready.of(t - 1, hf + 1))
            for j in range(2):
                mm = PE.matmul(bank[:, col(j, 2 * P)], bt[:, par, 2 * hf + j, col(i)],
                               ct[:, par, 2 * hf + j, i, :, :], start=True, stop=True)
            mm.then_inc(gg_done.sem, 1)

    def pe_turns(pe, t, i, g, par, fr):
        c = col(i)
        if i == 0:
            pe.wait_ge(xt_ready.sem, xt_ready.of(g))
        fr.free(pe, "xtr", i)
        for n in range(NB):
            mm = PE.transpose(fr.bank("xtr", i)[:, col(n)], xt[:, par, n, c], ident[:])
        mm.then_inc(xtr_done.sem, 1)
        if due(t - 1):
            pe.wait_ge(state_ready.sem, state_ready.of(t - 1))
        for j in range(NP):
            mm = PE.transpose(banks[7][:, col(j)], bt[:, par, j, c], ident[:])
        mm.then_inc(btr_done.sem, 1)
        if due(t - 1):
            pe.wait_ge(y_step.sem, y_step.of(t - 1, 3))
        for n in range(NB):
            PE.matmul(banks[6][:, col(n)], sel_e[:, n, :], parts[:, par, c], start=True, stop=True,
                      skip_group_check=True)
        last = parts[:, par, i * P + P - 1:i * P + P]
        PE.matmul(banks[6][:, DI:DI + NH], last.to_broadcast([P, P]), sel_a[:, :, 0], start=True, stop=True,
                  skip_group_check=True).then_inc(ee_done.sem, 1)

    def pe_out_tile(pe, t, tp, last=False):
        pe.wait_ge(y4_ready.sem, y4_ready.of(t))
        pe.wait_ge(ysq_ready.sem, ysq_ready.of(t))
        if last:
            pe.wait_ge(state_ready.sem, state_ready.of(t))
        else:
            pe.wait_ge(btok_ready.sem, btok_ready.of(t + 1))
        bank = banks[7]
        for n in range(NB):
            PE.matmul(bank[:, 0:D], y4[:, tp, n, :], wo[:, n, :], start=n == 0, stop=n == NB - 1)
        for n in range(NB):
            mm = PE.matmul(bank[:, D:2 * D], ysq[:, tp, n, :], ones[:], start=n == 0, stop=n == NB - 1)
        mm.then_inc(oo_done.sem, 1)

    def pe_y(pe, t, i, g, par, tp, first_tile):
        pe.wait_ge(xtok_ready.sem, xtok_ready.of(t))
        pe.wait_ge(e_ready.sem, e_ready.of(t))
        pe.wait_ge(mg_ready.sem, mg_ready.of(t, 1))
        for hd in range(NH):
            if hd == HH:
                pe.wait_ge(mg_ready.sem, mg_ready.of(t, 2))
            q, n = hd % 4, hd // 4
            PE.matmul(banks[6][q * HD:(q + 1) * HD, col(n)], xtok[:, tp, hd * HD:(hd + 1) * HD], mg[:, tp, hd, :],
                      start=True, stop=True, skip_group_check=True)
        if due(t - 1):
            pe.wait_ge(state_ready.sem, state_ready.of(t - 1))
        for hd in range(NH):
            q, n = hd % 4, hd // 4
            mm = PE.matmul(banks[6][q * HD:(q + 1) * HD, DI + n * P:DI + (n + 1) * P],
                           state[:, 1 - tp, hd // 2, :], ct[:, par, hd // 2, i, hd % 2, :],
                           start=True, stop=True, skip_group_check=True)
        mm.then_inc(yy_done.sem, 1)
        pe.wait_ge(btok_ready.sem, btok_ready.of(t))
        pe.wait_ge(xw_ready.sem, xw_ready.of(t))
        if due(t - 1):
            pe.wait_ge(og_ready.sem, og_ready.of(t - 1))
        for j in range(NP):
            n = j // 2
            mm = PE.matmul(banks[7][:, col(j)], btok[:, tp, col(j)], xw[:, tp, col(n)], start=True, stop=True,
                           skip_group_check=True)
        mm.then_inc(ss_done.sem, 1)

    def act_decays(act, t, tp):
        for hf in range(2):
            act.wait_ge(dd_done.sem, dd_done.of(t, hf + 1))
            if hf == 0 and due(t - 2):
                act.wait_ge(mg_ready.sem, mg_ready.of(t - 2))
                act.wait_ge(xw_ready.sem, xw_ready.of(t - 2))
            SE.activation(m[:, tp, hf * HH:(hf + 1) * HH, :], banks[2 + hf][:].rearrange("p (h l) -> p h l", l=P),
                          ACT.Exp).then_inc(m_ready.sem, 1)

    def act_turned(act, t, i, tp, fr):
        act.wait_ge(xtr_done.sem, xtr_done.of(t))
        if due(t - 2):
            act.wait_ge(yy_done.sem, yy_done.of(t - 2))
            act.wait_ge(xw_ready.sem, xw_ready.of(t - 2))
        SE.activation(xtok[:, tp, :], fr.bank("xtr", i)[:, 0:DI], ACT.Copy).then_inc(xtok_ready.sem, 1)
        act.wait_ge(btr_done.sem, btr_done.of(t))
        if due(t - 2):
            act.wait_ge(ss_done.sem, ss_done.of(t - 2))
        SE.activation(btok[:, tp, :], banks[7][:], ACT.Copy).then_inc(btok_ready.sem, 1)
        act.wait_ge(ee_done.sem, ee_done.of(t))
        if due(t - 2):
            act.wait_ge(y_step.sem, y_step.of(t - 2))
            act.wait_ge(dec_ready.sem, dec_ready.of(t - 2))
        SE.activation(edec[:, tp, :, :], banks[6][:, 0:DI].rearrange("p (n l) -> p n l", l=P),
                      ACT.Exp).then_inc(e_ready.sem, 1)
        for q in range(2):
            rows = slice(q * NS, (q + 1) * NS)
            SE.activation(tdec[rows, tp, :], banks[6][rows, DI + q:DI + NH:2], ACT.Exp).then_inc(e_ready.sem, 1)

    def act_square(act, t, tp):
        act.wait_ge(y4_ready.sem, y4_ready.of(t))
        if due(t - 2):
            act.wait_ge(oo_done.sem, oo_done.of(t - 2))
        SE.activation(ysq[:, tp, :, :], y4[:, tp, :, :], ACT.Square).then_inc(ysq_ready.sem, 1)

    def act_out(act, t, i, par, g):
        if i == 0:
            if due(g - 2):
                act.wait_ge(post_dve1.sem, post_dve1.of(g - 2))
        act.wait_ge(oo_done.sem, oo_done.of(t))
        SE.activation(og[:, par, i, 0:D + 1], banks[7][:, 0:D + 1], ACT.Copy).then_inc(og_ready.sem, 1)

    def pool_tile(pl, t, i, g, par, tp, first_tile):
        for hf in range(2):
            v = m[:, tp, hf * HH:(hf + 1) * HH, :]
            pl.wait_ge(m_ready.sem, m_ready.of(t, hf + 1))
            apart(pl, t)
            PL.affine_select(out=v, in_=v, compare_op=ALU.is_ge, fill=0.0, base=0, pattern=[[0, HH], [1, P]],
                             channel_multiplier=-1).then_inc(mm_ready.sem, 1)
        pl.wait_ge(xtok_ready.sem, xtok_ready.of(t))
        if due(t - 2):
            pl.wait_ge(ss_done.sem, ss_done.of(t - 2))
        for hf in range(2):
            pl.wait_ge(mm_ready.sem, mm_ready.of(t, hf + 1))
            apart(pl, t)
            PL.tensor_tensor(xw[:, tp, col(hf)].rearrange("p (h d) -> p h d", d=HD),
                             xtok[:, tp, col(hf)].rearrange("p (h d) -> p h d", d=HD),
                             m[:, tp, hf * HH:(hf + 1) * HH, P - 1:P].to_broadcast([P, HH, HD]),
                             ALU.mult).then_inc(xw_ready.sem, 1)
        pl.wait_ge(e_ready.sem, e_ready.of(t))
        if due(t - 1):
            pl.wait_ge(state_ready.sem, state_ready.of(t - 1))
        apart(pl, t)
        PL.tensor_tensor(decayed[:], state[:, 1 - tp, :, :],
                         tdec[:, tp, :].rearrange("p (j o) -> p j o", o=1).to_broadcast([P, NP, HD]),
                         ALU.mult).then_inc(dec_ready.sem, 1)

    def pool_gate(pl, t, i, par, tp):
        pl.wait_ge(y_step.sem, y_step.of(t))
        if due(t - 2):
            pl.wait_ge(oo_done.sem, oo_done.of(t - 2))
        apart(pl, t)
        PL.tensor_tensor(y4[:, tp, :, :], y3[:], zt[:, par, :, col(i)], ALU.mult).then_inc(y4_ready.sem, 1)

    def dve_scores(dve, t, tp):
        if due(t - 2):
            dve.wait_ge(yy_done.sem, yy_done.of(t - 2))
        for hf in range(2):
            heads = slice(hf * HH, (hf + 1) * HH)
            dve.wait_ge(gg_done.sem, gg_done.of(t, hf + 1))
            dve.wait_ge(mm_ready.sem, mm_ready.of(t, hf + 1))
            DVE.tensor_tensor(mg[:, tp, heads, :], banks[4 + hf][:].rearrange("p (h l) -> p h l", l=P),
                              m[:, tp, heads, :], ALU.mult).then_inc(mg_ready.sem, 1)

    def dve_y(dve, t, i, par, tp):
        dve.wait_ge(yy_done.sem, yy_done.of(t))
        dve.wait_ge(e_ready.sem, e_ready.of(t))
        DVE.tensor_tensor(y1[:], banks[6][:, DI:2 * DI].rearrange("p (n l) -> p n l", l=P), edec[:, tp, :, :],
                          ALU.mult).then_inc(y_step.sem, 1)
        for n in range(NB):
            DVE.scalar_tensor_tensor(out=y2[:, n, :], in0=xt[:, par, n, col(i)], scalar=dcol[:, n:n + 1],
                                     in1=banks[6][:, col(n)], op0=ALU.mult, op1=ALU.add).then_inc(y_step.sem, 1)
        dve.wait_ge(y_step.sem, y_step.of(t, 3))
        if due(t - 1):
            dve.wait_ge(y4_ready.sem, y4_ready.of(t - 1))
        DVE.tensor_tensor(y3[:], y1[:], y2[:], ALU.add).then_inc(y_step.sem, 1)

    def dve_state(dve, t, tp, last_of_batch):
        dve.wait_ge(ss_done.sem, ss_done.of(t))
        dve.wait_ge(dec_ready.sem, dec_ready.of(t))
        for q in range(2):
            rows = slice(q * NS, (q + 1) * NS)
            if last_of_batch:
                DVE.memset(state[rows, tp, :, :], 0.0).then_inc(state_ready.sem, 1)
                continue
            s = banks[7][rows, :].rearrange("p (n k d) -> p n k d", n=NB, d=HD)[:, :, q:q + 7:6, :]
            DVE.tensor_tensor(state[rows, tp, :, :].rearrange("p (n j) d -> p n j d", n=2), s,
                              decayed[rows, :, :].rearrange("p (n j) d -> p n j d", n=2),
                              ALU.add).then_inc(state_ready.sem, 1)

    def pool_post1(pl, g, par):
        pl.wait_ge(og_ready.sem, og_ready.of(g * TG + TG - 1))
        apart(pl, g)
        PL.tensor_scalar(pt[:, 0, :], og[:, par, :, D], 1.0 / DI, RMS_EPS, ALU.mult, ALU.add
                         ).then_inc(post_pool1.sem, 1)
        pl.wait_ge(post_pool1.sem, post_pool1.of(g, 1))
        apart(pl, g)
        PL.tensor_tensor(pt[:, 1, :], pt[:, 0, :], neghalf[:], ALU.pow).then_inc(post_pool1.sem, 1)

    def dve_xn(dve, g, dyn):
        for i in range(TG):
            t1 = dyn(g * TG + i, 1)
            DVE.tensor_scalar(xn[:, i, :], xall[:, t1, :].rearrange("p o d -> p (o d)"), s1[:, t1], nb1[:, t1],
                              ALU.mult, ALU.add).then_inc(xn_ready.sem, 1)

    def dve_post1(dve, g, par):
        dve.wait_ge(post_pool1.sem, post_pool1.of(g))
        for i in range(TG):
            dve.wait_ge(xn_ready.sem, xn_ready.of(g, i + 1))
            DVE.scalar_tensor_tensor(out=ob[:, i, :], in0=og[:, par, i, 0:D], scalar=pt[:, 1, i:i + 1],
                                     in1=xn[:, i, :], op0=ALU.mult, op1=ALU.add).then_inc(post_dve1.sem, 1)
        for i in range(TG):
            dve.wait_ge(post_dve1.sem, post_dve1.of(g, i + 1))
            DVE.bn_stats(pst6[:, i, :], ob[:, i, :]).then_inc(post_dve1.sem, 1)
        for i in range(TG):
            dve.wait_ge(post_dve1.sem, post_dve1.of(g, TG + i + 1))
            apart(dve, g)
            DVE.bn_aggr(pmv[:, i, :], pst6[:, i, :]).then_inc(post_dve1.sem, 1)

    def pool_post2(pl, g):
        pl.wait_ge(post_dve1.sem, post_dve1.of(g))
        apart(pl, g)
        PL.tensor_scalar(pt[:, 2, :], pmv[:, :, 1], LN_EPS, None, ALU.add).then_inc(post_pool2.sem, 1)
        pl.wait_ge(post_pool2.sem, post_pool2.of(g, 1))
        apart(pl, g)
        PL.tensor_tensor(pt[:, 3, :], pt[:, 2, :], neghalf[:], ALU.pow).then_inc(post_pool2.sem, 1)
        pl.wait_ge(post_pool2.sem, post_pool2.of(g, 2))
        apart(pl, g)
        PL.tensor_scalar(pt[:, 4, :], pmv[:, :, 0], -1.0, None, ALU.mult).then_inc(post_pool2.sem, 1)
        pl.wait_ge(post_pool2.sem, post_pool2.of(g, 3))
        apart(pl, g)
        PL.tensor_tensor(pt[:, 5, :], pt[:, 4, :], pt[:, 3, :], ALU.mult).then_inc(post_pool2.sem, 1)

    def dve_post2(dve, g, dyn):
        dve.wait_ge(post_pool2.sem, post_pool2.of(g))
        for i in range(TG):
            DVE.tensor_scalar(xb[:, i, :], xall[:, dyn(g * TG + i, 1), :].rearrange("p o d -> p (o d)"),
                              pt[:, 5, i:i + 1], None, ALU.add).then_inc(xb_ready.sem, 1)
        for i in range(TG):
            dve.wait_ge(xb_ready.sem, xb_ready.of(g, i + 1))
            DVE.scalar_tensor_tensor(out=xall[:, dyn(g * TG + i, 1), :].rearrange("p o d -> p (o d)"),
                                     in0=ob[:, i, :], scalar=pt[:, 3, i:i + 1],
                                     in1=xb[:, i, :], op0=ALU.mult, op1=ALU.add).then_inc(x2_ready.sem, 1)

    def run(eng, what, b, u, last):
        g = b * GB + u
        dyn = static if isinstance(b, int) else dynamic
        par = u
        ahead = not (last and u == GB - 1)
        f = g + 1 if ahead else None
        prior = fr_uses(g, g - 1 if not (isinstance(g, int) and g == 0) else None)
        if isinstance(g, int) and g == 0:
            prior = [x for x in prior if x]
        fr = Front(g, f, prior)
        norm = not (last)
        for i in range(TG):
            t, tp = g * TG + i, i % 2
            what(eng, t=t, i=i, g=g, f=f, par=par, tp=tp, fr=fr, dyn=dyn, norm=norm,
                 end_of_batch=u == GB - 1 and i == TG - 1, begin=isinstance(t, int) and t == 0, fu=(u + 1) % GB)

    def pe_body(pe, t, i, g, f, par, tp, fr, dyn, norm, end_of_batch, begin, fu):
        pe_decays(pe, t, i, g, par)
        if f is not None:
            pe_front(pe, f, fu, fr, i, 0)
        pe_scores(pe, t, i, g, par)
        if f is not None:
            pe_front(pe, f, fu, fr, i, 1)
        pe_turns(pe, t, i, g, par, fr)
        if f is not None:
            pe_front(pe, f, fu, fr, i, 2)
        if not begin:
            pe_out_tile(pe, t - 1, 1 - tp)
        if f is not None:
            pe_front(pe, f, fu, fr, i, 3)
        pe_y(pe, t, i, g, par, tp, begin)

    def act_body(act, t, i, g, f, par, tp, fr, dyn, norm, end_of_batch, begin, fu):
        act_decays(act, t, tp)
        if not begin:
            act_square(act, t - 1, 1 - tp)
        if f is not None:
            act_front(act, f, fu, fr, i, 0)
            act_front(act, f, fu, fr, i, 1)
        act_turned(act, t, i, tp, fr)
        if f is not None:
            act_front(act, f, fu, fr, i, 2)
        if not begin:
            act_out(act, t - 1, (i - 1) % TG, par if i else 1 - par, g)
        if f is not None:
            act_front(act, f, fu, fr, i, 3)
        if i == 3 and norm:
            act_h(act, g + 2, par, dyn)

    def dve_body(dve, t, i, g, f, par, tp, fr, dyn, norm, end_of_batch, begin, fu):
        if f is not None:
            dve_front(dve, f, fu, fr, i, 0)
            dve_front(dve, f, fu, fr, i, 1)
        has_post = not (isinstance(g, int) and g == 0)
        if i == 2 and has_post:
            dve_post1(dve, g - 1, 1 - par)
        dve_scores(dve, t, tp)
        if f is not None:
            dve_front(dve, f, fu, fr, i, 2)
        if i == 0 and norm:
            dve_stats(dve, g + 2, dyn)
        if i == 0 and has_post and not (isinstance(g, int) and g == 1):
            dve_post2(dve, g - 2, dyn)
        if i == 1 and has_post:
            dve_xn(dve, g - 1, dyn)
        if f is not None:
            dve_front(dve, f, fu, fr, i, 3)
        dve_y(dve, t, i, par, tp)
        dve_state(dve, t, tp, end_of_batch)

    def pool_body(pl, t, i, g, f, par, tp, fr, dyn, norm, end_of_batch, begin, fu):
        pool_tile(pl, t, i, g, par, tp, begin)
        has_post = not (isinstance(g, int) and g == 0)
        if i == 0:
            if f is not None:
                pool_history(pl, f, fu, fu == 0)
            if has_post:
                pool_post1(pl, g - 1, 1 - par)
        if i == 1 and f is not None:
            pool_softplus(pl, f)
        if i == 2 and norm:
            pool_norm(pl, g + 2, dyn)
        if i == 3 and has_post:
            pool_post2(pl, g - 1)
        pool_gate(pl, t, i, par, tp)

    def over_sequences(eng, body):
        for u in range(GB):
            run(eng, body, 0, u, False)
        with eng.Fori(1, BATCH - 1) as b:
            for u in range(GB):
                run(eng, body, b, u, False)
        for u in range(GB):
            run(eng, body, BATCH - 1, u, True)

    G_LAST, T_LAST = GROUPS - 1, TILES - 1
    with nc.Block() as block:
        @block.sync
        def _(sp):
            load_all(sp)

        @block.tensor
        def _(pe):
            pe_prepare(pe)
            fr = Front(None, 0, [])
            for i in range(TG):
                for slot in range(SLOTS):
                    pe_front(pe, 0, 0, fr, i, slot)
            over_sequences(pe, pe_body)
            pe_out_tile(pe, T_LAST, T_LAST % 2, last=True)

        @block.scalar
        def _(act):
            act_prepare(act)
            act_h(act, 0, 0, static)
            act_h(act, 1, 1, static)
            fr = Front(None, 0, [])
            for i in range(TG):
                for slot in range(SLOTS):
                    act_front(act, 0, 0, fr, i, slot)
            over_sequences(act, act_body)
            act_square(act, T_LAST, T_LAST % 2)
            act_out(act, T_LAST, TG - 1, 1, G_LAST)

        @block.vector
        def _(dve):
            dve.wait_ge(loaded0, 32)
            dve_stats(dve, 0, static)
            dve_stats(dve, 1, static)
            dve_prepare(dve)
            dve.wait_ge(const_step.sem, const_step.of(0, CONSTS))
            fr = Front(None, 0, [])
            for i in range(TG):
                for slot in range(SLOTS):
                    dve_front(dve, 0, 0, fr, i, slot)
            dve.wait_ge(loaded1, 16)
            over_sequences(dve, dve_body)
            dve_post2(dve, G_LAST - 1, static)
            dve_xn(dve, G_LAST, static)
            dve_post1(dve, G_LAST, 1)
            dve_post2(dve, G_LAST, static)

        @block.gpsimd
        def _(pl):
            assert pool_constants(pl) == CONSTS
            pl.wait_ge(loaded0, 32)
            pool_norm(pl, 0, static)
            pool_norm(pl, 1, static)
            pool_history(pl, 0, 0, True)
            pool_softplus(pl, 0)
            over_sequences(pl, pool_body)
            pool_post1(pl, G_LAST, 1)
            pool_post2(pl, G_LAST)


def experts(nc, buffers, xall, banks, wg_d, w1_d, b1_d, w2_d, b2_d, out):
    def sb(name, shape, dt=F32):
        return buffers.enter_context(nc.sbuf_tensor("moe_" + name, shape, dt))

    def sig(name, per=1):
        return Signal(nc, "moe_" + name, per)

    PE, DVE, SE, PL = nc.tensor, nc.vector, nc.scalar, nc.gpsimd

    ident = sb("ident", [P, P])
    neghalf = sb("neghalf", [P, TG])
    ones3 = sb("ones3", [P, P], BF16)
    b2p = sb("b2_parts", [P, NE * D], BF16)
    b2row = sb("b2_row", [1, NE * D])
    b2res = sb("b2_rest", [1, NE * D])
    b2mid = sb("b2_mid", [1, NE * D], BF16)
    w1f = sb("w1", [P, NE, FH])
    w1hi = sb("w1_hi", [P, NE, FH], F32R)
    w1lo = sb("w1_lo", [P, NE, FH], F32R)
    w2 = sb("w2", [P, NE, FB, D])
    wg = sb("wg", [P, NE])
    b1row = sb("b1_rows", [NE * FB, P])
    b1 = sb("b1", [P, NE * FB])
    rank = sb("rank", [P, TG, NE])
    iota = sb("iota", [P, TG, NE])

    st6 = sb("st6", [P, TG, 6])
    mv = sb("mv", [P, TG, 2])
    lnt = sb("lnt", [P, 4, TG])
    h = sb("h", [P, TG, D])
    thi = sb("t_hi", [P, 2, GT], F32R)
    tlo = sb("t_lo", [P, 2, GT], F32R)
    tf = sb("t", [P, GT])
    route = sb("route", [P, 10, TG, NE])
    rmax = sb("rmax", [P, 6, TG])
    scores = sb("scores", [P, 2, TG, NE])
    hid = sb("hid", [P, 2, FB, GT])
    acc = sb("acc", [P, 2, TG, D])
    post = sb("post", [P, 4, TG])
    pst6 = sb("pst6", [P, TG, 6])
    pmv = sb("pmv", [P, TG, 2])
    xb = sb("xb", [P, TG, D])
    outb = sb("outb", [P, 2, TG, D])

    loaded = nc.alloc_semaphore("moe_weights_loaded")
    LOADS = 5 * 16
    const_step = sig("constants", 1)
    prep = sig("weights_prepared", 1)
    prep_pe = sig("b1_turned", 1)
    ln_stats = sig("ln_stats_ready", 2 * TG)
    coef_step = sig("ln_coefficient_steps", 4)
    h_ready = sig("h_ready", TG)
    turned = sig("h_turned")
    thi_ready = sig("t_hi_ready")
    tf_ready = sig("t_ready")
    tlo_ready = sig("t_lo_ready")
    logits = sig("logits_done")
    route_a = sig("route_before_exp", 2)
    exp_ready = sig("exp_ready")
    ROUTE = 13
    route_b = sig("route_steps", ROUTE)
    up_done = sig("up_done", NE * FB)
    hid_ready = sig("hidden_ready", NE * FB)
    down_done = sig("down_done", NE)
    acc_step = sig("mix_steps", NE * TG)
    stats2 = sig("post_stats", 2 * TG)
    post_pool = sig("post_ln", 4)
    xb_ready = sig("xb_ready", TG)
    out_ready = sig("out_ready", TG)
    stored = [nc.alloc_semaphore(f"moe_stored{u}") for u in range(2)]

    def tile(g, i, dyn):
        return xall[:, dyn(g * TG + i, 1), :].rearrange("p o d -> p (o d)")

    def pool_constants(pl):
        n = [0]

        def then(ins):
            ins.then_inc(const_step.sem, 1)
            n[0] += 1
            pl.wait_ge(const_step.sem, const_step.of(0, n[0]))

        for ap, v in ((ident[:], 0.0), (neghalf[:], -0.5), (ones3[:], 0.0), (b2p[:], 0.0)):
            then(PL.memset(ap, v))
        then(PL.affine_select(out=ident[:], in_=ident[:], compare_op=ALU.not_equal, fill=1.0, base=0,
                              pattern=[[-1, P]], channel_multiplier=1))
        for k in range(PARTS):
            then(PL.memset(ones3[32 * k:32 * k + 1, :], 1.0))
        for e in range(NE):
            then(PL.memset(rank[:, :, e:e + 1], float(NE - e)))
        return n[0]

    CONSTS = 4 + 1 + PARTS + NE
    PREP = 9

    def dve_prepare(dve):
        n = [0]

        def then(ins):
            ins.then_inc(prep.sem, 1)
            n[0] += 1
            dve.wait_ge(prep.sem, prep.of(0, n[0]))

        dve.wait_ge(loaded, LOADS)
        dve.wait_ge(const_step.sem, const_step.of(0, CONSTS))
        then(DVE.tensor_copy(w1hi[:], w1f[:]))
        then(DVE.tensor_tensor(w1lo[:], w1f[:], w1hi[:].bitcast(F32), ALU.subtract))
        then(DVE.tensor_copy(b2p[0:1, :], b2row[:]))
        then(DVE.tensor_tensor(b2res[:], b2row[:], b2p[0:1, :], ALU.subtract))
        then(DVE.tensor_copy(b2p[32:33, :], b2res[:]))
        then(DVE.tensor_copy(b2mid[:], b2res[:]))
        then(DVE.tensor_tensor(b2p[64:65, :], b2res[:], b2mid[:], ALU.subtract))
        dve.wait_ge(prep_pe.sem, prep_pe.of(0, 1))
        then(DVE.tensor_copy(b1[:], banks[7][:, 0:NE * FB]))
        then(DVE.memset(acc[:], 0.0))
        assert n[0] == PREP

    def dve_stats(dve, f, dyn):
        if due(f - 1):
            dve.wait_ge(coef_step.sem, coef_step.of(f - 1))
        for i in range(TG):
            DVE.bn_stats(st6[:, i, :], tile(f, i, dyn)).then_inc(ln_stats.sem, 1)
        for i in range(TG):
            dve.wait_ge(ln_stats.sem, ln_stats.of(f, i + 1))
            apart(dve, f)
            DVE.bn_aggr(mv[:, i, :], st6[:, i, :]).then_inc(ln_stats.sem, 1)

    def pool_norm(pl, f):
        pl.wait_ge(ln_stats.sem, ln_stats.of(f))
        if due(f - 1):
            pl.wait_ge(h_ready.sem, h_ready.of(f - 1))
        apart(pl, f)
        PL.tensor_scalar(lnt[:, 0, :], mv[:, :, 1], LN_EPS, None, ALU.add).then_inc(coef_step.sem, 1)
        pl.wait_ge(coef_step.sem, coef_step.of(f, 1))
        apart(pl, f)
        PL.tensor_tensor(lnt[:, 1, :], lnt[:, 0, :], neghalf[:], ALU.pow).then_inc(coef_step.sem, 1)
        pl.wait_ge(coef_step.sem, coef_step.of(f, 2))
        apart(pl, f)
        PL.tensor_scalar(lnt[:, 2, :], mv[:, :, 0], -1.0, None, ALU.mult).then_inc(coef_step.sem, 1)
        pl.wait_ge(coef_step.sem, coef_step.of(f, 3))
        apart(pl, f)
        PL.tensor_tensor(lnt[:, 3, :], lnt[:, 2, :], lnt[:, 1, :], ALU.mult).then_inc(coef_step.sem, 1)

    def dve_h(dve, f, dyn):
        dve.wait_ge(coef_step.sem, coef_step.of(f))
        if due(f - 1):
            dve.wait_ge(turned.sem, turned.of(f - 1))
        for i in range(TG):
            DVE.tensor_scalar(h[:, i, :], tile(f, i, dyn), lnt[:, 1, i:i + 1], lnt[:, 3, i:i + 1],
                              ALU.mult, ALU.add).then_inc(h_ready.sem, 1)

    def pe_turn(pe, f):
        pe.wait_ge(h_ready.sem, h_ready.of(f))
        if due(f - 1):
            pe.wait_ge(tlo_ready.sem, tlo_ready.of(f - 1))
            pe.wait_ge(tf_ready.sem, tf_ready.of(f - 1))
        for i in range(TG):
            mm = PE.transpose(banks[6][:, col(i)], h[:, i, :], ident[:])
        mm.then_inc(turned.sem, 1)

    def act_turned(act, f, par):
        act.wait_ge(turned.sem, turned.of(f))
        if due(f - 2):
            act.wait_ge(up_done.sem, up_done.of(f - 2))
        SE.activation(thi[:, par, :], banks[6][:], ACT.Copy).then_inc(thi_ready.sem, 1)
        if due(f - 1):
            act.wait_ge(logits.sem, logits.of(f - 1))
        SE.activation(tf[:], banks[6][:], ACT.Copy).then_inc(tf_ready.sem, 1)

    def dve_turned(dve, f, par):
        dve.wait_ge(thi_ready.sem, thi_ready.of(f))
        dve.wait_ge(tf_ready.sem, tf_ready.of(f))
        if due(f - 2):
            dve.wait_ge(up_done.sem, up_done.of(f - 2))
        DVE.tensor_tensor(tlo[:, par, :], banks[6][:], thi[:, par, :].bitcast(F32),
                          ALU.subtract).then_inc(tlo_ready.sem, 1)

    def pe_logits(pe, f):
        pe.wait_ge(tf_ready.sem, tf_ready.of(f))
        if due(f - 1):
            pe.wait_ge(route_a.sem, route_a.of(f - 1))
        for i in range(TG):
            mm = PE.matmul(banks[7][:, i * NE:(i + 1) * NE], tf[:, col(i)], wg[:], start=True, stop=True,
                           skip_group_check=True)
        mm.then_inc(logits.sem, 1)

    def wide(v):
        return v.rearrange("p (t o) -> p t o", o=1).to_broadcast([P, TG, NE])

    def dve_route_a(dve, f):
        lg = banks[7][:, 0:TG * NE].rearrange("p (t e) -> p t e", e=NE)
        dve.wait_ge(logits.sem, logits.of(f))
        if due(f - 1):
            dve.wait_ge(route_b.sem, route_b.of(f - 1))
        DVE.tensor_reduce(rmax[:, 0, :], lg, AX, ALU.max).then_inc(route_a.sem, 1)
        dve.wait_ge(route_a.sem, route_a.of(f, 1))
        if due(f - 1):
            dve.wait_ge(exp_ready.sem, exp_ready.of(f - 1))
        DVE.tensor_tensor(route[:, 0], lg, wide(rmax[:, 0, :]), ALU.subtract).then_inc(route_a.sem, 1)

    def act_exp(act, f):
        act.wait_ge(route_a.sem, route_a.of(f))
        if due(f - 1):
            act.wait_ge(route_b.sem, route_b.of(f - 1))
        SE.activation(route[:, 1], route[:, 0], ACT.Exp).then_inc(exp_ready.sem, 1)

    def dve_route_b(dve, f, par):
        d, e, r = route[:, 0], route[:, 1], lambda k: route[:, 2 + k]
        dve.wait_ge(route_a.sem, route_a.of(f))
        DVE.scalar_tensor_tensor(out=r(0), in0=d, scalar=0.0, in1=rank[:], op0=ALU.is_equal,
                                 op1=ALU.mult).then_inc(route_b.sem, 1)
        dve.wait_ge(route_b.sem, route_b.of(f, 1))
        DVE.tensor_reduce(rmax[:, 1, :], r(0), AX, ALU.max).then_inc(route_b.sem, 1)
        dve.wait_ge(route_b.sem, route_b.of(f, 2))
        DVE.tensor_tensor(r(1), rank[:], wide(rmax[:, 1, :]), ALU.is_equal).then_inc(route_b.sem, 1)
        dve.wait_ge(route_b.sem, route_b.of(f, 3))
        DVE.scalar_tensor_tensor(out=r(2), in0=r(1), scalar=-1e30, in1=d, op0=ALU.mult,
                                 op1=ALU.add).then_inc(route_b.sem, 1)
        dve.wait_ge(route_b.sem, route_b.of(f, 4))
        DVE.tensor_reduce(rmax[:, 2, :], r(2), AX, ALU.max).then_inc(route_b.sem, 1)
        dve.wait_ge(route_b.sem, route_b.of(f, 5))
        DVE.tensor_tensor(r(3), r(2), wide(rmax[:, 2, :]), ALU.is_equal).then_inc(route_b.sem, 1)
        dve.wait_ge(route_b.sem, route_b.of(f, 6))
        DVE.tensor_tensor(r(4), r(3), rank[:], ALU.mult).then_inc(route_b.sem, 1)
        dve.wait_ge(route_b.sem, route_b.of(f, 7))
        DVE.tensor_reduce(rmax[:, 3, :], r(4), AX, ALU.max).then_inc(route_b.sem, 1)
        dve.wait_ge(route_b.sem, route_b.of(f, 8))
        DVE.tensor_tensor(r(5), rank[:], wide(rmax[:, 3, :]), ALU.is_equal).then_inc(route_b.sem, 1)
        dve.wait_ge(route_b.sem, route_b.of(f, 9))
        DVE.tensor_tensor(r(6), r(1), r(5), ALU.add).then_inc(route_b.sem, 1)
        dve.wait_ge(route_b.sem, route_b.of(f, 10))
        dve.wait_ge(exp_ready.sem, exp_ready.of(f))
        DVE.tensor_tensor(r(7), r(6), e, ALU.mult).then_inc(route_b.sem, 1)
        dve.wait_ge(route_b.sem, route_b.of(f, 11))
        DVE.tensor_reduce(rmax[:, 4, :], r(7), AX, ALU.add).then_inc(route_b.sem, 1)
        dve.wait_ge(route_b.sem, route_b.of(f, 12))
        DVE.reciprocal(rmax[:, 5, :], rmax[:, 4, :]).then_inc(route_b.sem, 1)
        dve.wait_ge(route_b.sem, route_b.of(f))
        if due(f - 2):
            dve.wait_ge(acc_step.sem, acc_step.of(f - 2))
        DVE.tensor_tensor(scores[:, par], r(7), wide(rmax[:, 5, :]), ALU.mult).then_inc(score_ready.sem, 1)

    score_ready = sig("scores_ready")

    def pe_up(pe, g, par, e):
        if e == 0:
            pe.wait_ge(thi_ready.sem, thi_ready.of(g))
            pe.wait_ge(tlo_ready.sem, tlo_ready.of(g))
        for n in range(FB):
            k = e * FB + n
            bank = banks[k % 4]
            if k >= 4:
                pe.wait_ge(hid_ready.sem, hid_ready.of(g, k - 3))
            else:
                if due(g - 1):
                    pe.wait_ge(hid_ready.sem, hid_ready.of(g - 1, NE * FB + k - 3))
            w = slice(n * P, (n + 1) * P)
            PE.matmul(bank[:], w1hi[:, e, w], thi[:, par, :], start=True, stop=False)
            PE.matmul(bank[:], w1hi[:, e, w], tlo[:, par, :], start=False, stop=False)
            PE.matmul(bank[:], w1lo[:, e, w], thi[:, par, :], start=False, stop=True).then_inc(up_done.sem, 1)

    def act_hidden(act, g, e):
        for n in range(FB):
            k = e * FB + n
            act.wait_ge(up_done.sem, up_done.of(g, k + 1))
            if e > 1 or due(g - 1):
                act.wait_ge(down_done.sem, down_done.of(g, e - 1))
            SE.activation(hid[:, e % 2, n, :], banks[k % 4][:], ACT.Relu, bias=b1[:, k:k + 1]
                          ).then_inc(hid_ready.sem, 1)

    def pe_down(pe, g, e):
        bank = banks[4 + e % 2]
        if e > 1 or due(g - 1):
            pe.wait_ge(acc_step.sem, acc_step.of(g, (e - 1) * TG))
        PE.matmul(bank[:], ones3[:], b2p[:, e * D:(e + 1) * D].rearrange("p (o d) -> p o d", o=1).to_broadcast([P, TG, D]),
                  start=True, stop=False, skip_group_check=True)
        pe.wait_ge(hid_ready.sem, hid_ready.of(g, (e + 1) * FB))
        for i in range(TG):
            for n in range(FB):
                mm = PE.matmul(bank[:, col(i)], hid[:, e % 2, n, col(i)], w2[:, e, n, :], start=False,
                               stop=i == TG - 1 and n == FB - 1, skip_group_check=True)
        mm.then_inc(down_done.sem, 1)

    def dve_mix(dve, g, par, e):
        dve.wait_ge(down_done.sem, down_done.of(g, e + 1))
        if e == 0:
            dve.wait_ge(score_ready.sem, score_ready.of(g))
            if due(g - 2):
                dve.wait_ge(stats2.sem, stats2.of(g - 2))
                dve.wait_ge(out_ready.sem, out_ready.of(g - 2))
        for i in range(TG):
            y, s = banks[4 + e % 2][:, col(i)], scores[:, par, i, e:e + 1]
            if e == 0:
                ins = DVE.tensor_scalar(acc[:, par, i, :], y, s, None, ALU.mult)
            else:
                dve.wait_ge(acc_step.sem, acc_step.of(g, (e - 1) * TG + i + 1))
                ins = DVE.scalar_tensor_tensor(out=acc[:, par, i, :], in0=y, scalar=s, in1=acc[:, par, i, :],
                                               op0=ALU.mult, op1=ALU.add)
            ins.then_inc(acc_step.sem, 1)

    def dve_post1(dve, g, par):
        if due(g - 1):
            dve.wait_ge(post_pool.sem, post_pool.of(g - 1))
        for i in range(TG):
            dve.wait_ge(acc_step.sem, acc_step.of(g, (NE - 1) * TG + i + 1))
            DVE.bn_stats(pst6[:, i, :], acc[:, par, i, :]).then_inc(stats2.sem, 1)
        for i in range(TG):
            dve.wait_ge(stats2.sem, stats2.of(g, i + 1))
            apart(dve, g)
            DVE.bn_aggr(pmv[:, i, :], pst6[:, i, :]).then_inc(stats2.sem, 1)

    def pool_post(pl, g):
        pl.wait_ge(stats2.sem, stats2.of(g))
        if due(g - 1):
            pl.wait_ge(out_ready.sem, out_ready.of(g - 1))
        apart(pl, g)
        PL.tensor_scalar(post[:, 0, :], pmv[:, :, 1], LN_EPS, None, ALU.add).then_inc(post_pool.sem, 1)
        pl.wait_ge(post_pool.sem, post_pool.of(g, 1))
        apart(pl, g)
        PL.tensor_tensor(post[:, 1, :], post[:, 0, :], neghalf[:], ALU.pow).then_inc(post_pool.sem, 1)
        pl.wait_ge(post_pool.sem, post_pool.of(g, 2))
        apart(pl, g)
        PL.tensor_scalar(post[:, 2, :], pmv[:, :, 0], -1.0, None, ALU.mult).then_inc(post_pool.sem, 1)
        pl.wait_ge(post_pool.sem, post_pool.of(g, 3))
        apart(pl, g)
        PL.tensor_tensor(post[:, 3, :], post[:, 2, :], post[:, 1, :], ALU.mult).then_inc(post_pool.sem, 1)

    def dve_post2(dve, g, par, b, dyn):
        dve.wait_ge(post_pool.sem, post_pool.of(g))
        for i in range(TG):
            DVE.tensor_scalar(xb[:, i, :], tile(g, i, dyn), post[:, 3, i:i + 1], None,
                              ALU.add).then_inc(xb_ready.sem, 1)
        if not (isinstance(b, int) and b == 0):
            dve.wait_ge(stored[par], 1 + b * 16)
        for i in range(TG):
            dve.wait_ge(xb_ready.sem, xb_ready.of(g, i + 1))
            DVE.scalar_tensor_tensor(out=outb[:, par, i, :], in0=acc[:, par, i, :], scalar=post[:, 1, i:i + 1],
                                     in1=xb[:, i, :], op0=ALU.mult, op1=ALU.add).then_inc(out_ready.sem, 1)

    ov = out.rearrange("b (n p) d -> p (b n) d", p=P)

    def pe_body(pe, b, u, dyn, first, last):
        g, par = 2 * b + u, u
        for e in range(NE):
            pe_up(pe, g, par, e)
            if e:
                pe_down(pe, g, e - 1)
            elif not first:
                pe_down(pe, g - 1, NE - 1)
            if e == 2 and not last:
                pe_turn(pe, g + 1)
            if e == 4 and not last:
                pe_logits(pe, g + 1)

    def act_body(act, b, u, dyn, first, last):
        g, par = 2 * b + u, u
        for e in range(NE):
            act_hidden(act, g, e)
            if e == 2 and not last:
                act_turned(act, g + 1, 1 - par)
            if e == 5 and not last:
                act_exp(act, g + 1)

    def dve_body(dve, b, u, dyn, first, last):
        g, par = 2 * b + u, u
        if not last:
            dve_stats(dve, g + 1, dyn)
        for e in range(NE):
            if e:
                dve_mix(dve, g, par, e - 1)
            elif not first:
                dve_mix(dve, g - 1, 1 - par, NE - 1)
                dve_post1(dve, g - 1, 1 - par)
            if e == 1 and not last:
                dve_h(dve, g + 1, dyn)
            if e == 2 and not first:
                dve_post2(dve, g - 1, 1 - par, b if u else b - 1, dyn)
            if e == 3 and not last:
                dve_turned(dve, g + 1, 1 - par)
            if e == 5 and not last:
                dve_route_a(dve, g + 1)
            if e == 6 and not last:
                dve_route_b(dve, g + 1, 1 - par)

    def pool_body(pl, b, u, dyn, first, last):
        g = 2 * b + u
        if not last:
            pool_norm(pl, g + 1)
        if not first:
            pool_post(pl, g - 1)

    def over_groups(eng, body):
        for u in range(2):
            body(eng, 0, u, static, u == 0, False)
        with eng.Fori(1, GROUPS // 2 - 1) as b:
            for u in range(2):
                body(eng, b, u, dynamic, False, False)
        for u in range(2):
            body(eng, GROUPS // 2 - 1, u, static, False, u == 1)

    LAST = GROUPS - 1
    with nc.Block() as block:
        @block.sync
        def _(sp):
            sp.dma_start(w1f[:], w1_d.rearrange("e d h -> d e h")).then_inc(loaded, 16)
            sp.dma_start(wg[:], wg_d).then_inc(loaded, 16)
            sp.dma_start(b1row[:], b1_d.rearrange("e (n p) -> (e n) p", p=P)).then_inc(loaded, 16)
            sp.dma_start(b2row[:], b2_d.rearrange("(o e) d -> o (e d)", o=1)).then_inc(loaded, 16)
            sp.dma_start(w2[:], w2_d.rearrange("e (n p) d -> p e n d", p=P)).then_inc(loaded, 16)
            for u in range(2):
                sp.nop(nofuse=True).then_inc(stored[u], 1)
            with sp.Fori(0, GROUPS // 2) as b:
                for u in range(2):
                    g = 2 * b + u
                    sp.wait_ge(out_ready.sem, out_ready.of(g))
                    sp.dma_start(ov[:, bass.ds(g * TG, TG), :], outb[:, u, :, :]).then_inc(stored[u], 16)
            for u in range(2):
                sp.wait_ge(stored[u], 1 + 16 * GROUPS // 2)

        @block.tensor
        def _(pe):
            pe.wait_ge(loaded, LOADS)
            pe.wait_ge(const_step.sem, const_step.of(0, CONSTS))
            PE.transpose(banks[7][:, 0:NE * FB], b1row[:], ident[0:NE * FB, 0:NE * FB]).then_inc(prep_pe.sem, 1)
            pe.wait_ge(prep.sem, prep.of(0, PREP))
            pe_turn(pe, 0)
            pe_logits(pe, 0)
            over_groups(pe, pe_body)
            pe_down(pe, LAST, NE - 1)

        @block.scalar
        def _(act):
            act.wait_ge(prep.sem, prep.of(0, PREP))
            act_turned(act, 0, 0)
            act_exp(act, 0)
            over_groups(act, act_body)

        @block.vector
        def _(dve):
            dve_prepare(dve)
            dve_stats(dve, 0, static)
            dve_h(dve, 0, static)
            dve_turned(dve, 0, 0)
            dve_route_a(dve, 0)
            dve_route_b(dve, 0, 0)
            over_groups(dve, dve_body)
            dve_mix(dve, LAST, 1, NE - 1)
            dve_post1(dve, LAST, 1)
            dve_post2(dve, LAST, 1, GROUPS // 2 - 1, static)

        @block.gpsimd
        def _(pl):
            assert pool_constants(pl) == CONSTS
            pool_norm(pl, 0)
            over_groups(pl, pool_body)
            pool_post(pl, LAST)


_INS = ["L0_attn_hidden", "L0_attn_w_norm_in", "L0_attn_w_in_proj", "L0_attn_conv_w", "L0_attn_conv_b",
        "L0_attn_w_dt", "L0_attn_b_dt", "L0_attn_A_log", "L0_attn_D", "L0_attn_w_norm_out", "L0_attn_w_out_proj",
        "L0_ffn_Wg", "L0_ffn_W1", "L0_ffn_b1", "L0_ffn_W2", "L0_ffn_b2"]
_OUTS = [((BATCH, SEQ, D), "float32")]


def kernel(**inputs):
    import numpy as _np
    import concourse.bacc as _bacc
    from concourse import mybir as _mybir
    from concourse.bass_utils import run_bass_kernel_spmd as _run

    nc = _bacc.Bacc("TRN2", target_bir_lowering=False, num_devices=1)
    arrays, args = {}, []
    for name in _INS:
        a = _np.ascontiguousarray(inputs[name])
        arrays[f"in_{name}_dram"] = a
        args.append(nc.dram_tensor(f"in_{name}_dram", a.shape, _mybir.dt.from_np(a.dtype), kind="ExternalInput").ap())
    for i, (shape, dtype) in enumerate(_OUTS):
        dt = _mybir.dt.from_np(_np.dtype(dtype))
        args.append(nc.dram_tensor(f"out_{i}_dram", shape, dt, kind="ExternalOutput").ap())
    build(nc, *args)
    r = _run(nc, [arrays], core_ids=[0])
    return r.results[0]["out_0_dram"]
```

```python
from contextlib import ExitStack

import numpy as np
import concourse.bass as bass
from concourse import mybir

ALU = mybir.AluOpType
ACT = mybir.ActivationFunctionType
F32 = mybir.dt.float32
F32R = mybir.dt.float32r
BF16 = mybir.dt.bfloat16
AX = mybir.AxisListType.X

P = 128
BATCH, SEQ, D = 8, 1024, 128
TOK = BATCH * SEQ
TILES = TOK // P
TG = 4
GT = TG * P
GROUPS = TOK // GT
GB = SEQ // GT
DI, NH, HD, NS, KC = 256, 8, 32, 64, 4
NP = NH // 2
HH = NH // 2
SLOTS = 4
NB = DI // P
O_X, O_B, O_C, O_DT = DI, 2 * DI, 2 * DI + NH * NS, 2 * DI + 2 * NH * NS
PROJ = O_DT + NH
WCOLS = O_DT + DI
LN_EPS = 1e-5
RMS_EPS = float(np.finfo(np.float32).eps)
SILU_MIN = -44.0
EXP_MAX = float(np.exp(np.float32(-SILU_MIN)))
NE, FH = 8, 256
FB = FH // P
PARTS = 3


class Signal:

    def __init__(self, nc, name, per):
        self.sem, self.per = nc.alloc_semaphore(name), per

    def of(self, idx, k=None):
        return idx * self.per + (self.per if k is None else k)


def due(idx):
    return not isinstance(idx, int) or idx >= 0


def apart(eng, idx):
    if not isinstance(idx, int):
        eng.nop(nofuse=True)


class Part:
    pass


def build(nc, hidden, w_norm_in, w_in, conv_w, conv_b, w_dt, b_dt, a_log, d_skip, w_norm_out, w_out,
          wg, w1, b1, w2, b2, out):
    xall = nc.alloc_sbuf_tensor("xall", [P, TILES, D], F32)
    banks = [nc.alloc_psum_tensor(f"bank{i}", [P, 512], F32) for i in range(8)]
    with ExitStack() as front_buffers:
        att = attention(nc, front_buffers, xall, banks, hidden, w_norm_in, w_in, conv_w, conv_b, w_dt, b_dt, a_log,
                        d_skip, w_norm_out, w_out)
    with ExitStack() as expert_buffers:
        moe = experts(nc, expert_buffers, xall, banks, att, wg, w1, b1, w2, b2, out)

        with nc.Block() as block:
            @block.sync
            def _(sp):
                att.sync(sp)
                moe.sync(sp)

            @block.tensor
            def _(pe):
                att.tensor(pe, moe)
                moe.tensor(pe)

            @block.scalar
            def _(act):
                att.scalar(act, moe)
                moe.scalar(act)

            @block.vector
            def _(dve):
                att.vector(dve, moe)
                moe.vector(dve)

            @block.gpsimd
            def _(pl):
                att.gpsimd(pl, moe)
                moe.gpsimd(pl)


def static(a, n):
    return slice(a, a + n)


def dynamic(a, n):
    return bass.ds(a, n)


def col(i, w=P):
    return slice(i * w, (i + 1) * w)


def attention(nc, buffers, xall, banks, hidden, w_norm_in, w_in, conv_w, conv_b, w_dt, b_dt, a_log,
              d_skip, w_norm_out, w_out):
    def keep(name, shape, dt=F32):
        return nc.alloc_sbuf_tensor(name, shape, dt)

    def sb(name, shape, dt=F32):
        return buffers.enter_context(nc.sbuf_tensor(name, shape, dt))

    def sig(name, per=1):
        return Signal(nc, name, per)

    PE, DVE, SE, PL = nc.tensor, nc.vector, nc.scalar, nc.gpsimd

    ident = keep("ident", [P, P])
    ones = keep("ones", [P, P])
    zeros = keep("zeros", [P, 1])
    neghalf = keep("neghalf", [P, TG])
    rank = keep("rank", [P, TG, NE])
    sel_a = keep("sel_a", [P, NH], BF16)
    rows1 = keep("rows1", [P, NH, GT], BF16)
    sel_e = keep("sel_e", [P, NB, P], BF16)
    dcol = keep("dcol", [P, NB])
    wo = keep("wo", [P, NB, D])
    s1 = keep("ln1_scale", [P, TILES])
    nb1 = keep("ln1_shift", [P, TILES])
    parts = keep("parts", [P, 2, GT], BF16)

    edec = keep("edec", [P, 2, NB, P])
    tdec = keep("tdec", [P, 2, NP])
    m_flat = keep("m", [P, 2 * NH * P])
    mg_flat = keep("mg", [P, 2 * NH * P])
    m = m_flat[:].rearrange("p (b h l) -> p b h l", b=2, h=NH)
    mg = mg_flat[:].rearrange("p (b h l) -> p b h l", b=2, h=NH)
    btok = keep("btok", [P, 2, NP * P])
    xtok = keep("xtok", [P, 2, DI])
    xw = keep("xw", [P, 2, DI])
    state = keep("state", [P, 2, NP, HD])
    decayed = keep("decayed", [P, NP, HD])
    y1 = keep("y1", [P, NB, P])
    y2 = keep("y2", [P, NB, P])
    y4 = keep("y4", [P, 2, NB, P])
    ysq = keep("ysq", [P, 2, NB, P])
    ysum = keep("ysum", [P, 2, P])
    og = keep("og", [P, 2, TG, D + 2])
    pt = keep("pt", [P, 4, TG])
    ob = keep("ob", [P, TG, D])
    pst6 = keep("pst6", [P, TG, 6])
    pmv = keep("pmv", [P, TG, 2])

    bt1, ct1 = keep("bt1", [P, NP, GT]), keep("ct1", [P, NP, TG, 2, P])
    xt1, zt1 = keep("xt1", [P, NB, GT]), keep("zt1", [P, NB, GT])
    rows = [sb("rows0", [P, NH, GT], BF16), rows1]
    bt = [sb("bt0", [P, NP, GT]), bt1]
    ct = [sb("ct0", [P, NP, TG, 2, P]), ct1]
    xt = [sb("xt0", [P, NB, GT]), xt1]
    zt = [sb("zt0", [P, NB, GT]), zt1]
    h = sb("h", [P, 2, TG, D])
    st6 = sb("st6", [P, TG, 6])
    mv = sb("mv", [P, TG, 2])
    lnt = sb("lnt", [P, 6, TG])
    thi = sb("thi", [P, GT], F32R)
    tlo = sb("tlo", [P, GT], F32R)
    dtv = sb("dtv", [P, NB, GT])
    dta = sb("dta", [P, NB, GT])
    cs = sb("cs", [NH, GT])
    mid = sb("mid", [NH, GT], BF16)
    xraw = sb("xraw", [P, 2, NB, KC - 1 + GT])
    xsig = sb("xsig", [P, NB, GT])
    zsig = sb("zsig", [P, NB, GT])

    wraw, wf = m_flat[:, 0:PROJ], mg_flat[:, 0:WCOLS]
    wdt_rows, wdt_in_t = m_flat[0:NH, PROJ:PROJ + DI], m_flat[0:NH, PROJ + DI:PROJ + DI + P]
    wo_raw = mg_flat[:, WCOLS:WCOLS + NB * D].rearrange("p (n d) -> p n d", n=NB)
    hsum = sb("hsum", [P, NB, NH])
    whi = sb("whi", [P, WCOLS], F32R)
    wlo = sb("wlo", [P, WCOLS], F32R)
    wn_in = sb("wn_in", [P, 1])
    cw = sb("cw", [P, NB, KC])
    cb = sb("cb", [P, NB])
    bdt = sb("bdt", [P, NB])
    alog = sb("alog", [NH, 1])
    ascale = sb("ascale", [NH, 1])
    wn_out = sb("wn_out", [P, NB])

    loaded0 = nc.alloc_semaphore("x_first_group_loaded")
    loaded_second = nc.alloc_semaphore("x_second_group_loaded")
    loaded1 = nc.alloc_semaphore("x_other_groups_loaded")
    w_loaded = nc.alloc_semaphore("projection_loaded")
    v_loaded = nc.alloc_semaphore("other_weights_loaded")
    const_step = sig("pool_constants_built", 1)
    prep = sig("dve_weights_prepared", 1)
    prep_pe = sig("pe_dt_weights_made", 1)
    prep_act = sig("act_weights_prepared", 1)
    cleared = sig("buffers_cleared", 1)

    ln_stats = sig("ln_stats_ready", 2 * TG)
    coef_step = sig("ln1_coefficient_steps", 10)
    h_ready = sig("h_ready", TG)
    fr_done = sig("front_products_done", 16)
    thi_ready = sig("thi_ready")
    tlo_ready = sig("tlo_ready")
    dtv_ready = sig("dtv_ready", NB)
    dta_ready = sig("softplus_tail_ready", 4)
    dtr_ready = sig("softplus_ready")
    scan_ready = sig("log_decay_scanned", TG)
    rows_ready = [nc.alloc_semaphore(f"log_decay_rows_ready{u}") for u in range(2)]
    part_ready = sig("log_decay_parts_ready", 5)
    xraw_ready = sig("xraw_ready", NB)
    hist_ready = sig("conv_history_ready")
    conv_step = sig("conv_steps", NB * KC + 1)
    xsig_step = sig("x_sigmoid_steps", 3)
    xt_ready = sig("xt_ready")
    bt_ready = sig("bt_ready", NP)
    cta_ready = sig("c_by_act_ready", 6)
    ctd_ready = sig("c_by_dve_ready", 2)
    zsig_step = sig("z_sigmoid_steps", 3)
    zheld = sig("z_held")
    z_ready = sig("z_ready", NB)
    zt_ready = sig("zt_ready")

    btr_done = sig("b_turned")
    xtr_done = sig("x_turned")
    dd_done = sig("log_decays_done", 2)
    gg_done = sig("scores_done", 2)
    ee_done = sig("decay_rows_done")
    oo_done = sig("out_projected")
    yy_done = sig("y_products_done")
    ss_done = sig("state_products_done")
    e_ready = sig("decay_rows_ready", 3)
    m_ready = sig("decays_ready", 2)
    btok_ready = sig("btok_ready")
    xtok_ready = sig("xtok_ready")
    ysq_ready = sig("ysq_ready")
    ysum_ready = sig("y_squares_summed")
    og_ready = sig("og_ready")
    mm_ready = sig("decays_masked", 2)
    xw_ready = sig("xw_ready", 2)
    dec_ready = sig("state_decayed")
    y4_ready = sig("y_gated")
    mg_ready = sig("scores_decayed", 2)
    state_ready = sig("state_ready", 2)
    y_step = sig("y_steps", 4)
    post_pool1 = sig("post_rms", 2)
    xn_ready = sig("xn_ready", TG)
    post_dve1 = sig("post_stats", 3 * TG)
    post_pool2 = sig("post_ln2", 2)
    centred = sig("post_centred", TG)
    x2_ready = sig("x2_ready", TG)

    def fr_uses(f, g):
        products = [("h", tlo_ready, 1), ("dt0", dtv_ready, 1), ("dt1", dtv_ready, 2), ("x0", xraw_ready, 1),
                    ("x1", xraw_ready, 2), ("b0", bt_ready, 1), ("b1", bt_ready, 2), ("b2", bt_ready, 3),
                    ("b3", bt_ready, 4), ("a", scan_ready, TG), ("z0", z_ready, 1), ("z1", z_ready, 2),
                    ("c0", cta_ready, 2), ("c1", ctd_ready, 2), ("c2", cta_ready, 4), ("c3", cta_ready, 6)]
        seq = []
        for n, (key, s, k) in enumerate(products):
            if g is not None and n % SLOTS == SLOTS // 2:
                seq.append((("xtr", n // SLOTS), xtok_ready, g * TG + n // SLOTS, 1))
            seq.append(((key,), s, f, k) if f is not None else None)
        return seq

    FRONT = [["h", "dt0", "dt1", "x0"], ["x1", "b0", "b1", "b2"], ["b3", "a", "z0", "z1"], ["c0", "c1", "c2", "c3"]]
    BLOCK = {"dt0": O_DT, "dt1": O_DT + P, "x0": O_X, "x1": O_X + P, "z0": 0, "z1": P}
    BLOCK.update({f"b{j}": O_B + j * P for j in range(NP)})
    BLOCK.update({f"c{j}": O_C + j * P for j in range(NP)})
    FR_INDEX = {k: n for n, k in enumerate(sum(FRONT, []))}

    class Front:

        def __init__(self, g, f, before):
            self.seq, self.before = fr_uses(f, g), before
            self.at = {u[0]: n for n, u in enumerate(self.seq) if u}

        def bank(self, *key):
            return banks[self.at[key] % 2]

        def free(self, eng, *key):
            both = self.before + self.seq
            n = len(self.before) + self.at[key] - 2
            while n >= 0 and both[n] is None:
                n -= 2
            if n >= 0:
                _, s, idx, k = both[n]
                eng.wait_ge(s.sem, s.of(idx, k))

    def load_all(sp):
        small = dict(allow_slow_non_contiguous=True)
        v = hidden.rearrange("b (n p) d -> p (b n) d", p=P)
        first = 2 * TG
        cvec = lambda a: a.rearrange("(n p) -> p n", p=P)
        sp.dma_start(xall[:, 0:TG, :], v[:, 0:TG, :]).then_inc(loaded0, 16)
        sp.dma_start(wraw, w_in).then_inc(w_loaded, 16)
        sp.dma_start(wn_in[:], cvec(w_norm_in), **small).then_inc(w_loaded, 16)
        sp.dma_start(wdt_rows, w_dt).then_inc(w_loaded, 16)
        sp.dma_start(xall[:, TG:first, :], v[:, TG:first, :]).then_inc(loaded_second, 16)
        sp.dma_start(bdt[:], cvec(b_dt), **small).then_inc(v_loaded, 16)
        sp.dma_start(cw[:], conv_w.rearrange("(n p) o k -> p n (o k)", p=P)).then_inc(v_loaded, 16)
        sp.dma_start(cb[:], cvec(conv_b), **small).then_inc(v_loaded, 16)
        sp.dma_start(alog[:], a_log.rearrange("(h o) -> h o", o=1), **small).then_inc(v_loaded, 16)
        sp.dma_start(wn_out[:], cvec(w_norm_out), **small).then_inc(v_loaded, 16)
        sp.dma_start(wo_raw, w_out.rearrange("(n p) d -> p n d", p=P)).then_inc(v_loaded, 16)
        for n in range(NB):
            for q in range(P // HD):
                hh = n * (P // HD) + q
                sp.dma_start(dcol[q * HD:(q + 1) * HD, n:n + 1],
                             d_skip[hh:hh + 1].rearrange("(h o) -> h o", o=1).to_broadcast([HD, 1]), **small
                             ).then_inc(v_loaded, 16)
        sp.dma_start(xall[:, first:TILES, :], v[:, first:TILES, :]).then_inc(loaded1, 16)

    W_LOADS = 3 * 16
    V_LOADS = (6 + NH) * 16

    CONST_IDENT = 3

    def pool_identity(pl):
        PL.memset(neghalf[:], -0.5).then_inc(const_step.sem, 1)
        PL.memset(ident[:], 0.0).then_inc(const_step.sem, 1)
        pl.wait_ge(const_step.sem, 2)
        PL.affine_select(out=ident[:], in_=ident[:], compare_op=ALU.not_equal, fill=1.0, base=0,
                         pattern=[[-1, P]], channel_multiplier=1).then_inc(const_step.sem, 1)
        pl.wait_ge(const_step.sem, CONST_IDENT)

    def pool_selectors(pl):
        PL.memset(sel_a[:], 0.0).then_inc(const_step.sem, 1)
        done = CONST_IDENT + 1
        for k in range(PARTS):
            pl.wait_ge(const_step.sem, done)
            PL.affine_select(out=sel_a[:], in_=sel_a[:], compare_op=ALU.not_equal, fill=1.0, base=-32 * k,
                             pattern=[[-1, NH]], channel_multiplier=1).then_inc(const_step.sem, 1)
            done += 1
        assert done == CONST_HEADS
        for buf in (hsum, sel_e, parts):
            PL.memset(buf[:], 0.0).then_inc(const_step.sem, 1)
            done += 1
        pl.wait_ge(const_step.sem, done)
        for n in range(NB):
            for q in range(P // HD):
                PL.memset(hsum[q * HD:(q + 1) * HD, n, n * 4 + q:n * 4 + q + 1], 1.0).then_inc(const_step.sem, 1)
                done += 1
        for k in range(PARTS):
            pl.wait_ge(const_step.sem, done)
            PL.affine_select(out=parts[:], in_=parts[:], compare_op=ALU.not_equal, fill=1.0, base=-32 * k - NH,
                             pattern=[[0, 2], [0, GT]], channel_multiplier=1).then_inc(const_step.sem, 1)
            for n in range(NB):
                v = sel_e[:, n, :].rearrange("p (q d) -> p q d", d=HD)
                PL.affine_select(out=v, in_=v, compare_op=ALU.not_equal, fill=1.0, base=-32 * k - 4 * n,
                                 pattern=[[-1, P // HD], [0, HD]], channel_multiplier=1).then_inc(const_step.sem, 1)
            done += 1 + NB
        assert done == CONSTS

    CONST_HEADS = CONST_IDENT + 1 + PARTS
    CONSTS = CONST_HEADS + 3 + NB * 4 + PARTS * (1 + NB)
    CLEARED = 2
    ALL_CONSTS = CONSTS + 3

    def dve_clear(dve):
        DVE.memset(ones[:], 1.0).then_inc(cleared.sem, 1)
        DVE.memset(state[:], 0.0).then_inc(cleared.sem, 1)

    def dve_row_constants(dve, u):
        dve.wait_ge(const_step.sem, CONST_HEADS)
        heads = sel_a[:].rearrange("p (h o) -> p h o", o=1).to_broadcast([P, NH, GT])
        DVE.tensor_scalar(rows[u][:], heads, -1.0, None, ALU.mult).then_inc(cleared.sem, 1)

    def pool_clear(pl):
        PL.memset(ct[1][:], 0.0).then_inc(const_step.sem, 1)
        PL.memset(og[:], 0.0).then_inc(const_step.sem, 1)

    PREP_PROJ = 5
    PREP = PREP_PROJ + NB + 1

    def dve_prepare(dve):
        dve.wait_ge(w_loaded, W_LOADS)
        DVE.tensor_scalar(wf[:, 0:O_DT], wraw[:, 0:O_DT], wn_in[:, 0:1], None, ALU.mult).then_inc(prep.sem, 1)
        dve.wait_ge(prep_pe.sem, 1)
        DVE.tensor_copy(wdt_in_t, banks[7][0:NH, 0:P]).then_inc(prep.sem, 1)
        dve.wait_ge(prep_act.sem, 1)
        DVE.tensor_tensor(wlo[:, 0:O_DT], wf[:, 0:O_DT], whi[:, 0:O_DT].bitcast(F32), ALU.subtract
                          ).then_inc(prep.sem, 1)
        dve.wait_ge(prep_pe.sem, 2)
        DVE.tensor_scalar(wf[:, O_DT:WCOLS], banks[6][:, 0:DI], wn_in[:, 0:1], None, ALU.mult
                          ).then_inc(prep.sem, 1)
        dve.wait_ge(prep_act.sem, 2)
        DVE.tensor_tensor(wlo[:, O_DT:WCOLS], wf[:, O_DT:WCOLS], whi[:, O_DT:WCOLS].bitcast(F32), ALU.subtract
                          ).then_inc(prep.sem, 1)

    def dve_prepare_small(dve):
        dve.wait_ge(v_loaded, V_LOADS)
        for n in range(NB):
            DVE.tensor_scalar(wo[:, n, :], wo_raw[:, n, :], wn_out[:, n:n + 1], None, ALU.mult
                              ).then_inc(prep.sem, 1)
        dve.wait_ge(prep_act.sem, 3)
        DVE.tensor_scalar(ascale[:], alog[:], -1.0 / HD, None, ALU.mult).then_inc(prep.sem, 1)

    def pe_prepare(pe):
        pe.wait_ge(const_step.sem, CONST_IDENT)
        pe.wait_ge(w_loaded, W_LOADS)
        PE.transpose(banks[7][0:NH, 0:P], wraw[:, O_DT:PROJ], ident[:]).then_inc(prep_pe.sem, 1)
        pe.wait_ge(prep.sem, 2)
        PE.matmul(banks[6][:, 0:DI], wdt_in_t, wdt_rows, start=True, stop=True).then_inc(prep_pe.sem, 1)

    def act_prepare(act):
        act.wait_ge(prep.sem, 1)
        SE.activation(whi[:, 0:O_DT], wf[:, 0:O_DT], ACT.Copy).then_inc(prep_act.sem, 1)
        act.wait_ge(loaded0, 16)
        act_h(act, 0, 0, static)
        act.wait_ge(prep.sem, 4)
        SE.activation(whi[:, O_DT:WCOLS], wf[:, O_DT:WCOLS], ACT.Copy).then_inc(prep_act.sem, 1)
        act.wait_ge(v_loaded, V_LOADS)
        SE.activation(alog[:], alog[:], ACT.Exp).then_inc(prep_act.sem, 1)

    def dve_stats(dve, f, dyn):
        xg = lambda i: xall[:, dyn(f * TG + i, 1), :].rearrange("p o d -> p (o d)")
        if due(f - 1):
            dve.wait_ge(coef_step.sem, coef_step.of(f - 1))
        for i in range(TG):
            DVE.bn_stats(st6[:, i, :], xg(i)).then_inc(ln_stats.sem, 1)
        for i in range(TG):
            dve.wait_ge(ln_stats.sem, ln_stats.of(f, i + 1))
            apart(dve, f)
            DVE.bn_aggr(mv[:, i, :], st6[:, i, :]).then_inc(ln_stats.sem, 1)

    def pool_norm(pl, f, dyn):
        mean, var = mv[:, :, 0], mv[:, :, 1]
        rs, ns = s1[:, dyn(f * TG, TG)], nb1[:, dyn(f * TG, TG)]
        pl.wait_ge(ln_stats.sem, ln_stats.of(f))
        if due(f - 1):
            pl.wait_ge(h_ready.sem, h_ready.of(f - 1))
        apart(pl, f)
        PL.tensor_scalar(lnt[:, 0, :], var, LN_EPS, None, ALU.add).then_inc(coef_step.sem, 1)
        pl.wait_ge(coef_step.sem, coef_step.of(f, 1))
        apart(pl, f)
        PL.tensor_tensor(rs, lnt[:, 0, :], neghalf[:], ALU.pow).then_inc(coef_step.sem, 1)
        pl.wait_ge(coef_step.sem, coef_step.of(f, 2))
        apart(pl, f)
        PL.tensor_tensor(lnt[:, 1, :], rs, rs, ALU.mult).then_inc(coef_step.sem, 1)
        pl.wait_ge(coef_step.sem, coef_step.of(f, 3))
        apart(pl, f)
        PL.tensor_tensor(lnt[:, 2, :], lnt[:, 1, :], var, ALU.mult).then_inc(coef_step.sem, 1)
        pl.wait_ge(coef_step.sem, coef_step.of(f, 4))
        apart(pl, f)
        PL.tensor_scalar(lnt[:, 3, :], lnt[:, 2, :], RMS_EPS, None, ALU.add).then_inc(coef_step.sem, 1)
        pl.wait_ge(coef_step.sem, coef_step.of(f, 5))
        apart(pl, f)
        PL.tensor_tensor(lnt[:, 4, :], lnt[:, 3, :], neghalf[:], ALU.pow).then_inc(coef_step.sem, 1)
        pl.wait_ge(coef_step.sem, coef_step.of(f, 6))
        apart(pl, f)
        PL.tensor_tensor(lnt[:, 0, :], lnt[:, 4, :], rs, ALU.mult).then_inc(coef_step.sem, 1)
        pl.wait_ge(coef_step.sem, coef_step.of(f, 7))
        apart(pl, f)
        PL.tensor_scalar(lnt[:, 5, :], mean, -1.0, None, ALU.mult).then_inc(coef_step.sem, 1)
        pl.wait_ge(coef_step.sem, coef_step.of(f, 8))
        apart(pl, f)
        PL.tensor_tensor(ns, lnt[:, 5, :], rs, ALU.mult).then_inc(coef_step.sem, 1)
        pl.wait_ge(coef_step.sem, coef_step.of(f, 9))
        apart(pl, f)
        PL.tensor_tensor(lnt[:, 1, :], lnt[:, 5, :], lnt[:, 0, :], ALU.mult).then_inc(coef_step.sem, 1)

    def act_h(act, f, par, dyn):
        act.wait_ge(coef_step.sem, coef_step.of(f))
        if due(f - 2):
            act.wait_ge(fr_done.sem, fr_done.of(f - 2, 1))
        for i in range(TG):
            x = xall[:, dyn(f * TG + i, 1), :].rearrange("p o d -> p (o d)")
            SE.activation(h[:, par, i, :], x, ACT.Identity, scale=lnt[:, 0, i:i + 1], bias=lnt[:, 1, i:i + 1]
                          ).then_inc(h_ready.sem, 1)

    def pe_front(pe, f, par, fr, i, slot):
        key = FRONT[i][slot]
        bank = fr.bank(key)
        fr.free(pe, key)
        if key == "h":
            pe.wait_ge(h_ready.sem, h_ready.of(f))
            for i in range(TG):
                mm = PE.transpose(bank[:, col(i)], h[:, par, i, :], ident[:])
        elif key == "a":
            if isinstance(f, int) and f == 0:
                pe.wait_ge(const_step.sem, CONSTS)
            pe.wait_ge(dtr_ready.sem, dtr_ready.of(f))
            for n in range(NB):
                mm = PE.matmul(bank[0:NH, :], hsum[:, n, :], dtv[:, n, :], start=n == 0, stop=n == NB - 1)
        else:
            if key == "dt0":
                pe.wait_ge(thi_ready.sem, thi_ready.of(f))
                pe.wait_ge(tlo_ready.sem, tlo_ready.of(f))
                if isinstance(f, int) and f == 0:
                    pe.wait_ge(prep.sem, PREP_PROJ)
            w = slice(BLOCK[key], BLOCK[key] + P)
            PE.matmul(bank[:], whi[:, w], thi[:], start=True, stop=False)
            PE.matmul(bank[:], whi[:, w], tlo[:], start=False, stop=False)
            mm = PE.matmul(bank[:], wlo[:, w], thi[:], start=False, stop=True)
        mm.then_inc(fr_done.sem, 1)

    def fdone(f, key):
        return fr_done.of(f, FR_INDEX[key] + 1)

    def act_front(act, f, par, fr, i, slot):
        key = FRONT[i][slot]
        if key == "h":
            act.wait_ge(fr_done.sem, fdone(f, "h"))
            if due(f - 1):
                act.wait_ge(fr_done.sem, fr_done.of(f - 1, 16))
            SE.activation(thi[:], fr.bank("h")[:], ACT.Copy).then_inc(thi_ready.sem, 1)
        if key in ("dt0", "dt1"):
            n = int(key[2])
            act.wait_ge(fr_done.sem, fdone(f, key))
            if n == 0 and due(f - 1):
                act.wait_ge(dtr_ready.sem, dtr_ready.of(f - 1))
            SE.activation(dta[:, n, :], fr.bank(key)[:], ACT.Abs, bias=bdt[:, n:n + 1]).then_inc(dta_ready.sem, 1)
        if key in ("x0", "x1"):
            n = int(key[1])
            act.wait_ge(fr_done.sem, fdone(f, key))
            if n == 0:
                if due(f - 1):
                    act.wait_ge(hist_ready.sem, hist_ready.of(f - 1))
                if due(f - 2):
                    act.wait_ge(conv_step.sem, conv_step.of(f - 2))
            SE.activation(xraw[:, par, n, KC - 1:], fr.bank(key)[:], ACT.Copy).then_inc(xraw_ready.sem, 1)
            act.wait_ge(dta_ready.sem, dta_ready.of(f, 2 + n))
            if n == 0:
                SE.activation(dta[:], dta[:], ACT.Exp, scale=-1.0).then_inc(dta_ready.sem, 1)
            else:
                SE.activation(dta[:], dta[:], ACT.Ln, bias=1.0).then_inc(dta_ready.sem, 1)
        if key in ("b0", "b1", "b2", "b3"):
            j = int(key[1])
            act.wait_ge(fr_done.sem, fdone(f, key))
            if j == 0 and due(f - 2):
                act.wait_ge(btr_done.sem, btr_done.of((f - 2) * TG + TG - 1))
                act.wait_ge(gg_done.sem, gg_done.of((f - 2) * TG + TG - 1))
            SE.activation(bt[par][:, j, :], fr.bank(key)[:], ACT.Copy).then_inc(bt_ready.sem, 1)
        if key in ("c0", "c2", "c3"):
            act.wait_ge(fr_done.sem, fdone(f, key))
            if key == "c0" and isinstance(f, int) and f == 0:
                act.wait_ge(const_step.sem, CONSTS + 1)
            if key == "c0" and due(f - 2):
                act.wait_ge(yy_done.sem, yy_done.of((f - 2) * TG + TG - 1))
            split_c(SE.copy, int(key[1]), par, fr, cta_ready)
        if key in ("z0", "z1"):
            n = int(key[1])
            act.wait_ge(fr_done.sem, fdone(f, key))
            if n == 0 and due(f - 2):
                act.wait_ge(y4_ready.sem, y4_ready.of((f - 2) * TG + TG - 1))
            SE.activation(zt[par][:, n, :], fr.bank(key)[:], ACT.Copy).then_inc(z_ready.sem, 1)

    def act_x_sigmoid(act, f, par, step):
        if step == 0:
            act.wait_ge(conv_step.sem, conv_step.of(f))
            if due(f - 1):
                act.wait_ge(xt_ready.sem, xt_ready.of(f - 1))
            SE.activation(xsig[:], xt[par][:], ACT.Exp, scale=-1.0).then_inc(xsig_step.sem, 1)
        if step == 1:
            act.wait_ge(xsig_step.sem, xsig_step.of(f, 1))
            SE.activation(xsig[:], xsig[:], ACT.Ln, bias=1.0).then_inc(xsig_step.sem, 1)
        if step == 2:
            act.wait_ge(xsig_step.sem, xsig_step.of(f, 2))
            SE.activation(xsig[:], xsig[:], ACT.Exp, scale=-1.0).then_inc(xsig_step.sem, 1)

    def act_z_sigmoid(act, f, par, step):
        if step == 0:
            act.wait_ge(z_ready.sem, z_ready.of(f))
            if due(f - 1):
                act.wait_ge(zt_ready.sem, zt_ready.of(f - 1))
            SE.activation(zsig[:], zt[par][:], ACT.Exp, scale=-1.0).then_inc(zsig_step.sem, 1)
        if step == 1:
            act.wait_ge(zheld.sem, zheld.of(f))
            SE.activation(zsig[:], zsig[:], ACT.Ln, bias=1.0).then_inc(zsig_step.sem, 1)
        if step == 2:
            act.wait_ge(zsig_step.sem, zsig_step.of(f, 2))
            SE.activation(zsig[:], zsig[:], ACT.Exp, scale=-1.0).then_inc(zsig_step.sem, 1)

    def split_c(copy, j, par, fr, ready):
        for q in range(2):
            rows = slice(q * NS, (q + 1) * NS)
            copy(ct[par][rows, j, :, q, :], fr.bank(f"c{j}")[rows, :].rearrange("p (t l) -> p t l", l=P)
                 ).then_inc(ready.sem, 1)

    def dve_conv(dve, f, par, taps):
        for k in taps:
            for n in range(NB):
                dve.wait_ge(xraw_ready.sem, xraw_ready.of(f, n + 1))
                src = xraw[:, par, n, k:k + GT]
                if k == 0:
                    DVE.tensor_scalar(xt[par][:, n, :], src, cw[:, n, 0:1], cb[:, n:n + 1], ALU.mult, ALU.add
                                      ).then_inc(conv_step.sem, 1)
                else:
                    dve.wait_ge(conv_step.sem, conv_step.of(f, (k - 1) * NB + n + 1))
                    DVE.scalar_tensor_tensor(out=xt[par][:, n, :], in0=src, scalar=cw[:, n, k:k + 1],
                                             in1=xt[par][:, n, :], op0=ALU.mult, op1=ALU.add
                                             ).then_inc(conv_step.sem, 1)

    def dve_front(dve, f, par, fr, i, slot):
        key = FRONT[i][slot]
        pr = lambda k: parts[32 * k:32 * k + NH, par, :]
        if key == "h":
            dve.wait_ge(thi_ready.sem, thi_ready.of(f))
            if due(f - 1):
                dve.wait_ge(fr_done.sem, fr_done.of(f - 1, 16))
            DVE.tensor_tensor(tlo[:], fr.bank("h")[:], thi[:].bitcast(F32), ALU.subtract).then_inc(tlo_ready.sem, 1)
        if key in ("dt0", "dt1"):
            n = int(key[2])
            dve.wait_ge(dta_ready.sem, dta_ready.of(f, n + 1))
            if n == 0 and due(f - 1):
                dve.wait_ge(fr_done.sem, fdone(f - 1, "a"))
            DVE.tensor_scalar(dtv[:, n, :], fr.bank(key)[:], bdt[:, n:n + 1], 0.0, ALU.add, ALU.max
                              ).then_inc(dtv_ready.sem, 1)
        if key == "x1":
            dve.wait_ge(hist_ready.sem, hist_ready.of(f))
            if isinstance(f, int) and f == 0:
                dve.wait_ge(prep.sem, PREP)
            if due(f - 2):
                dve.wait_ge(y_step.sem, y_step.of((f - 2) * TG + TG - 1))
            dve_conv(dve, f, par, range(0, KC // 2))
        if key == "b1":
            dve_conv(dve, f, par, range(KC // 2, KC))
            dve.wait_ge(conv_step.sem, conv_step.of(f, NB * KC))
            DVE.tensor_scalar(xt[par][:], xt[par][:], SILU_MIN, None, ALU.max).then_inc(conv_step.sem, 1)
        if key == "a":
            dve.wait_ge(fr_done.sem, fdone(f, "a"))
            if due(f - 1):
                dve.wait_ge(part_ready.sem, part_ready.of(f - 1))
            for i in range(TG):
                DVE.tensor_tensor_scan(cs[:, col(i)], ones[0:NH, :], fr.bank("a")[0:NH, col(i)], 0.0,
                                       ALU.mult, ALU.add).then_inc(scan_ready.sem, 1)
        if key == "z0":
            if isinstance(f, int) and f == 0:
                dve.wait_ge(const_step.sem, CONSTS)
            dve.wait_ge(scan_ready.sem, scan_ready.of(f))
            if due(f - 2):
                dve.wait_ge(ee_done.sem, ee_done.of((f - 2) * TG + TG - 1))
            DVE.tensor_scalar(pr(0), cs[:], ascale[:, 0:1], None, ALU.mult).then_inc(part_ready.sem, 1)
            dve.wait_ge(part_ready.sem, part_ready.of(f, 1))
            DVE.scalar_tensor_tensor(out=cs[:], in0=cs[:], scalar=ascale[:, 0:1], in1=pr(0),
                                     op0=ALU.mult, op1=ALU.subtract).then_inc(part_ready.sem, 1)
        if key == "c1":
            dve.wait_ge(fr_done.sem, fdone(f, "c1"))
            if isinstance(f, int) and f == 0:
                dve.wait_ge(const_step.sem, CONSTS + 1)
            if due(f - 2):
                dve.wait_ge(yy_done.sem, yy_done.of((f - 2) * TG + TG - 1))
            split_c(DVE.tensor_copy, 1, par, fr, ctd_ready)
        if key == "c0":
            dve.wait_ge(zsig_step.sem, zsig_step.of(f, 1))
            DVE.tensor_scalar(zsig[:], zsig[:], EXP_MAX, None, ALU.min).then_inc(zheld.sem, 1)
            dve.wait_ge(part_ready.sem, part_ready.of(f, 2))
            DVE.tensor_copy(mid[:], cs[:]).then_inc(part_ready.sem, 1)
            DVE.tensor_copy(pr(1), cs[:]).then_inc(part_ready.sem, 1)
            dve.wait_ge(part_ready.sem, part_ready.of(f, 3))
            DVE.tensor_tensor(pr(2), cs[:], mid[:], ALU.subtract).then_inc(part_ready.sem, 1)
        if key == "c3":
            dve.wait_ge(xsig_step.sem, xsig_step.of(f))
            DVE.tensor_tensor(xt[par][:], xsig[:], xt[par][:], ALU.mult).then_inc(xt_ready.sem, 1)

    def pool_silu_z(pl, g, par):
        pl.wait_ge(zsig_step.sem, zsig_step.of(g))
        apart(pl, g)
        PL.tensor_tensor(zt[par][:], zsig[:], zt[par][:], ALU.mult).then_inc(zt_ready.sem, 1)

    def pool_history(pl, f, par, first_of_batch):
        if due(f - 2):
            pl.wait_ge(conv_step.sem, conv_step.of(f - 2))
        if first_of_batch:
            apart(pl, f)
            PL.memset(xraw[:, par, :, 0:KC - 1], 0.0).then_inc(hist_ready.sem, 1)
        else:
            if due(f - 1):
                pl.wait_ge(xraw_ready.sem, xraw_ready.of(f - 1))
            apart(pl, f)
            PL.tensor_copy(xraw[:, par, :, 0:KC - 1], xraw[:, 1 - par, :, GT:GT + KC - 1]
                           ).then_inc(hist_ready.sem, 1)

    def pool_softplus(pl, f):
        pl.wait_ge(dta_ready.sem, dta_ready.of(f))
        pl.wait_ge(dtv_ready.sem, dtv_ready.of(f))
        apart(pl, f)
        PL.tensor_tensor(dtv[:], dtv[:], dta[:], ALU.add).then_inc(dtr_ready.sem, 1)

    def pe_decays(pe, t, i, g, par, seq):
        c = col(i)
        if i == 0:
            pe.wait_ge(part_ready.sem, part_ready.of(g))
            pe.wait_ge(rows_ready[par], 16 * PARTS * (seq + 1))
        for hf in range(2):
            if due(t - 1):
                pe.wait_ge(m_ready.sem, m_ready.of(t - 1, hf + 1))
            PE.matmul(banks[2 + hf][:], parts[:, par, c], rows[par][:, hf * HH:(hf + 1) * HH, c], start=True,
                      stop=True).then_inc(dd_done.sem, 1)

    def pe_scores(pe, t, i, g, par, hf):
        if i == 0 and hf == 0:
            pe.wait_ge(bt_ready.sem, bt_ready.of(g))
            pe.wait_ge(cta_ready.sem, cta_ready.of(g))
            pe.wait_ge(ctd_ready.sem, ctd_ready.of(g))
        bank = banks[4 + hf]
        if due(t - 1):
            pe.wait_ge(mg_ready.sem, mg_ready.of(t - 1, hf + 1))
        for j in range(2):
            mm = PE.matmul(bank[:, col(j, 2 * P)], bt[par][:, 2 * hf + j, col(i)],
                           ct[par][:, 2 * hf + j, i, :, :], start=True, stop=True)
        mm.then_inc(gg_done.sem, 1)

    def pe_turns(pe, t, i, g, par, fr):
        c = col(i)
        if i == 0:
            pe.wait_ge(xt_ready.sem, xt_ready.of(g))
        fr.free(pe, "xtr", i)
        for n in range(NB):
            mm = PE.transpose(fr.bank("xtr", i)[:, col(n)], xt[par][:, n, c], ident[:])
        mm.then_inc(xtr_done.sem, 1)
        if due(t - 1):
            pe.wait_ge(state_ready.sem, state_ready.of(t - 1))
        for j in range(NP):
            mm = PE.transpose(banks[7][:, col(j)], bt[par][:, j, c], ident[:])
        mm.then_inc(btr_done.sem, 1)
        if due(t - 1):
            pe.wait_ge(y_step.sem, y_step.of(t - 1, 3))
        for n in range(NB):
            PE.matmul(banks[6][:, col(n)], sel_e[:, n, :], parts[:, par, c], start=True, stop=True,
                      skip_group_check=True)
        last = parts[:, par, i * P + P - 1:i * P + P]
        PE.matmul(banks[6][:, DI:DI + NH], last.to_broadcast([P, P]), sel_a[:], start=True, stop=True,
                  skip_group_check=True).then_inc(ee_done.sem, 1)

    def pe_out_tile(pe, t, tp, last=False):
        pe.wait_ge(y4_ready.sem, y4_ready.of(t))
        pe.wait_ge(ysum_ready.sem, ysum_ready.of(t))
        if last:
            pe.wait_ge(state_ready.sem, state_ready.of(t))
        else:
            pe.wait_ge(btok_ready.sem, btok_ready.of(t + 1))
        bank = banks[7]
        for n in range(NB):
            PE.matmul(bank[:, 0:D], y4[:, tp, n, :], wo[:, n, :], start=n == 0, stop=n == NB - 1)
        PE.matmul(bank[:, D:2 * D], ysum[:, tp, :], ones[:], start=True, stop=True).then_inc(oo_done.sem, 1)

    def pe_y(pe, t, i, g, par, tp, first_tile):
        pe.wait_ge(xtok_ready.sem, xtok_ready.of(t))
        pe.wait_ge(e_ready.sem, e_ready.of(t))
        pe.wait_ge(mg_ready.sem, mg_ready.of(t, 1))
        for hd in range(NH):
            if hd == HH:
                pe.wait_ge(mg_ready.sem, mg_ready.of(t, 2))
            q, n = hd % 4, hd // 4
            PE.matmul(banks[6][q * HD:(q + 1) * HD, col(n)], xtok[:, tp, hd * HD:(hd + 1) * HD], mg[:, tp, hd, :],
                      start=True, stop=True, skip_group_check=True)
        if due(t - 1):
            pe.wait_ge(state_ready.sem, state_ready.of(t - 1))
        for hd in range(NH):
            q, n = hd % 4, hd // 4
            mm = PE.matmul(banks[6][q * HD:(q + 1) * HD, DI + n * P:DI + (n + 1) * P],
                           state[:, 1 - tp, hd // 2, :], ct[par][:, hd // 2, i, hd % 2, :],
                           start=True, stop=True, skip_group_check=True)
        mm.then_inc(yy_done.sem, 1)
        pe.wait_ge(btok_ready.sem, btok_ready.of(t))
        pe.wait_ge(xw_ready.sem, xw_ready.of(t))
        if due(t - 1):
            pe.wait_ge(og_ready.sem, og_ready.of(t - 1))
        for j in range(NP):
            n = j // 2
            mm = PE.matmul(banks[7][:, col(j)], btok[:, tp, col(j)], xw[:, tp, col(n)], start=True, stop=True,
                           skip_group_check=True)
        mm.then_inc(ss_done.sem, 1)

    def act_decays(act, t, tp):
        for hf in range(2):
            act.wait_ge(dd_done.sem, dd_done.of(t, hf + 1))
            if hf == 0 and due(t - 2):
                act.wait_ge(mg_ready.sem, mg_ready.of(t - 2))
                act.wait_ge(xw_ready.sem, xw_ready.of(t - 2))
            SE.activation(m[:, tp, hf * HH:(hf + 1) * HH, :], banks[2 + hf][:].rearrange("p (h l) -> p h l", l=P),
                          ACT.Exp).then_inc(m_ready.sem, 1)

    def act_turned(act, t, i, tp, fr):
        act.wait_ge(xtr_done.sem, xtr_done.of(t))
        if due(t - 2):
            act.wait_ge(yy_done.sem, yy_done.of(t - 2))
            act.wait_ge(xw_ready.sem, xw_ready.of(t - 2))
        SE.activation(xtok[:, tp, :], fr.bank("xtr", i)[:, 0:DI], ACT.Copy).then_inc(xtok_ready.sem, 1)
        act.wait_ge(btr_done.sem, btr_done.of(t))
        if due(t - 2):
            act.wait_ge(ss_done.sem, ss_done.of(t - 2))
        SE.activation(btok[:, tp, :], banks[7][:], ACT.Copy).then_inc(btok_ready.sem, 1)
        act.wait_ge(ee_done.sem, ee_done.of(t))
        if due(t - 2):
            act.wait_ge(y_step.sem, y_step.of(t - 2))
            act.wait_ge(dec_ready.sem, dec_ready.of(t - 2))
        SE.activation(edec[:, tp, :, :], banks[6][:, 0:DI].rearrange("p (n l) -> p n l", l=P),
                      ACT.Exp).then_inc(e_ready.sem, 1)
        for q in range(2):
            rows = slice(q * NS, (q + 1) * NS)
            SE.activation(tdec[rows, tp, :], banks[6][rows, DI + q:DI + NH:2], ACT.Exp).then_inc(e_ready.sem, 1)

    def act_square(act, t, tp):
        act.wait_ge(y4_ready.sem, y4_ready.of(t))
        if due(t - 2):
            act.wait_ge(ysum_ready.sem, ysum_ready.of(t - 2))
        SE.activation(ysq[:, tp, :, :], y4[:, tp, :, :], ACT.Square).then_inc(ysq_ready.sem, 1)

    def act_out(act, t, i, par, g):
        if i == 0:
            if due(g - 2):
                act.wait_ge(post_dve1.sem, post_dve1.of(g - 2))
        act.wait_ge(oo_done.sem, oo_done.of(t))
        SE.activation(og[:, par, i, 0:D + 1], banks[7][:, 0:D + 1], ACT.Copy).then_inc(og_ready.sem, 1)

    def pool_squares(pl, t, tp):
        pl.wait_ge(ysq_ready.sem, ysq_ready.of(t))
        if due(t - 2):
            pl.wait_ge(oo_done.sem, oo_done.of(t - 2))
        apart(pl, t)
        PL.tensor_tensor(ysum[:, tp, :], ysq[:, tp, 0, :], ysq[:, tp, 1, :], ALU.add).then_inc(ysum_ready.sem, 1)

    def pool_tile(pl, t, i, g, par, tp, first_tile):
        for hf in range(2):
            v = m[:, tp, hf * HH:(hf + 1) * HH, :]
            pl.wait_ge(m_ready.sem, m_ready.of(t, hf + 1))
            apart(pl, t)
            PL.affine_select(out=v, in_=v, compare_op=ALU.is_ge, fill=0.0, base=0, pattern=[[0, HH], [1, P]],
                             channel_multiplier=-1).then_inc(mm_ready.sem, 1)
        if not first_tile:
            pool_squares(pl, t - 1, 1 - tp)
        pl.wait_ge(xtok_ready.sem, xtok_ready.of(t))
        if due(t - 2):
            pl.wait_ge(ss_done.sem, ss_done.of(t - 2))
        for hf in range(2):
            pl.wait_ge(mm_ready.sem, mm_ready.of(t, hf + 1))
            apart(pl, t)
            PL.tensor_tensor(xw[:, tp, col(hf)].rearrange("p (h d) -> p h d", d=HD),
                             xtok[:, tp, col(hf)].rearrange("p (h d) -> p h d", d=HD),
                             m[:, tp, hf * HH:(hf + 1) * HH, P - 1:P].to_broadcast([P, HH, HD]),
                             ALU.mult).then_inc(xw_ready.sem, 1)
        pl.wait_ge(e_ready.sem, e_ready.of(t))
        if due(t - 1):
            pl.wait_ge(state_ready.sem, state_ready.of(t - 1))
        apart(pl, t)
        PL.tensor_tensor(decayed[:], state[:, 1 - tp, :, :],
                         tdec[:, tp, :].rearrange("p (j o) -> p j o", o=1).to_broadcast([P, NP, HD]),
                         ALU.mult).then_inc(dec_ready.sem, 1)

    def pool_gate(pl, t, i, g, par, tp):
        if i == 0:
            pl.wait_ge(zt_ready.sem, zt_ready.of(g))
        pl.wait_ge(y_step.sem, y_step.of(t))
        if due(t - 2):
            pl.wait_ge(oo_done.sem, oo_done.of(t - 2))
        apart(pl, t)
        PL.tensor_tensor(y4[:, tp, :, :], y1[:], zt[par][:, :, col(i)], ALU.mult).then_inc(y4_ready.sem, 1)

    def dve_scores(dve, t, tp):
        if due(t - 2):
            dve.wait_ge(yy_done.sem, yy_done.of(t - 2))
        for hf in range(2):
            heads = slice(hf * HH, (hf + 1) * HH)
            dve.wait_ge(gg_done.sem, gg_done.of(t, hf + 1))
            dve.wait_ge(mm_ready.sem, mm_ready.of(t, hf + 1))
            DVE.tensor_tensor(mg[:, tp, heads, :], banks[4 + hf][:].rearrange("p (h l) -> p h l", l=P),
                              m[:, tp, heads, :], ALU.mult).then_inc(mg_ready.sem, 1)

    def dve_y(dve, t, i, par, tp):
        dve.wait_ge(yy_done.sem, yy_done.of(t))
        dve.wait_ge(e_ready.sem, e_ready.of(t))
        if due(t - 1):
            dve.wait_ge(y4_ready.sem, y4_ready.of(t - 1))
        DVE.tensor_tensor(y1[:], banks[6][:, DI:2 * DI].rearrange("p (n l) -> p n l", l=P), edec[:, tp, :, :],
                          ALU.mult).then_inc(y_step.sem, 1)
        for n in range(NB):
            DVE.scalar_tensor_tensor(out=y2[:, n, :], in0=xt[par][:, n, col(i)], scalar=dcol[:, n:n + 1],
                                     in1=banks[6][:, col(n)], op0=ALU.mult, op1=ALU.add).then_inc(y_step.sem, 1)
        dve.wait_ge(y_step.sem, y_step.of(t, 3))
        DVE.tensor_tensor(y1[:], y1[:], y2[:], ALU.add).then_inc(y_step.sem, 1)

    def dve_state(dve, t, tp, last_of_batch):
        dve.wait_ge(ss_done.sem, ss_done.of(t))
        dve.wait_ge(dec_ready.sem, dec_ready.of(t))
        for q in range(2):
            rows = slice(q * NS, (q + 1) * NS)
            if last_of_batch:
                DVE.memset(state[rows, tp, :, :], 0.0).then_inc(state_ready.sem, 1)
                continue
            s = banks[7][rows, :].rearrange("p (n k d) -> p n k d", n=NB, d=HD)[:, :, q:q + 7:6, :]
            DVE.tensor_tensor(state[rows, tp, :, :].rearrange("p (n j) d -> p n j d", n=2), s,
                              decayed[rows, :, :].rearrange("p (n j) d -> p n j d", n=2),
                              ALU.add).then_inc(state_ready.sem, 1)

    def pool_post1(pl, g, par):
        pl.wait_ge(og_ready.sem, og_ready.of(g * TG + TG - 1))
        apart(pl, g)
        PL.tensor_scalar(pt[:, 0, :], og[:, par, :, D], 1.0 / DI, RMS_EPS, ALU.mult, ALU.add
                         ).then_inc(post_pool1.sem, 1)
        pl.wait_ge(post_pool1.sem, post_pool1.of(g, 1))
        apart(pl, g)
        PL.tensor_tensor(pt[:, 1, :], pt[:, 0, :], neghalf[:], ALU.pow).then_inc(post_pool1.sem, 1)

    def dve_xn(dve, g, dyn):
        if due(g - 1):
            dve.wait_ge(x2_ready.sem, x2_ready.of(g - 1))
        for i in range(TG):
            t1 = dyn(g * TG + i, 1)
            DVE.tensor_scalar(ob[:, i, :], xall[:, t1, :].rearrange("p o d -> p (o d)"), s1[:, t1], nb1[:, t1],
                              ALU.mult, ALU.add).then_inc(xn_ready.sem, 1)

    def dve_post1(dve, g, par):
        dve.wait_ge(post_pool1.sem, post_pool1.of(g))
        for i in range(TG):
            dve.wait_ge(xn_ready.sem, xn_ready.of(g, i + 1))
            DVE.scalar_tensor_tensor(out=ob[:, i, :], in0=og[:, par, i, 0:D], scalar=pt[:, 1, i:i + 1],
                                     in1=ob[:, i, :], op0=ALU.mult, op1=ALU.add).then_inc(post_dve1.sem, 1)

    def dve_post1_stats(dve, g):
        for i in range(TG):
            dve.wait_ge(post_dve1.sem, post_dve1.of(g, i + 1))
            DVE.bn_stats(pst6[:, i, :], ob[:, i, :]).then_inc(post_dve1.sem, 1)
        for i in range(TG):
            dve.wait_ge(post_dve1.sem, post_dve1.of(g, TG + i + 1))
            apart(dve, g)
            DVE.bn_aggr(pmv[:, i, :], pst6[:, i, :]).then_inc(post_dve1.sem, 1)

    def pool_post2(pl, g):
        pl.wait_ge(post_dve1.sem, post_dve1.of(g))
        apart(pl, g)
        PL.tensor_scalar(pt[:, 2, :], pmv[:, :, 1], LN_EPS, None, ALU.add).then_inc(post_pool2.sem, 1)
        pl.wait_ge(post_pool2.sem, post_pool2.of(g, 1))
        apart(pl, g)
        PL.tensor_tensor(pt[:, 3, :], pt[:, 2, :], neghalf[:], ALU.pow).then_inc(post_pool2.sem, 1)

    def dve_post2(dve, g, dyn):
        dve.wait_ge(post_dve1.sem, post_dve1.of(g))
        for i in range(TG):
            DVE.tensor_scalar(ob[:, i, :], ob[:, i, :], pmv[:, i, 0:1], None, ALU.subtract).then_inc(centred.sem, 1)
        dve.wait_ge(post_pool2.sem, post_pool2.of(g))
        for i in range(TG):
            x = xall[:, dyn(g * TG + i, 1), :].rearrange("p o d -> p (o d)")
            dve.wait_ge(centred.sem, centred.of(g, i + 1))
            DVE.scalar_tensor_tensor(out=x, in0=ob[:, i, :], scalar=pt[:, 3, i:i + 1], in1=x,
                                     op0=ALU.mult, op1=ALU.add).then_inc(x2_ready.sem, 1)

    def run(eng, what, b, u, last, moe=None):
        g = b * GB + u
        dyn = static if isinstance(b, int) else dynamic
        par = u
        ahead = not (last and u == GB - 1)
        f = g + 1 if ahead else None
        prior = fr_uses(g, g - 1 if not (isinstance(g, int) and g == 0) else None)
        if isinstance(g, int) and g == 0:
            prior = [x for x in prior if x]
        fr = Front(g, f, prior)
        norm = not (last)
        for i in range(TG):
            t, tp = g * TG + i, i % 2
            what(eng, t=t, i=i, g=g, f=f, par=par, tp=tp, fr=fr, dyn=dyn, norm=norm, moe=None if ahead else moe, seq=b,
                 end_of_batch=u == GB - 1 and i == TG - 1, begin=isinstance(t, int) and t == 0, fu=(u + 1) % GB)

    def pe_body(pe, t, i, g, f, par, tp, fr, dyn, norm, moe, seq, end_of_batch, begin, fu):
        if f is not None and i == 0:
            pe_front(pe, f, fu, fr, i, 0)
        pe_decays(pe, t, i, g, par, seq)
        if f is not None and i:
            pe_front(pe, f, fu, fr, i, 0)
        pe_scores(pe, t, i, g, par, 0)
        if f is not None:
            pe_front(pe, f, fu, fr, i, 1)
        pe_scores(pe, t, i, g, par, 1)
        pe_turns(pe, t, i, g, par, fr)
        if moe and i == 3:
            moe.pe_first(pe)
        if f is not None:
            pe_front(pe, f, fu, fr, i, 2)
        if not begin:
            pe_out_tile(pe, t - 1, 1 - tp)
        if f is not None:
            pe_front(pe, f, fu, fr, i, 3)
        pe_y(pe, t, i, g, par, tp, begin)

    def act_body(act, t, i, g, f, par, tp, fr, dyn, norm, moe, seq, end_of_batch, begin, fu):
        if f is not None and i == 0:
            act_front(act, f, fu, fr, i, 0)
        act_decays(act, t, tp)
        if f is not None and i:
            act_front(act, f, fu, fr, i, 0)
        if f is not None:
            act_front(act, f, fu, fr, i, 1)
        if not begin:
            act_square(act, t - 1, 1 - tp)
        if f is not None and i == 2:
            act_x_sigmoid(act, f, fu, 0)
        if f is not None and i == 3:
            act_z_sigmoid(act, f, fu, 1)
        act_turned(act, t, i, tp, fr)
        if moe and i == 2:
            moe.act_prepare(act)
        if moe and i == 3:
            moe.act_turned(act, 0, 0)
        if f is not None:
            act_front(act, f, fu, fr, i, 2)
        if i == 0:
            act_z_sigmoid(act, g, par, 2)
        if not begin:
            act_out(act, t - 1, (i - 1) % TG, par if i else 1 - par, g)
        if f is not None and i == 2:
            act_x_sigmoid(act, f, fu, 1)
        if i == 3 and norm:
            act_h(act, g + 2, par, dyn)
        if f is not None:
            act_front(act, f, fu, fr, i, 3)
        if f is not None and i == 2:
            act_x_sigmoid(act, f, fu, 2)
            act_z_sigmoid(act, f, fu, 0)

    def dve_body(dve, t, i, g, f, par, tp, fr, dyn, norm, moe, seq, end_of_batch, begin, fu):
        has_post = not (isinstance(g, int) and g == 0)
        if f is not None:
            dve_front(dve, f, fu, fr, i, 0)
        if i == 2 and has_post:
            dve_xn(dve, g - 1, dyn)
            dve_post1(dve, g - 1, 1 - par)
        if f is not None:
            dve_front(dve, f, fu, fr, i, 1)
        if i == 2 and has_post:
            dve_post1_stats(dve, g - 1)
        if moe and i == 2:
            moe.dve_stats(dve, 0, static)
        if moe and i == 3:
            moe.dve_h(dve, 0, static)
        dve_scores(dve, t, tp)
        if moe and i == 2:
            moe.dve_prepare(dve)
        if moe and i == 3:
            moe.dve_prepare_b1(dve)
            moe.dve_turned(dve, 0, 0)
        if i == 0 and norm:
            dve_stats(dve, g + 2, dyn)
        if f is not None:
            dve_front(dve, f, fu, fr, i, 2)
        if i == 0 and has_post and not (isinstance(g, int) and g == 1):
            dve_post2(dve, g - 2, dyn)
        if f is not None:
            dve_front(dve, f, fu, fr, i, 3)
        dve_y(dve, t, i, par, tp)
        dve_state(dve, t, tp, end_of_batch)

    def pool_body(pl, t, i, g, f, par, tp, fr, dyn, norm, moe, seq, end_of_batch, begin, fu):
        pool_tile(pl, t, i, g, par, tp, begin)
        has_post = not (isinstance(g, int) and g == 0)
        if i == 0:
            if f is not None:
                pool_history(pl, f, fu, fu == 0)
            pool_silu_z(pl, g, par)
            if has_post:
                pool_post1(pl, g - 1, 1 - par)
        if i == 1 and f is not None:
            pool_softplus(pl, f)
        if i == 2 and norm:
            pool_norm(pl, g + 2, dyn)
        if i == 3 and has_post:
            pool_post2(pl, g - 1)
        if moe and i == 2:
            moe.pool_norm(pl, 0)
        pool_gate(pl, t, i, g, par, tp)

    def over_sequences(eng, body, moe):
        for u in range(GB):
            run(eng, body, 0, u, False)
        with eng.Fori(1, BATCH - 1) as b:
            for u in range(GB):
                run(eng, body, b, u, False)
        for u in range(GB):
            run(eng, body, BATCH - 1, u, True, moe)

    G_LAST, T_LAST = GROUPS - 1, TILES - 1

    def tensor_program(pe, moe):
        pe_prepare(pe)
        fr = Front(None, 0, [])
        for i in range(TG):
            for slot in range(SLOTS):
                pe_front(pe, 0, 0, fr, i, slot)
        pe.wait_ge(cleared.sem, CLEARED + 1)
        pe.wait_ge(const_step.sem, ALL_CONSTS)
        pe.wait_ge(prep.sem, PREP)
        over_sequences(pe, pe_body, moe)
        pe_out_tile(pe, T_LAST, T_LAST % 2, last=True)

    def scalar_program(act, moe):
        act.preload_act_table_set("natural_log_exp_and_others")
        act_prepare(act)
        fr = Front(None, 0, [])
        for i in range(TG):
            for slot in range(SLOTS):
                act_front(act, 0, 0, fr, i, slot)
                if i == 2 and slot == 0:
                    act_x_sigmoid(act, 0, 0, 0)
                    act_x_sigmoid(act, 0, 0, 1)
                    act_x_sigmoid(act, 0, 0, 2)
                if i == 2 and slot == SLOTS - 1:
                    act_z_sigmoid(act, 0, 0, 0)
            if i == 1:
                act.wait_ge(loaded_second, 16)
                act_h(act, 1, 1, static)
        act_z_sigmoid(act, 0, 0, 1)
        act.wait_ge(loaded1, 16)
        act.wait_ge(const_step.sem, ALL_CONSTS)
        over_sequences(act, act_body, moe)
        act_square(act, T_LAST, T_LAST % 2)
        act_out(act, T_LAST, TG - 1, 1, G_LAST)

    def vector_program(dve, moe):
        dve.wait_ge(loaded0, 16)
        dve_stats(dve, 0, static)
        dve_clear(dve)
        dve_prepare(dve)
        dve.wait_ge(loaded_second, 16)
        dve_stats(dve, 1, static)
        dve_prepare_small(dve)
        dve.wait_ge(cleared.sem, CLEARED)
        fr = Front(None, 0, [])
        for i in range(TG):
            for slot in range(SLOTS):
                dve_front(dve, 0, 0, fr, i, slot)
                if i == 0 and slot == 0:
                    dve_row_constants(dve, 0)
        dve_row_constants(dve, 1)
        dve.wait_ge(const_step.sem, ALL_CONSTS)
        dve.wait_ge(loaded1, 16)
        over_sequences(dve, dve_body, moe)
        moe.dve_route_a(dve, 0)
        dve_post2(dve, G_LAST - 1, static)
        dve_xn(dve, G_LAST, static)
        moe.dve_route_b(dve, 0)
        moe.dve_route_c(dve, 0, 0)
        dve_post1(dve, G_LAST, 1)
        dve_post1_stats(dve, G_LAST)

    def dve_finish(dve):
        dve_post2(dve, G_LAST, static)

    def gpsimd_program(pl, moe):
        pool_identity(pl)
        pool_norm(pl, 0, static)
        moe.pool_constants(pl)
        pool_history(pl, 0, 0, True)
        pool_selectors(pl)
        pool_norm(pl, 1, static)
        pool_softplus(pl, 0)
        PL.memset(ct[0][:], 0.0).then_inc(const_step.sem, 1)
        pool_clear(pl)
        pl.wait_ge(cleared.sem, CLEARED)
        over_sequences(pl, pool_body, moe)
        pool_squares(pl, T_LAST, T_LAST % 2)
        pool_post1(pl, G_LAST, 1)
        pool_post2(pl, G_LAST)

    def row_copies(sp, b, u):
        g = GB * b + u
        sp.wait_ge(part_ready.sem, part_ready.of(g))
        if due(g - 2):
            sp.wait_ge(dd_done.sem, dd_done.of((g - 2) * TG + TG - 1))
        for k in range(PARTS):
            sp.dma_start(rows[u][32 * k + NH:32 * k + NH + 1, :, :], parts[32 * k:32 * k + NH, u, :]
                         ).then_inc(rows_ready[u], 16)

    def sync_program(sp):
        load_all(sp)
        for u in range(GB):
            sp.wait_ge(cleared.sem, CLEARED + 1 + u)
            row_copies(sp, 0, u)
        with sp.Fori(1, BATCH) as b:
            for u in range(GB):
                row_copies(sp, b, u)
        sp.wait_ge(fr_done.sem, fr_done.of(G_LAST))
        sp.wait_ge(zt_ready.sem, zt_ready.of(G_LAST))
        sp.wait_ge(part_ready.sem, part_ready.of(G_LAST))
        sp.wait_ge(ctd_ready.sem, ctd_ready.of(G_LAST))
        sp.wait_ge(xt_ready.sem, xt_ready.of(G_LAST))
        sp.wait_ge(y4_ready.sem, y4_ready.of(G_LAST * TG - 1))

    this = Part()
    this.ident = ident
    this.neghalf = neghalf
    this.rank = rank
    this.t_last = T_LAST
    this.g_last = G_LAST
    this.xtok_ready = xtok_ready
    this.y_step = y_step
    this.og_ready = og_ready
    this.x2_ready = x2_ready
    this.dve_finish = dve_finish
    this.sync = sync_program
    this.tensor = tensor_program
    this.scalar = scalar_program
    this.vector = vector_program
    this.gpsimd = gpsimd_program
    return this


def experts(nc, buffers, xall, banks, att, wg_d, w1_d, b1_d, w2_d, b2_d, out):
    def sb(name, shape, dt=F32):
        return buffers.enter_context(nc.sbuf_tensor("moe_" + name, shape, dt))

    def sig(name, per=1):
        return Signal(nc, "moe_" + name, per)

    PE, DVE, SE, PL = nc.tensor, nc.vector, nc.scalar, nc.gpsimd

    ident, neghalf = att.ident, att.neghalf
    up_banks, down_banks, turn_bank, logit_bank = banks[2:6], banks[6:8], banks[0], banks[1]
    rank = att.rank
    b2 = sb("b2", [P, NE, D])
    b2mix = sb("b2_mix", [P, 2, TG, D])
    w1f = sb("w1", [P, NE, FH])
    w1hi = sb("w1_hi", [P, NE, FH], F32R)
    w1lo = sb("w1_lo", [P, NE, FH], F32R)
    w2 = sb("w2", [P, NE, FB, D])
    wg = sb("wg", [P, NE])
    b1row = sb("b1_rows", [NE * FB, P])
    b1 = sb("b1", [P, NE * FB])

    st6 = sb("st6", [P, TG, 6])
    mv = sb("mv", [P, TG, 2])
    lnt = sb("lnt", [P, 4, TG])
    h = sb("h", [P, TG, D])
    thi = sb("t_hi", [P, 2, GT], F32R)
    tlo = sb("t_lo", [P, 2, GT], F32R)
    tf = sb("t", [P, GT])
    route = sb("route", [P, 10, TG, NE])
    rmax = sb("rmax", [P, 6, TG])
    scores = sb("scores", [P, 2, TG, NE])
    hid = sb("hid", [P, 2, FB, GT])
    acc = sb("acc", [P, 2, TG, D])
    post = sb("post", [P, 2, TG])
    pst6 = sb("pst6", [P, TG, 6])
    pmv = sb("pmv", [P, TG, 2])
    outb = sb("outb", [P, 2, TG, D])

    loaded = nc.alloc_semaphore("moe_weights_loaded")
    LOADS = 5 * 16
    const_step = sig("ranks_made", 1)
    prep_act = sig("w1_hi_made", 1)
    mix_step = sig("b2_mix_steps", 2 * (NE - 2) - 1)
    b2_step = sig("b2_steps", 2 * TG + 1)
    prep = sig("weights_prepared", 1)
    prep_pe = sig("b1_turned", 1)
    ln_stats = sig("ln_stats_ready", 2 * TG)
    coef_step = sig("ln_coefficient_steps", 4)
    h_ready = sig("h_ready", TG)
    turned = sig("h_turned")
    thi_ready = sig("t_hi_ready")
    tf_ready = sig("t_ready")
    tlo_ready = sig("t_lo_ready")
    logits = sig("logits_done")
    route_a = sig("route_before_exp", 2)
    exp_ready = sig("exp_ready")
    ROUTE = 13
    route_b = sig("route_steps", ROUTE)
    up_done = sig("up_done", NE * FB)
    hid_ready = sig("hidden_ready", NE * FB)
    down_done = sig("down_done", NE)
    acc_step = sig("mix_steps", NE * TG)
    stats2 = sig("post_stats", 2 * TG)
    post_pool = sig("post_ln", 2)
    centred = sig("post_centred", TG)
    out_ready = sig("out_ready", TG)
    stored = [nc.alloc_semaphore(f"moe_stored{u}") for u in range(2)]

    def tile(g, i, dyn):
        return xall[:, dyn(g * TG + i, 1), :].rearrange("p o d -> p (o d)")

    def pool_constants(pl):
        for e in range(NE):
            PL.memset(rank[:, :, e:e + 1], float(NE - e)).then_inc(const_step.sem, 1)

    def act_prepare(act):
        act.wait_ge(loaded, LOADS)
        SE.activation(w1hi[:], w1f[:], ACT.Copy).then_inc(prep_act.sem, 1)

    def dve_prepare(dve):
        dve.wait_ge(prep_act.sem, 1)
        DVE.tensor_tensor(w1lo[:], w1f[:], w1hi[:].bitcast(F32), ALU.subtract).then_inc(prep.sem, 1)

    def dve_prepare_b1(dve):
        dve.wait_ge(prep_pe.sem, 1)
        DVE.tensor_copy(b1[:], logit_bank[:, 0:NE * FB]).then_inc(prep.sem, 1)

    PREP = 2

    def pe_first(pe):
        pe.wait_ge(loaded, LOADS)
        pe.wait_ge(att.xtok_ready.sem, att.xtok_ready.of(att.t_last))
        PE.transpose(logit_bank[:, 0:NE * FB], b1row[:], ident[0:NE * FB, 0:NE * FB]).then_inc(prep_pe.sem, 1)
        pe_turn(pe, 0)
        pe.wait_ge(prep.sem, PREP)
        pe_logits(pe, 0)

    def dve_stats(dve, f, dyn):
        if isinstance(f, int) and f == 0:
            dve.wait_ge(loaded, LOADS)
        if due(f - 1):
            dve.wait_ge(coef_step.sem, coef_step.of(f - 1))
        dve.wait_ge(att.x2_ready.sem, att.x2_ready.of(f))
        for i in range(TG):
            DVE.bn_stats(st6[:, i, :], tile(f, i, dyn)).then_inc(ln_stats.sem, 1)
        for i in range(TG):
            dve.wait_ge(ln_stats.sem, ln_stats.of(f, i + 1))
            apart(dve, f)
            DVE.bn_aggr(mv[:, i, :], st6[:, i, :]).then_inc(ln_stats.sem, 1)

    def pool_norm(pl, f):
        pl.wait_ge(ln_stats.sem, ln_stats.of(f))
        if due(f - 1):
            pl.wait_ge(h_ready.sem, h_ready.of(f - 1))
        apart(pl, f)
        PL.tensor_scalar(lnt[:, 0, :], mv[:, :, 1], LN_EPS, None, ALU.add).then_inc(coef_step.sem, 1)
        pl.wait_ge(coef_step.sem, coef_step.of(f, 1))
        apart(pl, f)
        PL.tensor_tensor(lnt[:, 1, :], lnt[:, 0, :], neghalf[:], ALU.pow).then_inc(coef_step.sem, 1)
        pl.wait_ge(coef_step.sem, coef_step.of(f, 2))
        apart(pl, f)
        PL.tensor_scalar(lnt[:, 2, :], mv[:, :, 0], -1.0, None, ALU.mult).then_inc(coef_step.sem, 1)
        pl.wait_ge(coef_step.sem, coef_step.of(f, 3))
        apart(pl, f)
        PL.tensor_tensor(lnt[:, 3, :], lnt[:, 2, :], lnt[:, 1, :], ALU.mult).then_inc(coef_step.sem, 1)

    def dve_h(dve, f, dyn):
        dve.wait_ge(coef_step.sem, coef_step.of(f))
        if due(f - 1):
            dve.wait_ge(turned.sem, turned.of(f - 1))
        for i in range(TG):
            DVE.tensor_scalar(h[:, i, :], tile(f, i, dyn), lnt[:, 1, i:i + 1], lnt[:, 3, i:i + 1],
                              ALU.mult, ALU.add).then_inc(h_ready.sem, 1)

    def pe_turn(pe, f):
        pe.wait_ge(h_ready.sem, h_ready.of(f))
        if due(f - 1):
            pe.wait_ge(tlo_ready.sem, tlo_ready.of(f - 1))
            pe.wait_ge(tf_ready.sem, tf_ready.of(f - 1))
        for i in range(TG):
            mm = PE.transpose(turn_bank[:, col(i)], h[:, i, :], ident[:])
        mm.then_inc(turned.sem, 1)

    def act_turned(act, f, par):
        act.wait_ge(turned.sem, turned.of(f))
        if due(f - 2):
            act.wait_ge(up_done.sem, up_done.of(f - 2))
        SE.activation(thi[:, par, :], turn_bank[:], ACT.Copy).then_inc(thi_ready.sem, 1)
        if due(f - 1):
            act.wait_ge(logits.sem, logits.of(f - 1))
        SE.activation(tf[:], turn_bank[:], ACT.Copy).then_inc(tf_ready.sem, 1)

    def dve_turned(dve, f, par):
        dve.wait_ge(thi_ready.sem, thi_ready.of(f))
        dve.wait_ge(tf_ready.sem, tf_ready.of(f))
        if due(f - 2):
            dve.wait_ge(up_done.sem, up_done.of(f - 2))
        DVE.tensor_tensor(tlo[:, par, :], turn_bank[:], thi[:, par, :].bitcast(F32),
                          ALU.subtract).then_inc(tlo_ready.sem, 1)

    def pe_logits(pe, f):
        pe.wait_ge(tf_ready.sem, tf_ready.of(f))
        if due(f - 1):
            pe.wait_ge(route_a.sem, route_a.of(f - 1))
        for i in range(TG):
            mm = PE.matmul(logit_bank[:, i * NE:(i + 1) * NE], tf[:, col(i)], wg[:], start=True, stop=True,
                           skip_group_check=True)
        mm.then_inc(logits.sem, 1)

    def wide(v):
        return v.rearrange("p (t o) -> p t o", o=1).to_broadcast([P, TG, NE])

    def dve_route_a(dve, f):
        lg = logit_bank[:, 0:TG * NE].rearrange("p (t e) -> p t e", e=NE)
        dve.wait_ge(logits.sem, logits.of(f))
        if due(f - 1):
            dve.wait_ge(route_b.sem, route_b.of(f - 1))
        DVE.tensor_reduce(rmax[:, 0, :], lg, AX, ALU.max).then_inc(route_a.sem, 1)
        dve.wait_ge(route_a.sem, route_a.of(f, 1))
        if due(f - 1):
            dve.wait_ge(exp_ready.sem, exp_ready.of(f - 1))
        DVE.tensor_tensor(route[:, 0], lg, wide(rmax[:, 0, :]), ALU.subtract).then_inc(route_a.sem, 1)

    def act_exp(act, f):
        act.wait_ge(route_a.sem, route_a.of(f))
        if due(f - 1):
            act.wait_ge(route_b.sem, route_b.of(f - 1))
        SE.activation(route[:, 1], route[:, 0], ACT.Exp).then_inc(exp_ready.sem, 1)

    def dve_route_b(dve, f):
        d, e, r = route[:, 0], route[:, 1], lambda k: route[:, 2 + k]
        dve.wait_ge(route_a.sem, route_a.of(f))
        if isinstance(f, int) and f == 0:
            dve.wait_ge(const_step.sem, const_step.of(0, NE))
        DVE.scalar_tensor_tensor(out=r(0), in0=d, scalar=0.0, in1=rank[:], op0=ALU.is_equal,
                                 op1=ALU.mult).then_inc(route_b.sem, 1)
        dve.wait_ge(route_b.sem, route_b.of(f, 1))
        DVE.tensor_reduce(rmax[:, 1, :], r(0), AX, ALU.max).then_inc(route_b.sem, 1)
        dve.wait_ge(route_b.sem, route_b.of(f, 2))
        DVE.tensor_tensor(r(1), rank[:], wide(rmax[:, 1, :]), ALU.is_equal).then_inc(route_b.sem, 1)
        dve.wait_ge(route_b.sem, route_b.of(f, 3))
        DVE.scalar_tensor_tensor(out=r(2), in0=r(1), scalar=-1e30, in1=d, op0=ALU.mult,
                                 op1=ALU.add).then_inc(route_b.sem, 1)
        dve.wait_ge(route_b.sem, route_b.of(f, 4))
        DVE.tensor_reduce(rmax[:, 2, :], r(2), AX, ALU.max).then_inc(route_b.sem, 1)
        dve.wait_ge(route_b.sem, route_b.of(f, 5))
        DVE.tensor_tensor(r(3), r(2), wide(rmax[:, 2, :]), ALU.is_equal).then_inc(route_b.sem, 1)
        dve.wait_ge(route_b.sem, route_b.of(f, 6))
        DVE.tensor_tensor(r(4), r(3), rank[:], ALU.mult).then_inc(route_b.sem, 1)
        dve.wait_ge(route_b.sem, route_b.of(f, 7))
        DVE.tensor_reduce(rmax[:, 3, :], r(4), AX, ALU.max).then_inc(route_b.sem, 1)
        dve.wait_ge(route_b.sem, route_b.of(f, 8))
        DVE.tensor_tensor(r(5), rank[:], wide(rmax[:, 3, :]), ALU.is_equal).then_inc(route_b.sem, 1)
        dve.wait_ge(route_b.sem, route_b.of(f, 9))
        DVE.tensor_tensor(r(6), r(1), r(5), ALU.add).then_inc(route_b.sem, 1)

    def dve_route_c(dve, f, par):
        e, r = route[:, 1], lambda k: route[:, 2 + k]
        dve.wait_ge(route_b.sem, route_b.of(f, 10))
        dve.wait_ge(exp_ready.sem, exp_ready.of(f))
        DVE.tensor_tensor(r(7), r(6), e, ALU.mult).then_inc(route_b.sem, 1)
        dve.wait_ge(route_b.sem, route_b.of(f, 11))
        DVE.tensor_reduce(rmax[:, 4, :], r(7), AX, ALU.add).then_inc(route_b.sem, 1)
        dve.wait_ge(route_b.sem, route_b.of(f, 12))
        DVE.reciprocal(rmax[:, 5, :], rmax[:, 4, :]).then_inc(route_b.sem, 1)
        dve.wait_ge(route_b.sem, route_b.of(f))
        if due(f - 2):
            dve.wait_ge(acc_step.sem, acc_step.of(f - 2))
            dve.wait_ge(mix_step.sem, mix_step.of(f - 2))
        DVE.tensor_tensor(scores[:, par], r(7), wide(rmax[:, 5, :]), ALU.mult).then_inc(score_ready.sem, 1)

    score_ready = sig("scores_ready")

    def pe_up(pe, g, par, e):
        if e == 0:
            pe.wait_ge(thi_ready.sem, thi_ready.of(g))
            pe.wait_ge(tlo_ready.sem, tlo_ready.of(g))
        for n in range(FB):
            k = e * FB + n
            bank = up_banks[k % 4]
            if k >= 4:
                pe.wait_ge(hid_ready.sem, hid_ready.of(g, k - 3))
            else:
                if due(g - 1):
                    pe.wait_ge(hid_ready.sem, hid_ready.of(g - 1, NE * FB + k - 3))
            w = slice(n * P, (n + 1) * P)
            PE.matmul(bank[:], w1hi[:, e, w], thi[:, par, :], start=True, stop=False)
            PE.matmul(bank[:], w1hi[:, e, w], tlo[:, par, :], start=False, stop=False)
            PE.matmul(bank[:], w1lo[:, e, w], thi[:, par, :], start=False, stop=True).then_inc(up_done.sem, 1)

    def act_hidden(act, g, e):
        for n in range(FB):
            k = e * FB + n
            act.wait_ge(up_done.sem, up_done.of(g, k + 1))
            if e > 1 or due(g - 1):
                act.wait_ge(down_done.sem, down_done.of(g, e - 1))
            SE.activation(hid[:, e % 2, n, :], up_banks[k % 4][:], ACT.Relu, bias=b1[:, k:k + 1]
                          ).then_inc(hid_ready.sem, 1)

    def pe_down(pe, g, e):
        bank = down_banks[e % 2]
        if e > 1 or due(g - 1):
            pe.wait_ge(acc_step.sem, acc_step.of(g, (e - 1) * TG))
        elif e == 0:
            pe.wait_ge(att.y_step.sem, att.y_step.of(att.t_last))
        else:
            pe.wait_ge(att.og_ready.sem, att.og_ready.of(att.t_last))
        pe.wait_ge(hid_ready.sem, hid_ready.of(g, (e + 1) * FB))
        for i in range(TG):
            for n in range(FB):
                mm = PE.matmul(bank[:, col(i)], hid[:, e % 2, n, col(i)], w2[:, e, n, :], start=n == 0,
                               stop=n == FB - 1, skip_group_check=True)
        mm.then_inc(down_done.sem, 1)

    DVE_B2 = (3, 4)

    def pool_bias(pl, g, par):
        pl.wait_ge(score_ready.sem, score_ready.of(g))
        if due(g - 1):
            pl.wait_ge(b2_step.sem, b2_step.of(g - 1))
        done = 0
        for e in [e for e in range(NE) if e not in DVE_B2]:
            b = b2[:, e, :].rearrange("p (o d) -> p o d", o=1).to_broadcast([P, TG, D])
            s = scores[:, par, :, e:e + 1].to_broadcast([P, TG, D])
            if done == 0:
                apart(pl, g)
                PL.tensor_tensor(b2mix[:, 0], b, s, ALU.mult).then_inc(mix_step.sem, 1)
                done = 1
                continue
            pl.wait_ge(mix_step.sem, mix_step.of(g, done))
            apart(pl, g)
            PL.tensor_tensor(b2mix[:, 1], b, s, ALU.mult).then_inc(mix_step.sem, 1)
            pl.wait_ge(mix_step.sem, mix_step.of(g, done + 1))
            apart(pl, g)
            PL.tensor_tensor(b2mix[:, 0], b2mix[:, 0], b2mix[:, 1], ALU.add).then_inc(mix_step.sem, 1)
            done += 2

    def dve_mix(dve, g, par, e, last=False):
        dve.wait_ge(down_done.sem, down_done.of(g, e + 1))
        if e == 0:
            dve.wait_ge(score_ready.sem, score_ready.of(g))
            if due(g - 2):
                dve.wait_ge(stats2.sem, stats2.of(g - 2))
                dve.wait_ge(out_ready.sem, out_ready.of(g - 2))
        for i in range(TG):
            y, s = down_banks[e % 2][:, col(i)], scores[:, par, i, e:e + 1]
            if e == 0:
                DVE.tensor_scalar(acc[:, par, i, :], y, s, None, ALU.mult).then_inc(acc_step.sem, 1)
                continue
            if last and e == NE - 1:
                dve.wait_ge(b2_step.sem, b2_step.of(g))
            elif e - 1 in DVE_B2:
                dve.wait_ge(b2_step.sem, b2_step.of(g, DVE_B2.index(e - 1) * TG + i + 1))
            else:
                dve.wait_ge(acc_step.sem, acc_step.of(g, (e - 1) * TG + i + 1))
            DVE.scalar_tensor_tensor(out=acc[:, par, i, :], in0=y, scalar=s, in1=acc[:, par, i, :],
                                     op0=ALU.mult, op1=ALU.add).then_inc(acc_step.sem, 1)
        if e in DVE_B2:
            for i in range(TG):
                dve.wait_ge(acc_step.sem, acc_step.of(g, e * TG + i + 1))
                DVE.scalar_tensor_tensor(out=acc[:, par, i, :], in0=b2[:, e, :], scalar=scores[:, par, i, e:e + 1],
                                         in1=acc[:, par, i, :], op0=ALU.mult, op1=ALU.add).then_inc(b2_step.sem, 1)
        if e == (NE - 2 if last else NE - 1):
            dve.wait_ge(mix_step.sem, mix_step.of(g))
            dve.wait_ge(acc_step.sem, acc_step.of(g, (e + 1) * TG))
            DVE.tensor_tensor(acc[:, par, :, :], acc[:, par, :, :], b2mix[:, 0], ALU.add).then_inc(b2_step.sem, 1)

    def dve_post1(dve, g, par, last=False):
        if due(g - 1):
            dve.wait_ge(post_pool.sem, post_pool.of(g - 1))
        for i in range(TG):
            if last:
                dve.wait_ge(acc_step.sem, acc_step.of(g, (NE - 1) * TG + i + 1))
            else:
                dve.wait_ge(b2_step.sem, b2_step.of(g))
            DVE.bn_stats(pst6[:, i, :], acc[:, par, i, :]).then_inc(stats2.sem, 1)
        for i in range(TG):
            dve.wait_ge(stats2.sem, stats2.of(g, i + 1))
            apart(dve, g)
            DVE.bn_aggr(pmv[:, i, :], pst6[:, i, :]).then_inc(stats2.sem, 1)

    def pool_post(pl, g):
        pl.wait_ge(stats2.sem, stats2.of(g))
        if due(g - 1):
            pl.wait_ge(out_ready.sem, out_ready.of(g - 1))
        apart(pl, g)
        PL.tensor_scalar(post[:, 0, :], pmv[:, :, 1], LN_EPS, None, ALU.add).then_inc(post_pool.sem, 1)
        pl.wait_ge(post_pool.sem, post_pool.of(g, 1))
        apart(pl, g)
        PL.tensor_tensor(post[:, 1, :], post[:, 0, :], neghalf[:], ALU.pow).then_inc(post_pool.sem, 1)

    def dve_post2(dve, g, par, b, dyn):
        dve.wait_ge(stats2.sem, stats2.of(g))
        for i in range(TG):
            DVE.tensor_scalar(acc[:, par, i, :], acc[:, par, i, :], pmv[:, i, 0:1], None,
                              ALU.subtract).then_inc(centred.sem, 1)
        dve.wait_ge(post_pool.sem, post_pool.of(g))
        if not (isinstance(b, int) and b == 0):
            dve.wait_ge(stored[par], 1 + b * 16)
        for i in range(TG):
            dve.wait_ge(centred.sem, centred.of(g, i + 1))
            DVE.scalar_tensor_tensor(out=outb[:, par, i, :], in0=acc[:, par, i, :], scalar=post[:, 1, i:i + 1],
                                     in1=tile(g, i, dyn), op0=ALU.mult, op1=ALU.add).then_inc(out_ready.sem, 1)

    ov = out.rearrange("b (n p) d -> p (b n) d", p=P)

    def pe_body(pe, b, u, dyn, first, last):
        g, par = 2 * b + u, u
        for e in range(NE):
            pe_up(pe, g, par, e)
            if e:
                pe_down(pe, g, e - 1)
            elif not first:
                pe_down(pe, g - 1, NE - 1)
            if e == 3 and not last:
                pe_turn(pe, g + 1)
            if e == 5 and not last:
                pe_logits(pe, g + 1)

    def act_body(act, b, u, dyn, first, last):
        g, par = 2 * b + u, u
        for e in range(NE):
            act_hidden(act, g, e)
            if e == 3 and not last:
                act_turned(act, g + 1, 1 - par)
            if e == 6 and not last:
                act_exp(act, g + 1)

    def dve_body(dve, b, u, dyn, first, last):
        g, par = 2 * b + u, u
        for e in range(NE):
            if e:
                dve_mix(dve, g, par, e - 1, last)
            elif not first:
                dve_mix(dve, g - 1, 1 - par, NE - 1)
            if e == 2 and first:
                att.dve_finish(dve)
            if e == 0 and not last:
                dve_stats(dve, g + 1, dyn)
            if e == 1 and not first:
                dve_post1(dve, g - 1, 1 - par)
            if e == 2 and not last:
                dve_h(dve, g + 1, dyn)
            if e == 3 and not first:
                dve_post2(dve, g - 1, 1 - par, b if u else b - 1, dyn)
            if e == 4 and not last:
                dve_turned(dve, g + 1, 1 - par)
            if e == 5 and not last:
                dve_route_a(dve, g + 1)
            if e == 6 and not last:
                dve_route_b(dve, g + 1)
            if e == 7 and not last:
                dve_route_c(dve, g + 1, 1 - par)

    def pool_body(pl, b, u, dyn, first, last):
        g = 2 * b + u
        if not last:
            pool_norm(pl, g + 1)
        if not first:
            pool_post(pl, g - 1)
        pool_bias(pl, g, u)

    def over_groups(eng, body):
        for u in range(2):
            body(eng, 0, u, static, u == 0, False)
        with eng.Fori(1, GROUPS // 2 - 1) as b:
            for u in range(2):
                body(eng, b, u, dynamic, False, False)
        for u in range(2):
            body(eng, GROUPS // 2 - 1, u, static, False, u == 1)

    LAST = GROUPS - 1

    def sync_program(sp):
        sp.dma_start(w1f[:], w1_d.rearrange("e d h -> d e h")).then_inc(loaded, 16)
        sp.dma_start(b1row[:], b1_d.rearrange("e (n p) -> (e n) p", p=P)).then_inc(loaded, 16)
        sp.dma_start(wg[:], wg_d).then_inc(loaded, 16)
        sp.dma_start(w2[:], w2_d.rearrange("e (n p) d -> p e n d", p=P)).then_inc(loaded, 16)
        sp.dma_start(b2[:], b2_d.rearrange("(o e) d -> o e d", o=1).to_broadcast([P, NE, D])).then_inc(loaded, 16)
        for u in range(2):
            sp.nop(nofuse=True).then_inc(stored[u], 1)
        with sp.Fori(0, GROUPS // 2) as b:
            for u in range(2):
                g = 2 * b + u
                sp.wait_ge(out_ready.sem, out_ready.of(g))
                sp.dma_start(ov[:, bass.ds(g * TG, TG), :], outb[:, u, :, :]).then_inc(stored[u], 16)
        for u in range(2):
            sp.wait_ge(stored[u], 1 + 16 * GROUPS // 2)

    def tensor_program(pe):
        over_groups(pe, pe_body)
        pe_down(pe, LAST, NE - 1)

    def scalar_program(act):
        act_exp(act, 0)
        over_groups(act, act_body)

    def vector_program(dve):
        over_groups(dve, dve_body)
        dve_mix(dve, LAST, 1, NE - 1, last=True)
        dve_post1(dve, LAST, 1, last=True)
        dve_post2(dve, LAST, 1, GROUPS // 2 - 1, static)

    def gpsimd_program(pl):
        over_groups(pl, pool_body)
        pool_post(pl, LAST)

    this = Part()
    this.pool_constants = pool_constants
    this.act_prepare = act_prepare
    this.dve_prepare = dve_prepare
    this.dve_prepare_b1 = dve_prepare_b1
    this.pe_first = pe_first
    this.act_turned = act_turned
    this.dve_stats = dve_stats
    this.dve_h = dve_h
    this.dve_turned = dve_turned
    this.dve_route_a = dve_route_a
    this.dve_route_b = dve_route_b
    this.dve_route_c = dve_route_c
    this.pool_norm = pool_norm
    this.sync = sync_program
    this.tensor = tensor_program
    this.scalar = scalar_program
    this.vector = vector_program
    this.gpsimd = gpsimd_program
    return this


_INS = ["L0_attn_hidden", "L0_attn_w_norm_in", "L0_attn_w_in_proj", "L0_attn_conv_w", "L0_attn_conv_b",
        "L0_attn_w_dt", "L0_attn_b_dt", "L0_attn_A_log", "L0_attn_D", "L0_attn_w_norm_out", "L0_attn_w_out_proj",
        "L0_ffn_Wg", "L0_ffn_W1", "L0_ffn_b1", "L0_ffn_W2", "L0_ffn_b2"]
_OUTS = [((BATCH, SEQ, D), "float32")]


def kernel(**inputs):
    import numpy as _np
    import concourse.bacc as _bacc
    from concourse import mybir as _mybir
    from concourse.bass_utils import run_bass_kernel_spmd as _run

    nc = _bacc.Bacc("TRN2", target_bir_lowering=False, num_devices=1)
    arrays, args = {}, []
    for name in _INS:
        a = _np.ascontiguousarray(inputs[name])
        arrays[f"in_{name}_dram"] = a
        args.append(nc.dram_tensor(f"in_{name}_dram", a.shape, _mybir.dt.from_np(a.dtype), kind="ExternalInput").ap())
    for i, (shape, dtype) in enumerate(_OUTS):
        dt = _mybir.dt.from_np(_np.dtype(dtype))
        args.append(nc.dram_tensor(f"out_{i}_dram", shape, dt, kind="ExternalOutput").ap())
    build(nc, *args)
    r = _run(nc, [arrays], core_ids=[0])
    return r.results[0]["out_0_dram"]
```
